# Optimizing a Trainium2 kernel written in Bass

```python
import numpy as np
import jax
import jax.numpy as jnp

def _softmax(x, axis=-1):
    return jax.nn.softmax(x, axis=axis)

def _gelu(x):
    return jax.nn.gelu(x, approximate=True)

def _silu(x):
    return jax.nn.silu(x)

def _sigmoid(x):
    return jax.nn.sigmoid(x)

def _layernorm(x, axis=-1, eps=1e-05):
    m = jnp.mean(x, axis=axis, keepdims=True)
    v = jnp.var(x, axis=axis, keepdims=True)
    return (x - m) / jnp.sqrt(v + eps)

def _scatter_add(tgt, idx, src, axis=0):
    return tgt.at[idx].add(src)

def _segment_sum(src, seg, n):
    return jax.ops.segment_sum(src, seg, n)
kernel_name = 'mk_xattn_ffn_d2_seqx_r4_e822e7'

def setup_inputs(seed: int=0):
    np.random.seed(seed)
    _w = jnp.asarray

    def _rec_inputs():
        import jax
        import jax.numpy as jnp
        _rk = jax.random.key(seed)
        x = 7.22e-05 + 1 * jax.random.normal(jax.random.fold_in(_rk, 1), (16, 512, 256), jnp.float32)
        _lenS = 512 - jax.random.randint(jax.random.fold_in(_rk, 7), (16,), 0, max(1, 512 // 4) + 1, jnp.int32)
        _lenS2 = 64 - jax.random.randint(jax.random.fold_in(_rk, 8), (16,), 0, max(1, 64 // 4) + 1, jnp.int32)
        _ctx_1024P = jax.random.normal(jax.random.fold_in(_rk, 11), (16, 16, 256), jnp.float32)
        _ctx_1024c = jax.random.dirichlet(jax.random.fold_in(_rk, 511), 0.3 * jnp.ones((16,), jnp.float32), (16, 64))
        _ctx_1024t = jnp.einsum('bsk,bkd->bsd', _ctx_1024c, _ctx_1024P)
        _ctx_1024t = _ctx_1024t * jax.lax.rsqrt(jnp.mean(jnp.square(_ctx_1024t)) + 1e-12) * 0.953939
        ctx_1024 = 4.13588e-05 + 0.999923 * (_ctx_1024t + 0.3 * jax.random.normal(jax.random.fold_in(_rk, 611), (16, 64, 256), jnp.float32))
        _validS = jnp.arange(512)[None, :] < _lenS[:, None]
        _validS2 = jnp.arange(64)[None, :] < _lenS2[:, None]
        _causal = jnp.tril(jnp.ones((512, 512), dtype=bool))
        mask_SxS2_bk0 = jnp.logical_not(jnp.broadcast_to(_validS2[0:1, :], (512, 64)))
        mask_BxS2_bk1 = jnp.broadcast_to(_validS2[:, :], (16, 64))
        return (x, ctx_1024, mask_SxS2_bk0, mask_BxS2_bk1)
    x, ctx_1024, mask_SxS2_bk0, mask_BxS2_bk1 = _rec_inputs()

    def _L0_xattn_setup():
        import jax, jax.numpy as jnp
        import numpy as np
        EMB = 256
        HEADS = 16
        HEAD_DIM = EMB // HEADS
        key = jax.random.key(seed)
        ks = jax.random.split(key, 11)
        B, S = (4, 512)
        scale = 1.0 / np.sqrt(EMB)
        inp = {'query': jax.random.normal(ks[0], (B, S, EMB), jnp.float32), 'key': jax.random.normal(ks[1], (B, S, EMB), jnp.float32), 'value': jax.random.normal(ks[2], (B, S, EMB), jnp.float32), 'Wq': jax.random.normal(ks[3], (EMB, EMB), jnp.float32) * scale, 'bq': jnp.zeros((EMB,), jnp.float32), 'Wk': jax.random.normal(ks[4], (EMB, EMB), jnp.float32) * scale, 'bk': jnp.zeros((EMB,), jnp.float32), 'Wv': jax.random.normal(ks[5], (EMB, EMB), jnp.float32) * scale, 'bv': jnp.zeros((EMB,), jnp.float32), 'Wo': jax.random.normal(ks[6], (EMB, EMB), jnp.float32) * scale, 'bo': jnp.zeros((EMB,), jnp.float32)}
        return inp
    _L0_xattn_all = _L0_xattn_setup()
    _L0_xattn_in = {k: v for k, v in _L0_xattn_all.items() if k in ('Wq', 'bq', 'Wk', 'bk', 'Wv', 'bv', 'Wo', 'bo')}
    del _L0_xattn_all

    def _L0_ffn_setup():
        import jax, jax.numpy as jnp
        import numpy as np
        B, S, H = (4, 512, 256)
        E = 8
        GS = 2
        NG = E // GS
        F = int(H * 4 * (2.0 / 3.0))
        key = jax.random.key(seed)
        ks = jax.random.split(key, 7)
        sc_h = 1.0 / np.sqrt(H)
        sc_f = 1.0 / np.sqrt(F)
        return {'x': jax.random.normal(ks[0], (B, S, H), dtype=jnp.float32), 'Wr': jax.random.normal(ks[1], (H, E), dtype=jnp.float32) * sc_h, 'br': jnp.zeros((E,), dtype=jnp.float32), 'W_up': jax.random.normal(ks[2], (NG, H, F), dtype=jnp.float32) * sc_h, 'b_up': jax.random.normal(ks[3], (NG, F), dtype=jnp.float32) * 0.01, 'W_down': jax.random.normal(ks[4], (E, F, H), dtype=jnp.float32) * sc_f, 'b_down': jax.random.normal(ks[5], (E, H), dtype=jnp.float32) * 0.01}
    _L0_ffn_all = _L0_ffn_setup()
    _L0_ffn_in = {k: v for k, v in _L0_ffn_all.items() if k in ('Wr', 'br', 'W_up', 'b_up', 'W_down', 'b_down')}
    del _L0_ffn_all

    def _L1_xattn_setup():
        import jax, jax.numpy as jnp
        import numpy as np
        B, S, E, H = (4, 512, 256, 16)
        D = E // H
        key = jax.random.key(seed)
        ks = jax.random.split(key, 12)
        q = jax.random.normal(ks[0], (B, S, E), jnp.float32)
        k = jax.random.normal(ks[1], (B, S, E), jnp.float32)
        v = jax.random.normal(ks[2], (B, S, E), jnp.float32)
        mask = jnp.tril(jnp.ones((S, S), dtype=bool))
        pad_mask = jnp.ones((B, S), dtype=bool).at[0, 3 * S // 4:].set(False)
        sc = 1.0 / np.sqrt(E)
        wq = jax.random.normal(ks[3], (E, E), jnp.float32) * sc
        bq = jnp.zeros((E,), jnp.float32)
        wk = jax.random.normal(ks[4], (E, E), jnp.float32) * sc
        bk = jnp.zeros((E,), jnp.float32)
        wv = jax.random.normal(ks[5], (E, E), jnp.float32) * sc
        bv = jnp.zeros((E,), jnp.float32)
        wo = jax.random.normal(ks[6], (E, E), jnp.float32) * sc
        bo = jnp.zeros((E,), jnp.float32)
        return dict(q=q, k=k, v=v, mask=mask, pad_mask=pad_mask, wq=wq, bq=bq, wk=wk, bk=bk, wv=wv, bv=bv, wo=wo, bo=bo)
    _L1_xattn_all = _L1_xattn_setup()
    _L1_xattn_in = {k: v for k, v in _L1_xattn_all.items() if k in ('wq', 'bq', 'wk', 'bk', 'wv', 'bv', 'wo', 'bo')}
    del _L1_xattn_all

    def _L1_ffn_setup():
        import jax, jax.numpy as jnp
        import numpy as np
        import math
        GOLDEN_CENTER = 1.0 / math.e
        GOLDEN_LOWER = 0.5 - math.log(4.0 / 3.0)
        GOLDEN_UPPER = 0.5
        B, T, D = (4, 512, 256)
        E = 8
        I = 1024 // (E // 2)

        def _routing_weights(x, Wr, temperature):
            inh = jax.nn.sigmoid(x @ Wr / temperature)
            in_zone = (inh >= GOLDEN_LOWER) & (inh <= GOLDEN_UPPER)
            dist = jnp.abs(inh - GOLDEN_CENTER)
            w = jnp.exp(-dist / 0.1) * in_zone.astype(x.dtype)
            wsum = w.sum(axis=-1, keepdims=True)
            no_expert = wsum < 1e-08
            fb = jnp.exp(-dist / 0.3)
            _, top2 = jax.lax.top_k(fb, 2)
            fb_mask = jax.nn.one_hot(top2, E, dtype=x.dtype).sum(axis=-2)
            fb_w = fb * fb_mask
            fb_w = fb_w / jnp.clip(fb_w.sum(axis=-1, keepdims=True), 1e-08)
            w = jnp.where(no_expert, fb_w, w)
            wsum = w.sum(axis=-1, keepdims=True)
            return w / jnp.clip(wsum, 1e-08)
        key = jax.random.key(seed)
        k = jax.random.split(key, 6)
        s_d = 1.0 / math.sqrt(D)
        s_i = 1.0 / math.sqrt(I)
        return {'x': jax.random.normal(k[0], (B, T, D), jnp.float32), 'Wg': jax.random.normal(k[1], (E, D, I), jnp.float32) * s_d, 'Wu': jax.random.normal(k[2], (E, D, I), jnp.float32) * s_d, 'Wd': jax.random.normal(k[3], (E, I, D), jnp.float32) * s_i, 'Wr': jax.random.normal(k[4], (D, E), jnp.float32) * s_d, 'temperature': jnp.ones((1,), jnp.float32)}
    _L1_ffn_all = _L1_ffn_setup()
    _L1_ffn_in = {k: v for k, v in _L1_ffn_all.items() if k in ('Wg', 'Wu', 'Wd', 'Wr', 'temperature')}
    del _L1_ffn_all
    return {'x': x, 'ctx_1024': ctx_1024, 'mask_SxS2_bk0': mask_SxS2_bk0, 'mask_BxS2_bk1': mask_BxS2_bk1, 'L0_xattn_Wq': _L0_xattn_in['Wq'], 'L0_xattn_bq': _L0_xattn_in['bq'], 'L0_xattn_Wk': _L0_xattn_in['Wk'], 'L0_xattn_bk': _L0_xattn_in['bk'], 'L0_xattn_Wv': _L0_xattn_in['Wv'], 'L0_xattn_bv': _L0_xattn_in['bv'], 'L0_xattn_Wo': _L0_xattn_in['Wo'], 'L0_xattn_bo': _L0_xattn_in['bo'], 'L0_ffn_Wr': _L0_ffn_in['Wr'], 'L0_ffn_br': _L0_ffn_in['br'], 'L0_ffn_W_up': _L0_ffn_in['W_up'], 'L0_ffn_b_up': _L0_ffn_in['b_up'], 'L0_ffn_W_down': _L0_ffn_in['W_down'], 'L0_ffn_b_down': _L0_ffn_in['b_down'], 'L1_xattn_wq': _L1_xattn_in['wq'], 'L1_xattn_bq': _L1_xattn_in['bq'], 'L1_xattn_wk': _L1_xattn_in['wk'], 'L1_xattn_bk': _L1_xattn_in['bk'], 'L1_xattn_wv': _L1_xattn_in['wv'], 'L1_xattn_bv': _L1_xattn_in['bv'], 'L1_xattn_wo': _L1_xattn_in['wo'], 'L1_xattn_bo': _L1_xattn_in['bo'], 'L1_ffn_Wg': _L1_ffn_in['Wg'], 'L1_ffn_Wu': _L1_ffn_in['Wu'], 'L1_ffn_Wd': _L1_ffn_in['Wd'], 'L1_ffn_Wr': _L1_ffn_in['Wr'], 'L1_ffn_temperature': _L1_ffn_in['temperature']}

def reference(x, ctx_1024, mask_SxS2_bk0, mask_BxS2_bk1, L0_xattn_Wq, L0_xattn_bq, L0_xattn_Wk, L0_xattn_bk, L0_xattn_Wv, L0_xattn_bv, L0_xattn_Wo, L0_xattn_bo, L0_ffn_Wr, L0_ffn_br, L0_ffn_W_up, L0_ffn_b_up, L0_ffn_W_down, L0_ffn_b_down, L1_xattn_wq, L1_xattn_bq, L1_xattn_wk, L1_xattn_bk, L1_xattn_wv, L1_xattn_bv, L1_xattn_wo, L1_xattn_bo, L1_ffn_Wg, L1_ffn_Wu, L1_ffn_Wd, L1_ffn_Wr, L1_ffn_temperature):
    import jax
    import jax.numpy as jnp

    def _L0_xattn_ref(query, key, value, Wq, bq, Wk, bk, Wv, bv, Wo, bo):
        import jax, jax.numpy as jnp
        import numpy as np
        EMB = 256
        HEADS = 16
        HEAD_DIM = EMB // HEADS
        B, S, E = query.shape
        H, D = (HEADS, HEAD_DIM)

        def split_heads(x):
            return x.reshape(B, -1, H, D).transpose(0, 2, 1, 3)
        Q = split_heads(query @ Wq + bq)
        K = split_heads(key @ Wk + bk)
        V = split_heads(value @ Wv + bv)
        scores = jnp.einsum('bhqd,bhkd->bhqk', Q, K) / jnp.sqrt(jnp.float32(D))
        attn = jax.nn.softmax(scores, axis=-1)
        out = jnp.einsum('bhqk,bhkd->bhqd', attn, V)
        out = out.transpose(0, 2, 1, 3).reshape(B, S, E)
        return out @ Wo + bo

    def _L0_ffn_ref(x, Wr, br, W_up, b_up, W_down, b_down):
        import jax, jax.numpy as jnp
        import numpy as np
        B, S, H = (4, 512, 256)
        E = 8
        GS = 2
        NG = E // GS
        F = int(H * 4 * (2.0 / 3.0))
        b, s, h = x.shape
        n_tok = b * s
        k = n_tok // E
        xf = x.reshape(n_tok, h)
        logits = xf @ Wr + br
        Sm = jax.nn.softmax(logits, axis=-1)
        G_t, idx_t = jax.lax.top_k(Sm.T, k)
        G = G_t.T
        idx = idx_t.T
        tokens = xf[idx]
        group = jnp.arange(E) // GS
        Wu = W_up[group]
        bu = b_up[group]
        mid = jax.nn.silu(jnp.einsum('keh,ehf->kef', tokens, Wu) + bu)
        out = jnp.einsum('kef,efh->keh', mid, W_down) + b_down
        y = jnp.zeros_like(xf).at[idx].add(G[..., None] * out)
        return y.reshape(b, s, h)

    def _L1_xattn_ref(q, k, v, mask, pad_mask, wq, bq, wk, bk, wv, bv, wo, bo):
        import jax, jax.numpy as jnp
        import numpy as np
        B, S, E, H = (4, 512, 256, 16)
        D = E // H
        bs, q_len, _ = q.shape
        k_len = k.shape[1]
        scale = jnp.sqrt(jnp.asarray(D, q.dtype))
        Q = (q @ wq.T + bq).reshape(bs, q_len, H, D).transpose(0, 2, 1, 3)
        K = (k @ wk.T + bk).reshape(bs, k_len, H, D).transpose(0, 2, 1, 3)
        V = (v @ wv.T + bv).reshape(bs, k_len, H, D).transpose(0, 2, 1, 3)
        attn = jnp.einsum('bhqd,bhkd->bhqk', Q, K) / scale
        attn = jnp.where(mask, attn, jnp.asarray(-100000000.0, attn.dtype))
        attn = jnp.where(pad_mask[:, None, None, :], attn, jnp.asarray(-100000000.0, attn.dtype))
        attn = jax.nn.softmax(attn, axis=-1)
        out = jnp.einsum('bhqk,bhkd->bhqd', attn, V)
        out = out.transpose(0, 2, 1, 3).reshape(bs, q_len, E)
        return out @ wo.T + bo

    def _L1_ffn_ref(x, Wg, Wu, Wd, Wr, temperature):
        import jax, jax.numpy as jnp
        import numpy as np
        import math
        GOLDEN_CENTER = 1.0 / math.e
        GOLDEN_LOWER = 0.5 - math.log(4.0 / 3.0)
        GOLDEN_UPPER = 0.5
        B, T, D = (4, 512, 256)
        E = 8
        I = 1024 // (E // 2)

        def _routing_weights(x, Wr, temperature):
            inh = jax.nn.sigmoid(x @ Wr / temperature)
            in_zone = (inh >= GOLDEN_LOWER) & (inh <= GOLDEN_UPPER)
            dist = jnp.abs(inh - GOLDEN_CENTER)
            w = jnp.exp(-dist / 0.1) * in_zone.astype(x.dtype)
            wsum = w.sum(axis=-1, keepdims=True)
            no_expert = wsum < 1e-08
            fb = jnp.exp(-dist / 0.3)
            _, top2 = jax.lax.top_k(fb, 2)
            fb_mask = jax.nn.one_hot(top2, E, dtype=x.dtype).sum(axis=-2)
            fb_w = fb * fb_mask
            fb_w = fb_w / jnp.clip(fb_w.sum(axis=-1, keepdims=True), 1e-08)
            w = jnp.where(no_expert, fb_w, w)
            wsum = w.sum(axis=-1, keepdims=True)
            return w / jnp.clip(wsum, 1e-08)
        weights = _routing_weights(x, Wr, temperature)
        gate = jnp.einsum('btd,edi->beti', x, Wg)
        up = jnp.einsum('btd,edi->beti', x, Wu)
        h = jax.nn.silu(gate) * up
        e_out = jnp.einsum('beti,eid->betd', h, Wd)
        out = jnp.einsum('bte,betd->btd', weights, e_out)
        return out
    x = x + _L0_xattn_ref(_layernorm(x, axis=-1), ctx_1024, ctx_1024, L0_xattn_Wq, L0_xattn_bq, L0_xattn_Wk, L0_xattn_bk, L0_xattn_Wv, L0_xattn_bv, L0_xattn_Wo, L0_xattn_bo)
    x = x + _L0_ffn_ref(_layernorm(x, axis=-1), L0_ffn_Wr, L0_ffn_br, L0_ffn_W_up, L0_ffn_b_up, L0_ffn_W_down, L0_ffn_b_down)
    x = x + _L1_xattn_ref(_layernorm(x, axis=-1), ctx_1024, ctx_1024, mask_SxS2_bk0, mask_BxS2_bk1, L1_xattn_wq, L1_xattn_bq, L1_xattn_wk, L1_xattn_bk, L1_xattn_wv, L1_xattn_bv, L1_xattn_wo, L1_xattn_bo)
    x = x + _L1_ffn_ref(_layernorm(x, axis=-1), L1_ffn_Wg, L1_ffn_Wu, L1_ffn_Wd, L1_ffn_Wr, L1_ffn_temperature)
    return x

_drawn_inputs = setup_inputs


def setup_inputs(seed=0):
    import zlib

    import numpy as np

    out = dict(_drawn_inputs(seed))
    spreads = {'L0_xattn_bq': (0.0, 0.1),
     'L0_xattn_bk': (0.0, 0.8),
     'L0_xattn_bv': (0.0, 0.1),
     'L0_xattn_bo': (0.0, 0.1),
     'L0_ffn_br': (0.0, 0.1),
     'L1_xattn_bq': (0.0, 0.1),
     'L1_xattn_bk': (0.0, 0.8),
     'L1_xattn_bv': (0.0, 0.1),
     'L1_xattn_bo': (0.0, 0.1)}
    factors = {'L0_ffn_b_up': 7.862, 'L0_ffn_b_down': 4.699}
    for name, (base, spread) in spreads.items():
        noise = np.random.default_rng([zlib.crc32(name.encode()), seed]).standard_normal(out[name].shape)
        drawn = base * np.exp(spread * noise) if base else spread * noise
        out[name] = jnp.asarray(drawn.astype(out[name].dtype))
    for name, factor in factors.items():
        out[name] = (out[name] * factor).astype(out[name].dtype)
    return out
```

```python
import math
from contextlib import ExitStack

import numpy as np

import concourse.bass as bass
from concourse import mybir

F32 = mybir.dt.float32
F32R = mybir.dt.float32r
BF16 = mybir.dt.bfloat16
I32 = mybir.dt.int32
U8 = mybir.dt.uint8
ALU = mybir.AluOpType
ACT = mybir.ActivationFunctionType
AX = mybir.AxisListType

P = 128
B, S, D = 16, 512, 256
SK = 64
H, DH = 16, 16
KC = D // P
TT = S // P
HH = H // KC
NP = H // 2
NT = B * TT
VW = DH + 1
N_TOK = B * S
LN_EPS = 1e-5
BIG = float(2.0 ** 60)
PE_COLS = 96
RSQRT_MAGIC = float(0x5F3759DF)
NEWTON = 3
LN_STEPS = TT + TT + 3 + 3 * NEWTON


def done(count_per_batch, b, k):
    return b * count_per_batch + k


def after(eng, sem, value):
    if not isinstance(value, int) or value > 0:
        eng.wait_ge(sem, value)


class Semaphores:

    def __init__(self, nc):
        self.nc, self.stack, self.taken = nc, ExitStack(), []

    def take(self, name):
        self.taken.append(self.stack.enter_context(self.nc.semaphore(name)))
        return self.taken[-1]

    def give_back(self):
        with self.nc.Block() as block:
            @block.gpsimd
            def _(pool):
                for sem in self.taken:
                    pool.sem_clear(sem)
        self.stack.close()


class Scope:

    def __init__(self, nc, ctx, phase, const=None):
        self.nc, self.ctx, self.phase, self.const = nc, ctx, phase, const

    def sb(self, name, shape, dt=F32):
        return self.ctx.enter_context(self.nc.sbuf_tensor(f"{self.phase}_{name}", shape, dt))

    def sem(self, name):
        return self.const["sems"].take(f"{self.phase}_{name}")


def layernorm_stats(dve, x, stats, mv, rstd, tmp, sem, start, passed):
    n = 0
    for t in range(TT):
        dve.bn_stats(stats[:, t, :], x[:, t, :]).then_inc(sem, 1)
        n += 1
    dve.wait_ge(sem, start + n)
    dve.sem_inc(passed, 1)
    for t in range(TT):
        dve.bn_aggr(mv[:, t, :], stats[:, t, :]).then_inc(sem, 1)
        n += 1
    dve.wait_ge(sem, start + n)
    var, guess = tmp[:, 0, :], tmp[:, 1, :]
    dve.tensor_scalar(var, mv[:, :, 1], LN_EPS, None, ALU.add).then_inc(sem, 1)
    n += 1
    dve.wait_ge(sem, start + n)
    dve.tensor_scalar(guess.bitcast(I32), var.bitcast(I32), 1, None, ALU.logical_shift_right).then_inc(sem, 1)
    n += 1
    dve.wait_ge(sem, start + n)
    dve.tensor_scalar(rstd.bitcast(I32), guess.bitcast(I32), -1.0, RSQRT_MAGIC, ALU.mult, ALU.add).then_inc(sem, 1)
    n += 1
    for _ in range(NEWTON):
        dve.wait_ge(sem, start + n)
        dve.scalar_tensor_tensor(guess, rstd, -0.5, rstd, ALU.mult, ALU.mult).then_inc(sem, 1)
        n += 1
        dve.wait_ge(sem, start + n)
        dve.tensor_tensor(guess, guess, var, ALU.mult).then_inc(sem, 1)
        n += 1
        dve.wait_ge(sem, start + n)
        dve.scalar_tensor_tensor(rstd, guess, 1.5, rstd, ALU.add, ALU.mult).then_inc(sem, 1)
        n += 1
    assert n == LN_STEPS


def three_passes(pe, out, st_hi, st_lo, mv_hi, mv_lo, first, last):
    pe.matmul(out, st_hi, mv_hi, start=first, stop=False)
    pe.matmul(out, st_hi, mv_lo, start=False, stop=False)
    return pe.matmul(out, st_lo, mv_hi, start=False, stop=last)


def make_constants(nc, const):
    ident, headmask, negsel, keysel = const["ident"], const["headmask"], const["negsel"], const["keysel"]
    with ExitStack() as ctx:
        sc = Scope(nc, ctx, "const", const)
        made = sc.sem("const_made")
        negf = sc.sb("negsel_f", [P, NP, P])
        keyf = sc.sb("keysel_f", [P, H // 2, SK])
        block = ctx.enter_context(nc.Block())

        @block.gpsimd
        def _(pool):
            pool.memset(ident[:, :], 0.0).then_inc(made, 1)
            pool.memset(headmask[:, :], 1.0).then_inc(made, 1)
            pool.memset(negf[:, :, :], -1.0).then_inc(made, 1)
            pool.memset(keyf[:, :, :], 0.0).then_inc(made, 1)
            pool.wait_ge(made, 4)
            pool.affine_select(out=ident[:, :], in_=ident[:, :], compare_op=ALU.not_equal, fill=1.0, base=0,
                               pattern=[[-1, P]], channel_multiplier=1).then_inc(made, 1)
            pool.affine_select(out=headmask[:, :], in_=headmask[:, :], compare_op=ALU.is_ge, fill=0.0, base=0,
                               pattern=[[-DH, HH]], channel_multiplier=1).then_inc(made, 1)
            pool.affine_select(out=keyf[:, :, :], in_=keyf[:, :, :], compare_op=ALU.not_equal, fill=1.0, base=0,
                               pattern=[[0, HH], [-1, SK]], channel_multiplier=1).then_inc(made, 1)
            v = negf[:, :, :].rearrange("p j (a k) -> p j a k", a=2)
            pool.affine_select(out=v, in_=v, compare_op=ALU.is_equal, fill=0.0, base=0,
                               pattern=[[-2, NP], [-1, 2], [0, SK]], channel_multiplier=1).then_inc(made, 1)
            pool.wait_ge(made, 8)
            pool.affine_select(out=headmask[:, :], in_=headmask[:, :], compare_op=ALU.is_ge, fill=0.0, base=DH - 1,
                               pattern=[[DH, HH]], channel_multiplier=-1).then_inc(made, 1)
            pool.tensor_copy(negsel[:, :, :], negf[:, :, :]).then_inc(made, 1)
            pool.tensor_copy(keysel[:, :, :], keyf[:, :, :]).then_inc(made, 1)


def attention_setup(nc, const, kv, w, psum):
    KV_STEPS = 2 * KC
    with ExitStack() as ctx:
        sc = Scope(nc, ctx, kv["name"] + "_setup", const)
        ctx_in = sc.sb("ctx_in", [P, B * SK // P, D])
        ctxT = sc.sb("ctxT", [P, KC, B * SK])
        dup = sc.sb("ctx_dup", [P, 2, KC, 2, SK])
        wk, wv = sc.sb("wk", [P, KC, D]), sc.sb("wv", [P, KC, D])
        bv = sc.sb("bv_bcast", [P, D])
        wq, wo = sc.sb("wq", [P, KC, D]), sc.sb("wo", [P, KC, D])
        loaded, qo_loaded = sc.sem("kv_loaded"), sc.sem("qo_loaded")
        small_loaded = sc.sem("small_loaded")
        turned, turned_out = sc.sem("ctx_turned"), sc.sem("ctx_turned_out")
        k_made, k_hi, k_out = sc.sem("k_made"), sc.sem("k_hi"), sc.sem("k_out")
        dup_made, v_made, v_out = sc.sem("dup_made"), sc.sem("v_made"), sc.sem("v_out")
        v_cleared, split_hi, split_lo = sc.sem("v_cleared"), sc.sem("split_hi"), sc.sem("split_lo")
        passed = sc.sem("passed")
        mask_loaded, wr_cleared = sc.sem("mask_loaded"), sc.sem("wr_cleared")
        NC8 = B * SK // P
        if w["mask"] is not None:
            mask32, pad32 = sc.sb("mask_u8", [SK, S // 4], I32), sc.sb("pad_u8", [SK, B // 4], I32)
        block = ctx.enter_context(nc.Block())

        @block.sync
        def _(sp):
            sp.dma_start(ctx_in[:, :, :], w["ctx"].rearrange("(n p) d -> p n d", p=P)).then_inc(loaded, 16)
            sp.dma_start(wk[:, :, :], w["wk"].rearrange("(c p) d -> p c d", p=P)).then_inc(loaded, 16)
            sp.dma_start(wv[:, :, :], w["wv"].rearrange("(c p) d -> p c d", p=P)).then_inc(loaded, 16)
            sp.dma_start(bv[:, :], w["bv"].partition_broadcast(P)).then_inc(small_loaded, 16)
            sp.dma_start(kv["bo"][:, :], w["bo"].partition_broadcast(P)).then_inc(small_loaded, 16)
            sp.dma_start(kv["bk"][:, :], w["bk"]).then_inc(small_loaded, 16)
            sp.dma_start(kv["bq"][:, :], w["bq"]).then_inc(small_loaded, 16)
            sp.dma_start(wq[:, :, :], w["wq"].rearrange("(c p) d -> p c d", p=P)).then_inc(qo_loaded, 16)
            sp.dma_start(wo[:, :, :], w["wo"].rearrange("(c p) d -> p c d", p=P)).then_inc(qo_loaded, 16)
            sp.wait_ge(wr_cleared, 1)
            sp.dma_start(kv["wr"][:, :, 0:8], w["wr"].rearrange("(c p) e -> p c e", p=P)).then_inc(small_loaded, 16)
            if w["mask"] is not None:
                sp.dma_start(mask32[:, :], w["mask"]).then_inc(mask_loaded, 16)
                sp.dma_start(pad32[:, :], w["pad"]).then_inc(mask_loaded, 16)
                sp.wait_ge(mask_loaded, 32)
            sp.wait_ge(small_loaded, 5 * 16)

        @block.gpsimd
        def _(pool):
            pool.memset(kv["wr"][:, :, :], 0.0).then_inc(wr_cleared, 1)
            pool.memset(kv["v"][:, :, :, :], 0.0).then_inc(v_cleared, 1)
            pool.wait_ge(v_cleared, 1)
            ones = kv["v"][:, :, :, :].rearrange("p b j (a c) -> p (b j) a c", a=2)
            pool.memset(ones[0:SK, :, 0, DH:VW], 1.0).then_inc(v_cleared, 1)
            pool.memset(ones[SK:P, :, 1, DH:VW], 1.0).then_inc(v_cleared, 1)
            pool.wait_ge(v_cleared, 3)
            pool.wait_ge(turned_out, KC * 2)
            with pool.Fori(0, B // 2) as r:
                for p in range(2):
                    after(pool, v_made, r * 2 + p - 1 if p else r * 2)
                    pool.sem_inc(passed, 1)
                    for c in range(KC):
                        src = ctxT[:, c, bass.ds((r * 2 + p) * SK, SK)].unsqueeze(1).to_broadcast([P, 2, SK])
                        pool.tensor_copy(dup[:, p, c, :, :], src).then_inc(dup_made, 1)

        @block.tensor
        def _(pe):
            pe.wait_ge(loaded, 48)
            for c in range(KC):
                for n in range(NC8):
                    t = pe.transpose(psum[:, 2 * c + n // 4, (n % 4) * P:(n % 4 + 1) * P], ctx_in[:, n, c * P:(c + 1) * P],
                                     const["ident"][:, :])
                    if n % 4 == 3:
                        t.then_inc(turned, 1)
            pe.wait_ge(turned_out, KC * 2)
            for m in range(KC):
                for n in range(2):
                    for c in range(KC):
                        k = pe.matmul(psum[:, 4 + 2 * m + n, :], wk[:, c, m * P:(m + 1) * P], ctxT[:, c, n * 512:(n + 1) * 512],
                                      start=(c == 0), stop=(c == KC - 1))
                    k.then_inc(k_made, 1)
            with pe.Fori(0, B // 2) as r:
                for p in range(2):
                    pe.wait_ge(dup_made, (r * 2 + p + 1) * KC)
                    pe.wait_ge(v_out, r * 4 + 2 * p - 2 if p else r * 4)
                    for c in range(KC):
                        v = pe.matmul(psum[:, p, 0:D], dup[:, p, c, :, :], wv[:, c, :], start=(c == 0), stop=(c == KC - 1))
                    v.then_inc(v_made, 1)

        @block.scalar
        def _(act):
            for n in range(2 * KC):
                act.wait_ge(turned, n + 1)
                act.activation(ctxT[:, n // 2, (n % 2) * 512:(n % 2 + 1) * 512], psum[:, n, :], ACT.Copy).then_inc(turned_out, 1)
            act.wait_ge(small_loaded, 5 * 16)
            for m in range(KC):
                for n in range(2):
                    act.wait_ge(k_made, 2 * m + n + 1)
                    act.activation(kv["kT_hi"][:, m, n * 512:(n + 1) * 512], psum[:, 4 + 2 * m + n, :], ACT.Identity,
                                   bias=kv["bk"][:, m:m + 1]).then_inc(k_hi, 1)
            act.wait_ge(qo_loaded, 32)
            act.activation(kv["wq_hi"][:, :, :], wq[:, :, :], ACT.Copy).then_inc(split_hi, 1)
            act.activation(kv["wo_hi"][:, :, :], wo[:, :, :], ACT.Copy).then_inc(split_hi, 1)

        @block.vector
        def _(dve):
            dve.wait_ge(small_loaded, 5 * 16)
            for m in range(KC):
                for n in range(2):
                    dve.wait_ge(k_hi, 2 * m + n + 1)
                    cols = slice(n * 512, (n + 1) * 512)
                    dve.scalar_tensor_tensor(kv["kT_lo"][:, m, cols], psum[:, 4 + 2 * m + n, :], kv["bk"][:, m:m + 1],
                                             kv["kT_hi"][:, m, cols].bitcast(F32), ALU.add, ALU.subtract).then_inc(k_out, 1)
            dve.wait_ge(split_hi, 2)
            dve.wait_ge(qo_loaded, 32)
            dve.tensor_tensor(kv["wq_lo"][:, :, :], wq[:, :, :], kv["wq_hi"][:, :, :].bitcast(F32), ALU.subtract).then_inc(split_lo, 1)
            dve.tensor_tensor(kv["wo_lo"][:, :, :], wo[:, :, :], kv["wo_hi"][:, :, :].bitcast(F32), ALU.subtract).then_inc(split_lo, 1)
            if w["mask"] is not None:
                dve.wait_ge(mask_loaded, 32)
                dve.tensor_copy(kv["mask"][:, :], mask32[:, :].bitcast(U8))
                dve.tensor_scalar(kv["pad"][:, :], pad32[:, :].bitcast(U8), BIG, None, ALU.mult)
            dve.wait_ge(v_cleared, 3)
            with dve.Fori(0, B // 2) as r:
                for p in range(2):
                    dve.wait_ge(v_made, r * 2 + p + 1)
                    for a in range(2):
                        rows = slice(a * SK, (a + 1) * SK)
                        heads = psum[rows, p, 0:D].rearrange("p (j a c) -> p j a c", a=2, c=DH)[:, :, a, :]
                        bias = bv[rows, :].rearrange("p (j a c) -> p j a c", a=2, c=DH)[:, :, a, :]
                        out = kv["v"][rows, bass.ds(r * 2 + p, 1), :, a * VW:a * VW + DH].rearrange("p b j c -> p (b j) c")
                        dve.tensor_tensor(out, heads, bias, ALU.add).then_inc(v_out, 1)


def attention(nc, const, kv, psum, src, dst, dst_normed, logits_all):
    masked = kv["masked"]
    ident = const["ident"]
    STORES = 2
    with ExitStack() as ctx:
        sc = Scope(nc, ctx, kv["name"], const)
        x_in = sc.sb("x_in", [P, 2, TT, D])
        x_bias = sc.sb("x_bias", [P, 2, TT, D])
        x_new = sc.sb("x_new", [P, 2, TT, D])
        normed = sc.sb("normed", [P, TT, D])
        normed_new = sc.sb("normed_new", [P, 2, TT, D])
        nT_hi, nT_lo = sc.sb("nT_hi", [P, KC, S], F32R), sc.sb("nT_lo", [P, KC, S], F32R)
        newT = sc.sb("newT", [P, KC, S])
        qT_hi, qT_lo = sc.sb("qT_hi", [P, 2, KC, S], F32R), sc.sb("qT_lo", [P, 2, KC, S], F32R)
        kb_hi, kb_lo = sc.sb("kb_hi", [P, 2, KC, HH, SK], F32R), sc.sb("kb_lo", [P, 2, KC, HH, SK], F32R)
        v_cur = sc.sb("v_cur", [P, 2, (NP - 1) * 2 * VW + PE_COLS])
        s_max = sc.sb("s_max", [P, TT, H])
        maxT = sc.sb("maxT", [P, S], F32R)
        probs = sc.sb("probs", [P, NP, S])
        recip = sc.sb("recip", [P, TT, H])
        att = sc.sb("att", [P, TT, D])
        aT_hi, aT_lo = sc.sb("aT_hi", [P, KC, S], F32R), sc.sb("aT_lo", [P, KC, S], F32R)
        stats, mv = sc.sb("stats", [P, TT, 6]), sc.sb("mv", [P, TT, 2])
        stats2, mv2 = sc.sb("stats2", [P, TT, 6]), sc.sb("mv2", [P, TT, 2])
        rstd, rstd2, shift2 = sc.sb("rstd", [P, TT]), sc.sb("rstd2", [P, TT]), sc.sb("shift2", [P, TT])
        tmp, tmp2 = sc.sb("ln_tmp", [P, 2, TT]), sc.sb("ln_tmp2", [P, 2, TT])
        mask_cur = sc.sb("mask_cur", [P, 2, S], BF16) if masked else None

        x_loaded = [sc.sem(f"x_loaded{p}") for p in range(2)]
        stored = [sc.sem(f"stored{p}") for p in range(2)]
        ln_in, ln_out = sc.sem("ln_in"), sc.sem("ln_out")
        norm_in, norm_out = sc.sem("norm_in"), sc.sem("norm_out")
        bias_done = sc.sem("bias_done")
        v_ready = sc.sem("v_ready")
        kb_ready = sc.sem("kb_ready")
        mask_ready = sc.sem("mask_ready")
        turned, turned_hi, turned_lo = sc.sem("turned"), sc.sem("turned_hi"), sc.sem("turned_lo")
        q_made, q_hi, q_lo = sc.sem("q_made"), sc.sem("q_hi"), sc.sem("q_lo")
        s_made, s_taken = sc.sem("s_made"), sc.sem("s_taken")
        max_turned, max_ready = sc.sem("max_turned"), sc.sem("max_ready")
        st_made, exp_done = sc.sem("st_made"), sc.sem("exp_done")
        av_made, av_recip, av_taken = sc.sem("av_made"), sc.sem("av_recip"), sc.sem("av_taken")
        a_turned, a_hi, a_lo = sc.sem("a_turned"), sc.sem("a_hi"), sc.sem("a_lo")
        o_made, x_ready = sc.sem("o_made"), sc.sem("x_ready")
        new_turned, new_out = sc.sem("new_turned"), sc.sem("new_out")
        lg_made, lg_out = sc.sem("lg_made"), sc.sem("lg_out")
        cleared, passed = sc.sem("cleared"), sc.sem("passed")
        block = ctx.enter_context(nc.Block())

        def batches(eng, body, close=None):
            body(0, 0, 0, True, False)
            with eng.Fori(0, (B - 2) // 2) as r:
                body(r * 2 + 1, 1, r, False, False)
                body(r * 2 + 2, 0, r + 1, False, False)
            body(B - 1, 1, B // 2 - 1, False, True)
            if close:
                close(B)

        @block.sync
        def _(sp):
            def load(b, p, half):
                after(sp, norm_in, done(TT, b - 1, 0))
                after(sp, bias_done, b - 1)
                sp.dma_start(x_in[:, p, :, :], src[bass.ds(b, 1), :, :].rearrange("o (t p) d -> p (o t) d", p=P)).then_inc(x_loaded[p], 16)

            def store(b, p, half):
                sp.wait_ge(x_ready, done(KC, b, KC))
                sp.dma_start(dst[bass.ds(b, 1), :, :].rearrange("o (t p) d -> p (o t) d", p=P), x_new[:, p, :, :]).then_inc(stored[p], 16)
                sp.wait_ge(norm_out, done(TT, b, TT))
                sp.dma_start(dst_normed[bass.ds(b, 1), :, :].rearrange("o (t p) d -> p (o t) d", p=P),
                             normed_new[:, p, :, :]).then_inc(stored[p], 16)

            def body(b, p, half, first, last):
                if first:
                    load(0, 0, 0)
                if not last:
                    load(b + 1, 1 - p, half + p)
                if not first:
                    store(b - 1, 1 - p, half + p - 1)
            batches(sp, body, lambda n: store(n - 1, 1, B // 2 - 1))
            for p in range(2):
                sp.wait_ge(stored[p], 16 * STORES * (B // 2))

        @block.gpsimd
        def _(pool):
            pool.memset(maxT[:, :].bitcast(F32), 0.0).then_inc(cleared, 1)
            pool.memset(v_cur[:, :, NP * 2 * VW:], 0.0).then_inc(cleared, 1)
            if masked:
                pool.memset(mask_cur[:, :, :], 0.0).then_inc(cleared, 1)

            def input_side(b, p, half):
                pool.wait_ge(x_loaded[p], 16 * (half + 1))
                after(pool, x_ready, done(KC, b - 1, 0))
                bo = kv["bo"][:, :].unsqueeze(1).to_broadcast([P, TT, D])
                pool.tensor_tensor(x_bias[:, p, :, :], x_in[:, p, :, :], bo, ALU.add).then_inc(bias_done, 1)
                after(pool, av_made, done(TT, b - 1, 0))
                pool.sem_inc(passed, 1)
                pool.tensor_copy(v_cur[:, p, 0:NP * 2 * VW], kv["v"][:, bass.ds(b, 1), :, :].rearrange("p o j c -> p (o j c)")).then_inc(v_ready, 1)
                after(pool, st_made, done(NP, b - 1, 0))
                hm = const["headmask"][:, :].unsqueeze(2).to_broadcast([P, HH, SK])
                for c in range(KC):
                    for out, k in ((kb_hi, kv["kT_hi"]), (kb_lo, kv["kT_lo"])):
                        cols = k[:, c, bass.ds(b * SK, SK)].bitcast(F32).unsqueeze(1).to_broadcast([P, HH, SK])
                        pool.tensor_tensor(out[:, p, c, :, :], cols, hm, ALU.mult).then_inc(kb_ready, 1)

            def body(b, p, half, first, last):
                if first:
                    input_side(0, 0, 0)
                if not last:
                    input_side(b + 1, 1 - p, half + p)
            batches(pool, body)

        @block.tensor
        def _(pe):
            def turn_input(b, p):
                pe.wait_ge(norm_in, done(TT, b, TT))
                after(pe, a_lo, b - 1)
                for c in range(KC):
                    for t in range(TT):
                        m = pe.transpose(psum[:, c, t * P:(t + 1) * P], normed[:, t, c * P:(c + 1) * P], ident[:, :])
                m.then_inc(turned, 1)

            def queries(b, p):
                pe.wait_ge(turned_lo, b + 1)
                for m in range(KC):
                    for c in range(KC):
                        cols = slice(m * P, (m + 1) * P)
                        q = three_passes(pe, psum[:, m, :], kv["wq_hi"][:, c, cols], kv["wq_lo"][:, c, cols],
                                         nT_hi[:, c, :], nT_lo[:, c, :], c == 0, c == KC - 1)
                    q.then_inc(q_made, 1)

            def maxima(b, p, tiles):
                if 0 in tiles:
                    pe.wait_ge(q_hi, done(KC, b, KC))
                    pe.wait_ge(kb_ready, done(2 * KC, b, 2 * KC))
                    after(pe, max_ready, b)
                    if masked:
                        pe.wait_ge(mask_ready, b + 1)
                for t in tiles:
                    for c in range(KC):
                        after(pe, s_taken, done(TT * KC, b, t * KC + c - 1))
                        m = pe.matmul(psum[:, 2 + c, :], qT_hi[:, p, c, t * P:(t + 1) * P], kb_hi[:, p, c, :, :],
                                      start=True, stop=not masked)
                        if masked:
                            m = pe.matmul(psum[:, 2 + c, :], mask_cur[:, p, t * P:(t + 1) * P], const["keysel"][:, :, :],
                                          start=False, stop=True)
                        m.then_inc(s_made, 1)

            def turn_maxima(b):
                pe.wait_ge(s_taken, done(TT * KC, b, TT * KC))
                for t in range(TT):
                    m = pe.transpose(psum[0:H, 3, t * P:(t + 1) * P], s_max[:, t, :], ident[:, :])
                m.then_inc(max_turned, 1)

            def scores(b, p, pairs):
                if 0 in pairs:
                    pe.wait_ge(q_lo, done(KC, b, KC))
                    pe.wait_ge(max_ready, b + 1)
                    after(pe, lg_out, b - 1)
                for j in pairs:
                    after(pe, exp_done, done(NP, b, j - 1))
                    c, heads = j // (NP // KC), slice(2 * (j % (NP // KC)), 2 * (j % (NP // KC)) + 2)
                    out = psum[:, 4 + j % 2, :]
                    three_passes(pe, out, kb_hi[:, p, c, heads, :], kb_lo[:, p, c, heads, :],
                                 qT_hi[:, p, c, :], qT_lo[:, p, c, :], True, False)
                    if masked:
                        pe.matmul(out, const["keysel"][:, 0:2, :], mask_cur[:, p, :], start=False, stop=False)
                    pe.matmul(out, const["negsel"][:, j, :], maxT[:, :], start=False, stop=True).then_inc(st_made, 1)

            def weighted_values(b, p):
                pe.wait_ge(exp_done, done(NP, b, NP))
                pe.wait_ge(v_ready, b + 1)
                after(pe, x_ready, done(KC, b, 0))
                for t in range(TT):
                    if t >= 2:
                        pe.wait_ge(av_taken, done(TT, b, t - 1))
                    for j in range(NP):
                        cols = slice(j * 2 * VW, j * 2 * VW + PE_COLS)
                        m = pe.matmul(psum[:, 6 + t % 2, cols], probs[:, j, t * P:(t + 1) * P], v_cur[:, p, cols],
                                      start=True, stop=True)
                    m.then_inc(av_made, 1)

            def turn_attention(b, first):
                pe.wait_ge(av_taken, done(TT, b, TT))
                if not first:
                    pe.wait_ge(new_out, b)
                else:
                    pe.wait_ge(q_lo, 2 * KC)
                for c in range(KC):
                    for t in range(TT):
                        m = pe.transpose(psum[:, c, t * P:(t + 1) * P], att[:, t, c * P:(c + 1) * P], ident[:, :])
                m.then_inc(a_turned, 1)

            def outputs(b):
                pe.wait_ge(a_lo, b + 1)
                for t in range(TT):
                    for c in range(KC):
                        rows = slice(t * P, (t + 1) * P)
                        m = three_passes(pe, psum[:, 6 + t // 2, (t % 2) * D:(t % 2 + 1) * D], aT_hi[:, c, rows], aT_lo[:, c, rows],
                                         kv["wo_hi"][:, c, :], kv["wo_lo"][:, c, :], c == 0, c == KC - 1)
                    if t % 2:
                        m.then_inc(o_made, 1)

            def route(b, last):
                pe.wait_ge(new_out, b + 1)
                if not last:
                    pe.wait_ge(exp_done, done(NP, b + 1, NP - 1))
                for t in range(TT):
                    for c in range(KC):
                        m = pe.matmul(psum[:, 4, t * PE_COLS:(t + 1) * PE_COLS], newT[:, c, t * P:(t + 1) * P], kv["wr"][:, c, :],
                                      start=(c == 0), stop=(c == KC - 1))
                m.then_inc(lg_made, 1)

            pe.wait_ge(cleared, 3 if masked else 2)

            def body(b, p, half, first, last):
                if first:
                    turn_input(0, 0)
                    queries(0, 0)
                    maxima(0, 0, range(TT))
                    turn_maxima(0)
                scores(b, p, range(0, 4))
                if not last:
                    turn_input(b + 1, 1 - p)
                scores(b, p, range(4, 6))
                if not last:
                    queries(b + 1, 1 - p)
                scores(b, p, range(6, 8))
                if not last:
                    maxima(b + 1, 1 - p, range(0, 2))
                if not first:
                    if last:
                        pe.wait_ge(a_lo, b)
                        turn_new_last(b - 1, 1 - p)
                    else:
                        turn_new(b - 1, 1 - p, b)
                weighted_values(b, p)
                if not first:
                    route(b - 1, False)
                if not last:
                    maxima(b + 1, 1 - p, range(2, 4))
                turn_attention(b, first)
                if not last:
                    turn_maxima(b + 1)
                outputs(b)

            def turn_new(b, p, now):
                pe.wait_ge(norm_out, done(TT, b, TT))
                pe.wait_ge(q_lo, done(KC, now + 1, KC))
                new_transposes(b, p)

            def turn_new_last(b, p):
                pe.wait_ge(norm_out, done(TT, b, TT))
                new_transposes(b, p)

            def new_transposes(b, p):
                for c in range(KC):
                    for t in range(TT):
                        m = pe.transpose(psum[:, c, t * P:(t + 1) * P], normed_new[:, p, t, c * P:(c + 1) * P], ident[:, :])
                m.then_inc(new_turned, 1)

            def close(n):
                pe.wait_ge(a_lo, n)
                turn_new_last(n - 1, 1)
                route(n - 1, True)
            batches(pe, body, close)

        @block.scalar
        def _(act):
            def input_hi(b, p):
                act.wait_ge(turned, b + 1)
                after(act, q_made, done(KC, b, 0))
                act.activation(nT_hi[:, :, :], psum[:, 0:KC, :], ACT.Copy).then_inc(turned_hi, 1)

            def queries_hi(b, p):
                for m in range(KC):
                    act.wait_ge(q_made, done(KC, b, m + 1))
                    act.activation(qT_hi[:, p, m, :], psum[:, m, :], ACT.Identity, bias=kv["bq"][:, m:m + 1]).then_inc(q_hi, 1)

            def exps(b, pairs):
                if 0 in pairs:
                    after(act, av_made, done(TT, b, 0))
                for j in pairs:
                    act.wait_ge(st_made, done(NP, b, j + 1))
                    act.activation(probs[:, j, :], psum[:, 4 + j % 2, :], ACT.Exp, scale=DH ** -0.5).then_inc(exp_done, 1)

            def new_copy(b):
                act.wait_ge(new_turned, b + 1)
                after(act, lg_made, b)
                act.activation(newT[:, :, :], psum[:, 0:KC, :], ACT.Copy).then_inc(new_out, 1)

            def new_norm(b, p, half):
                act.wait_ge(ln_out, done(LN_STEPS + 1, b, LN_STEPS + 1))
                after(act, stored[p], half * (16 * STORES))
                after(act, new_turned, b)
                for t in range(TT):
                    act.activation(normed_new[:, p, t, :], x_new[:, p, t, :], ACT.Identity, bias=shift2[:, t:t + 1],
                                   scale=rstd2[:, t:t + 1]).then_inc(norm_out, 1)

            def attention_hi(b):
                act.wait_ge(a_turned, b + 1)
                after(act, o_made, done(KC, b, 0))
                act.activation(aT_hi[:, :, :], psum[:, 0:KC, :], ACT.Copy).then_inc(a_hi, 1)

            def body(b, p, half, first, last):
                if first:
                    input_hi(0, 0)
                    queries_hi(0, 0)
                exps(b, range(0, 4))
                if not last:
                    input_hi(b + 1, 1 - p)
                exps(b, range(4, 6))
                if not last:
                    queries_hi(b + 1, 1 - p)
                exps(b, range(6, 8))
                if not first:
                    new_norm(b - 1, 1 - p, half + p - 1)
                    new_copy(b - 1)
                attention_hi(b)

            def close(n):
                new_norm(n - 1, 1, B // 2 - 1)
                new_copy(n - 1)
            batches(act, body, close)

        @block.vector
        def _(dve):
            dve.wait_ge(cleared, 3 if masked else 2)

            def input_stats(b, p, half):
                dve.wait_ge(x_loaded[p], 16 * (half + 1))
                after(dve, norm_in, done(TT, b, 0))
                if masked:
                    after(dve, st_made, done(NP, b - 1, 0))
                    dve.tensor_scalar(mask_cur[0:SK, p, :], kv["mask"][:, :], kv["pad"][:, bass.ds(b, 1)], -BIG,
                                      ALU.mult, ALU.add).then_inc(mask_ready, 1)
                layernorm_stats(dve, x_in[:, p, :, :], stats, mv, rstd[:, :], tmp, ln_in, b * LN_STEPS, passed)
                dve.wait_ge(ln_in, done(LN_STEPS, b, LN_STEPS))
                after(dve, turned, b)
                for t in range(TT):
                    dve.tensor_scalar(normed[:, t, :], x_in[:, p, t, :], mv[:, t, 0:1], rstd[:, t:t + 1],
                                      ALU.subtract, ALU.mult).then_inc(norm_in, 1)

            def input_lo(b):
                dve.wait_ge(turned_hi, b + 1)
                dve.tensor_tensor(nT_lo[:, :, :], psum[:, 0:KC, :], nT_hi[:, :, :].bitcast(F32), ALU.subtract).then_inc(turned_lo, 1)

            def queries_lo(b, p):
                for m in range(KC):
                    dve.wait_ge(q_hi, done(KC, b, m + 1))
                    dve.scalar_tensor_tensor(qT_lo[:, p, m, :], psum[:, m, :], kv["bq"][:, m:m + 1],
                                             qT_hi[:, p, m, :].bitcast(F32), ALU.add, ALU.subtract).then_inc(q_lo, 1)

            def maxima(b, tiles):
                if 0 in tiles:
                    after(dve, max_turned, b)
                for t in tiles:
                    for c in range(KC):
                        dve.wait_ge(s_made, done(TT * KC, b, t * KC + c + 1))
                        s = psum[:, 2 + c, :].rearrange("p (h k) -> p h k", k=SK)
                        dve.tensor_reduce(s_max[:, t, c * HH:(c + 1) * HH], s, AX.X, ALU.max).then_inc(s_taken, 1)

            def maxima_copy(b):
                dve.wait_ge(max_turned, b + 1)
                after(dve, st_made, done(NP, b, 0))
                dve.tensor_copy(maxT[0:H, :], psum[0:H, 3, :]).then_inc(max_ready, 1)

            def normalise(b):
                after(dve, a_turned, b)
                for t in range(TT):
                    dve.wait_ge(av_made, done(TT, b, t + 1))
                    av = psum[:, 6 + t % 2, 0:H * VW].rearrange("p (h c) -> p h c", c=VW)
                    dve.reciprocal(recip[:, t, :], av[:, :, DH]).then_inc(av_recip, 1)
                    dve.wait_ge(av_recip, done(TT, b, t + 1))
                    dve.tensor_tensor(att[:, t, :].rearrange("p (h c) -> p h c", c=DH), av[:, :, 0:DH],
                                      recip[:, t, :].unsqueeze(2).to_broadcast([P, H, DH]), ALU.mult).then_inc(av_taken, 1)

            def router_copy(b):
                dve.wait_ge(lg_made, b + 1)
                dve.tensor_copy(logits_all[:, bass.ds(b * TT, TT), :], psum[:, 4, 0:TT * PE_COLS].rearrange("p (t e) -> p t e", e=PE_COLS)[:, :, 0:8]).then_inc(lg_out, 1)

            def attention_lo(b):
                dve.wait_ge(a_hi, b + 1)
                dve.tensor_tensor(aT_lo[:, :, :], psum[:, 0:KC, :], aT_hi[:, :, :].bitcast(F32), ALU.subtract).then_inc(a_lo, 1)

            def residual(b, p, half):
                dve.wait_ge(bias_done, b + 1)
                after(dve, stored[p], half * (16 * STORES))
                after(dve, norm_out, done(TT, b - 1, 0))
                for n in range(KC):
                    dve.wait_ge(o_made, done(KC, b, n + 1))
                    tiles = slice(2 * n, 2 * n + 2)
                    dve.tensor_tensor(x_new[:, p, tiles, :], psum[:, 6 + n, :].rearrange("p (t d) -> p t d", d=D),
                                      x_bias[:, p, tiles, :], ALU.add).then_inc(x_ready, 1)

            def new_stats(b, p):
                dve.wait_ge(x_ready, done(KC, b, KC))
                after(dve, norm_out, done(TT, b, 0))
                layernorm_stats(dve, x_new[:, p, :, :], stats2, mv2, rstd2[:, :], tmp2, ln_out, b * (LN_STEPS + 1), passed)
                dve.wait_ge(ln_out, done(LN_STEPS + 1, b, LN_STEPS))
                dve.scalar_tensor_tensor(shift2[:, :], mv2[:, :, 0], -1.0, rstd2[:, :], ALU.mult, ALU.mult).then_inc(ln_out, 1)

            def body(b, p, half, first, last):
                if first:
                    input_stats(0, 0, 0)
                    input_lo(0)
                    queries_lo(0, 0)
                    maxima(0, range(TT))
                    maxima_copy(0)
                if not last:
                    input_stats(b + 1, 1 - p, half + p)
                    input_lo(b + 1)
                if not first:
                    new_stats(b - 1, 1 - p)
                if not last:
                    queries_lo(b + 1, 1 - p)
                    maxima(b + 1, range(0, 2))
                normalise(b)
                if not first:
                    router_copy(b - 1)
                if not last:
                    maxima(b + 1, range(2, 4))
                attention_lo(b)
                if not last:
                    maxima_copy(b + 1)
                residual(b, p, half)

            def close(n):
                new_stats(n - 1, 1)
                router_copy(n - 1)
            batches(dve, body, close)


def alloc_layer(sc, masked):
    kv = {"masked": masked, "name": sc.phase}
    for n in ("kT_hi", "kT_lo"):
        kv[n] = sc.sb(n, [P, KC, B * SK], F32R)
    for n in ("wq_hi", "wq_lo", "wo_hi", "wo_lo"):
        kv[n] = sc.sb(n, [P, KC, D], F32R)
    kv["v"] = sc.sb("v_aug", [P, B, NP, 2 * VW])
    kv["bo"] = sc.sb("bo_bcast", [P, D])
    kv["bk"], kv["bq"] = sc.sb("bk_col", [P, KC]), sc.sb("bq_col", [P, KC])
    kv["wr"] = sc.sb("wr_sb", [P, KC, PE_COLS])
    if masked:
        kv["mask"], kv["pad"] = sc.sb("mask_keep", [SK, S], BF16), sc.sb("pad_keep", [SK, B])
    return kv


E = 8
TOPK = N_TOK // E
SLOT = 32
TOP_BIT = 29
F = 682
GROUPS_UP = 4
FC = -(-F // P)
FR = F - (FC - 1) * P
ROW = D + E
CHUNKS = P // E


def route_expert_choice(nc, const, psum, logits, br, rows_dram, thresh_dram, idx):
    with ExitStack() as ctx:
        sc = Scope(nc, ctx, "choice", const)
        bias = sc.sb("bias", [P, E])
        top, total = sc.sb("top", [P, NT]), sc.sb("total", [P, NT])
        score = sc.sb("score", [P, NT, E])
        by_e = sc.sb("by_e", [P, E, NT])
        turned = sc.sb("turned", [P, 4, P])
        hits = sc.sb("hits", [P, 4 * P], BF16)
        count, found, bit, cand, add = (sc.sb(n, [P, 1], d) for n, d in
                                        (("count", F32), ("found", I32), ("bit", I32), ("cand", I32), ("add", I32)))
        limits = sc.sb("limits", [P, 1], I32)
        same_e, before, ones = sc.sb("same_e", [P, E, CHUNKS]), sc.sb("before", [P, P], BF16), sc.sb("ones", [P, P], BF16)
        thresh = sc.sb("thresh", [P, P])
        above, equal, chosen = sc.sb("above", [P, E, NT], BF16), sc.sb("equal", [P, E, NT], BF16), sc.sb("chosen", [P, E, NT], BF16)
        keep_on = sc.sb("keep_on", [P, E, NT])
        run, rank, want = sc.sb("run", [P, E, NT]), sc.sb("rank", [P, E, NT]), sc.sb("want", [P, E])
        pos, part = sc.sb("pos", [P, E, NT], I32), sc.sb("part", [P, E, NT], I32)
        high, low = sc.sb("high", [P, E, NT]), sc.sb("low", [P, E, NT])
        slot_no, tile_no = sc.sb("slot_no", [P, SLOT]), sc.sb("tile_no", [P, NT])
        lane_no = sc.sb("lane_no", [P, 1])
        one_high = sc.sb("one_high", [P, 2, NT, SLOT], BF16)
        one_low = sc.sb("one_low", [P, 2, NT, SLOT], BF16)
        coded = sc.sb("coded", [P, 2, NT, 2, SLOT], BF16)
        listed = sc.sb("listed", [SLOT, E, 2, SLOT])

        made = sc.sem("made")
        bias_loaded, scores_stored = sc.sem("bias_loaded"), sc.sem("scores_stored")
        th_stored, th_loaded = sc.sem("th_stored"), sc.sem("th_loaded")
        step, exps, sums = sc.sem("step"), sc.sem("exps"), sc.sem("sums")
        t_made, counted = sc.sem("t_made"), sc.sem("counted")
        hit, decided = sc.sem("hit"), sc.sem("decided")
        found_all = sc.sem("found_all")
        high_made, low_made, lane_made, tile_made, list_made = (sc.sem(n) for n in ("high_made", "low_made", "lane_made", "tile_made", "list_made"))
        block = ctx.enter_context(nc.Block())

        @block.sync
        def _(sp):
            sp.dma_start(bias[:, :], br.partition_broadcast(P)).then_inc(bias_loaded, 16)
            sp.wait_ge(step, 6)
            sp.dma_start(rows_dram.rearrange("(t p) r -> p t r", p=P)[:, :, D:ROW], score[:, :, :]).then_inc(scores_stored, 16)
            sp.wait_ge(found_all, 1)
            sp.dma_start(thresh_dram.rearrange("(p o) -> p o", o=1), limits[:, :].bitcast(F32)).then_inc(th_stored, 16)
            sp.wait_ge(th_stored, 16)
            sp.dma_start(thresh[:, :], thresh_dram.partition_broadcast(P)).then_inc(th_loaded, 16)
            sp.wait_ge(scores_stored, 16)
            sp.wait_ge(th_loaded, 16)

        @block.gpsimd
        def _(pool):
            pool.memset(same_e[:, :, :], 1.0).then_inc(made, 1)
            pool.memset(before[:, :], 1.0).then_inc(made, 1)
            pool.memset(ones[:, :], 1.0).then_inc(made, 1)
            pool.memset(keep_on[:, :, :], 1.0).then_inc(made, 1)
            pool.iota(slot_no[:, :], pattern=[[1, SLOT]], base=0, channel_multiplier=0, allow_small_or_imprecise_dtypes=True).then_inc(made, 1)
            pool.iota(tile_no[:, :], pattern=[[1, NT]], base=0, channel_multiplier=0, allow_small_or_imprecise_dtypes=True).then_inc(made, 1)
            pool.iota(lane_no[:, :], pattern=[[0, 1]], base=0, channel_multiplier=1, allow_small_or_imprecise_dtypes=True).then_inc(made, 1)
            pool.wait_ge(made, 7)
            pool.memset(keep_on[:, :, 0:1], 0.0).then_inc(made, 1)
            pool.affine_select(out=before[:, :], in_=before[:, :], compare_op=ALU.is_gt, fill=0.0, base=0,
                               pattern=[[1, P]], channel_multiplier=-1).then_inc(made, 1)
            pool.affine_select(out=same_e[:, :, :], in_=same_e[:, :, :], compare_op=ALU.is_ge, fill=0.0, base=0,
                               pattern=[[-CHUNKS, E], [0, CHUNKS]], channel_multiplier=1).then_inc(made, 1)
            pool.wait_ge(made, 10)
            pool.affine_select(out=same_e[:, :, :], in_=same_e[:, :, :], compare_op=ALU.is_ge, fill=0.0, base=CHUNKS - 1,
                               pattern=[[CHUNKS, E], [0, CHUNKS]], channel_multiplier=-1).then_inc(made, 1)
            tiles = tile_no[:, :].unsqueeze(2).to_broadcast([P, NT, SLOT])
            for e in range(E):
                pool.wait_ge(low_made, e + 1)
                if e >= 2:
                    pool.wait_ge(list_made, e - 1)
                pool.tensor_tensor(coded[:, e % 2, :, 1, :], one_low[:, e % 2, :, :], tiles, ALU.mult).then_inc(tile_made, 1)

        @block.scalar
        def _(act):
            act.wait_ge(step, 3)
            act.activation(score[:, :, :], score[:, :, :], ACT.Exp).then_inc(exps, 1)
            for e in range(E):
                act.wait_ge(low_made, e + 1)
                if e >= 2:
                    act.wait_ge(list_made, e - 1)
                act.activation(coded[:, e % 2, :, 0, :], one_low[:, e % 2, :, :], ACT.Copy, scale=lane_no[:, 0:1]).then_inc(lane_made, 1)

        @block.tensor
        def _(pe):
            pe.wait_ge(step, 7)
            for r in range(4):
                t = pe.transpose(psum[:, 0, r * P:(r + 1) * P], by_e[:, :, r::4], const["ident"][:, :])
            t.then_inc(t_made, 1)
            pe.wait_ge(made, 11)
            with pe.Fori(0, TOP_BIT + 1) as i:
                pe.wait_ge(hit, i + 1)
                pe.matmul(psum[:, 1, 0:1], same_e[:, :, :], count[:, :], start=True, stop=True).then_inc(counted, 1)
            for n, x in enumerate((above, equal, chosen)):
                pe.wait_ge(sums, n + 1)
                pe.matmul(psum[:, 2 + 2 * n, :], before[:, :], x[:, :, :], start=True, stop=True)
                pe.matmul(psum[:, 3 + 2 * n if n < 2 else 0, :], ones[:, :], x[:, :, :], start=True, stop=True).then_inc(counted, 1)
            for e in range(E):
                pe.wait_ge(high_made, e + 1)
                pe.wait_ge(lane_made, e + 1)
                pe.wait_ge(tile_made, e + 1)
                for t in range(NT):
                    m = pe.matmul(psum[0:SLOT, 1, e * 2 * SLOT:(e + 1) * 2 * SLOT], one_high[:, e % 2, t, :],
                                  coded[:, e % 2, t, :, :], start=(t == 0), stop=(t == NT - 1))
                m.then_inc(list_made, 1)

        @block.vector
        def _(dve):
            n = 0

            def then(instruction):
                nonlocal n
                instruction.then_inc(step, 1)
                n += 1
                dve.wait_ge(step, n)

            def over_e(x):
                return x.unsqueeze(2).to_broadcast([P, NT, E])

            def over_t(x):
                return x.unsqueeze(2).to_broadcast([P, E, NT])

            dve.wait_ge(bias_loaded, 16)
            then(dve.tensor_tensor(score[:, :, :], logits[:, :, :], bias[:, :].unsqueeze(1).to_broadcast([P, NT, E]), ALU.add))
            then(dve.tensor_reduce(top[:, :], score[:, :, :], AX.X, ALU.max))
            then(dve.tensor_tensor(score[:, :, :], score[:, :, :], over_e(top[:, :]), ALU.subtract))
            dve.wait_ge(exps, 1)
            then(dve.tensor_reduce(total[:, :], score[:, :, :], AX.X, ALU.add))
            then(dve.reciprocal(total[:, :], total[:, :]))
            then(dve.tensor_tensor(score[:, :, :], score[:, :, :], over_e(total[:, :]), ALU.mult))
            then(dve.tensor_copy(by_e[:, :, :], score[:, :, :].rearrange("p t e -> p e t")))
            then(dve.memset(found[:, :], 0))
            then(dve.memset(bit[:, :], 1 << TOP_BIT))
            then(dve.memset(cand[:, :], 1 << TOP_BIT))
            dve.wait_ge(t_made, 1)
            then(dve.tensor_copy(turned[:, :, :], psum[:, 0, :].rearrange("p (r q) -> p r q", r=4)))
            with dve.Fori(0, TOP_BIT + 1) as i:
                dve.tensor_scalar(hits[:, :], turned[:, :, :].rearrange("p r q -> p (r q)"), cand[:, :].bitcast(F32), 0.0,
                                  ALU.is_ge, ALU.add, accum_out=count[:, :]).then_inc(hit, 1)
                dve.wait_ge(counted, i + 1)
                dve.scalar_tensor_tensor(add[:, :], psum[:, 1, 0:1], float(TOPK), bit[:, :], ALU.is_ge, ALU.mult).then_inc(decided, 1)
                dve.wait_ge(decided, i * 4 + 1)
                dve.tensor_tensor(found[:, :], found[:, :], add[:, :], ALU.bitwise_or).then_inc(decided, 1)
                dve.tensor_scalar(bit[:, :], bit[:, :], 1, None, ALU.logical_shift_right).then_inc(decided, 1)
                dve.wait_ge(decided, i * 4 + 3)
                dve.tensor_tensor(cand[:, :], found[:, :], bit[:, :], ALU.bitwise_or).then_inc(decided, 1)
                dve.wait_ge(decided, i * 4 + 4)
            dve.tensor_copy(limits[:, :], found[:, :]).then_inc(found_all, 1)
            dve.wait_ge(th_loaded, 16)
            dve.wait_ge(made, 11)
            limit = over_t(thresh[:, 0::CHUNKS])
            then(dve.tensor_tensor(above[:, :, :], by_e[:, :, :], limit, ALU.is_gt))
            dve.tensor_tensor(equal[:, :, :], by_e[:, :, :], limit, ALU.is_equal).then_inc(sums, 1)
            dve.wait_ge(sums, 1)
            dve.tensor_copy(add[:, :], found[:, :]).then_inc(sums, 1)
            dve.wait_ge(counted, TOP_BIT + 2)

            def flat(bank):
                return psum[:, bank, :].rearrange("p (e t) -> p e t", e=E)

            def ranks(within, totals):
                then(dve.tensor_copy(rank[:, :, :], flat(totals)))
                then(dve.tensor_tensor_scan(run[:, :, :].rearrange("p e t -> p (e t)"), keep_on[:, :, :].rearrange("p e t -> p (e t)"),
                                            rank[:, :, :].rearrange("p e t -> p (e t)"), 0.0, ALU.mult, ALU.add))
                then(dve.tensor_tensor(run[:, :, :], run[:, :, :], rank[:, :, :], ALU.subtract))
                then(dve.tensor_tensor(rank[:, :, :], flat(within), run[:, :, :], ALU.add))

            then(dve.tensor_reduce(want[:, :], flat(3), AX.X, ALU.add))
            then(dve.tensor_scalar(want[:, :], want[:, :], -1.0, float(TOPK), ALU.mult, ALU.add))
            dve.wait_ge(counted, TOP_BIT + 3)
            ranks(4, 5)
            then(dve.tensor_tensor(rank[:, :, :], rank[:, :, :], over_t(want[:, :]), ALU.is_lt))
            then(dve.tensor_tensor(rank[:, :, :], rank[:, :, :], equal[:, :, :], ALU.mult))
            then(dve.tensor_tensor(chosen[:, :, :], rank[:, :, :], above[:, :, :], ALU.add))
            dve.tensor_copy(add[:, :], found[:, :]).then_inc(sums, 1)
            dve.wait_ge(counted, TOP_BIT + 4)
            ranks(6, 0)
            then(dve.tensor_copy(pos[:, :, :], rank[:, :, :]))
            then(dve.tensor_scalar(part[:, :, :], pos[:, :, :], 5, None, ALU.logical_shift_right))
            then(dve.scalar_tensor_tensor(high[:, :, :], part[:, :, :], 1.0, chosen[:, :, :], ALU.add, ALU.mult))
            then(dve.tensor_scalar(high[:, :, :], high[:, :, :], -1.0, None, ALU.add))
            then(dve.tensor_scalar(part[:, :, :], pos[:, :, :], SLOT - 1, None, ALU.bitwise_and))
            then(dve.tensor_copy(low[:, :, :], part[:, :, :]))
            numbers = slot_no[:, :].unsqueeze(1).to_broadcast([P, NT, SLOT])
            for e in range(E):
                if e >= 2:
                    dve.wait_ge(list_made, e - 1)
                dve.tensor_tensor(one_low[:, e % 2, :, :], low[:, e, :].unsqueeze(2).to_broadcast([P, NT, SLOT]), numbers,
                                  ALU.is_equal).then_inc(low_made, 1)
                dve.tensor_tensor(one_high[:, e % 2, :, :], high[:, e, :].unsqueeze(2).to_broadcast([P, NT, SLOT]), numbers,
                                  ALU.is_equal).then_inc(high_made, 1)
            dve.wait_ge(list_made, E)
            then(dve.tensor_copy(listed[:, :, :, :], psum[0:SLOT, 1, :].rearrange("s (e c l) -> s e c l", e=E, c=2)))
            for q in range(P // SLOT):
                cols = slice(q * 8, (q + 1) * 8)
                then(dve.scalar_tensor_tensor(idx[q * SLOT:(q + 1) * SLOT, :, :], listed[:, :, 1, cols], float(P), listed[:, :, 0, cols],
                                              ALU.mult, ALU.add))


FP = FC * P
BIAS_ROW = 64
assert FR <= BIAS_ROW
EP = E // GROUPS_UP
HALF = TOPK // 2
HT = HALF // P
GJ = 2 * EP
PAIRS = FC // 2


def expert_choice_mixture(nc, const, psum, idx, x, x_normed, w_up, b_up, w_down):
    with ExitStack() as ctx:
        sc = Scope(nc, ctx, "moe", const)
        rows = sc.sb("rows", [P, GJ, HT, ROW])
        gates = sc.sb("gates", [P, GJ, HT])
        idx_get, idx_add = sc.sb("idx_get", [P, EP, 2 * HT], I32), sc.sb("idx_add", [P, EP, 2 * HT], I32)
        wu, wd = sc.sb("wu", [P, KC, FP]), sc.sb("wd", [P, FC, D])
        wu_hi, wu_lo = sc.sb("wu_hi", [P, KC, FP], F32R), sc.sb("wu_lo", [P, KC, FP], F32R)
        wd_hi, wd_lo = sc.sb("wd_hi", [P, EP, FC, D], F32R), sc.sb("wd_lo", [P, EP, FC, D], F32R)
        bu, bu_in = sc.sb("bu", [P, FC]), sc.sb("bu_in", [P, FC])
        xT_hi, xT_lo = sc.sb("xT_hi", [P, 2, KC, HALF], F32R), sc.sb("xT_lo", [P, 2, KC, HALF], F32R)
        mid = sc.sb("mid", [P, FC, HALF])
        mid_hi, mid_lo = sc.sb("mid_hi", [P, 2, FC, HALF], F32R), sc.sb("mid_lo", [P, 2, FC, HALF], F32R)
        y = sc.sb("y", [P, 2, HT, D])

        gates_copied = sc.sem("gates_copied")
        rows_in = [sc.sem(f"rows_in{j}") for j in range(GJ)]
        added = [sc.sem(f"added{p}") for p in range(2)]
        get_copied, add_copied = sc.sem("get_copied"), sc.sem("add_copied")
        wu_in, wd_in, wu_hi_made, wd_hi_made = sc.sem("wu_in"), sc.sem("wd_in"), sc.sem("wu_hi_made"), sc.sem("wd_hi_made")
        wu_ready, wd_ready = sc.sem("wu_ready"), sc.sem("wd_ready")
        turned, xT_hi_made, xT_ready = sc.sem("turned"), sc.sem("xT_hi_made"), sc.sem("xT_ready")
        up_made, silu_made = sc.sem("up_made"), sc.sem("silu_made")
        hi_made, lo_made = sc.sem("hi_made"), sc.sem("lo_made")
        down_made = [sc.sem(f"down_made{p}") for p in range(2)]
        y_made = sc.sem("y_made")
        cleared, passed, bu_copied = sc.sem("cleared"), sc.sem("passed"), sc.sem("bu_copied")
        block = ctx.enter_context(nc.Block())
        LAST = GROUPS_UP - 1

        def iterations(eng, body):
            with eng.Fori(0, LAST) as q:
                body(q, False)
            body(LAST, True)

        @block.sync
        def _(sp):
            def load_up(q):
                after(sp, wu_ready, q)
                sp.dma_start(wu[:, :, :], w_up[bass.ds(q, 1), :, :].rearrange("o (c p) f -> p (o c) f", p=P)).then_inc(wu_in, 16)
                sp.dma_start(bu_in[:, :], b_up[bass.ds(q, 1), :, :].rearrange("o p c -> p (o c)")).then_inc(wu_in, 16)

            def load_down(e):
                after(sp, wd_ready, e)
                sp.dma_start(wd[:, :, :], w_down[bass.ds(e, 1), :, :].rearrange("o (c p) d -> p (o c) d", p=P)).then_inc(wd_in, 16)
            with sp.Fori(0, GROUPS_UP) as q:
                load_up(q)
                for i in range(EP):
                    load_down(q * EP + i)

        @block.gpsimd
        def _(pool):
            for p in range(2):
                pool.memset(mid_lo[BIAS_ROW:, p, FC - 1, :].bitcast(F32), 0.0).then_inc(cleared, 1)
                pool.memset(mid_hi[BIAS_ROW:, p, FC - 1, :].bitcast(F32), 0.0).then_inc(cleared, 1)
            pool.wait_ge(cleared, 4)
            for p in range(2):
                pool.memset(mid_hi[BIAS_ROW:BIAS_ROW + 1, p, FC - 1, :].bitcast(F32), 1.0).then_inc(cleared, 1)
            pool.wait_ge(cleared, 6)

            def pass_wait():
                pool.sem_inc(passed, 1)

            def gather(e, i, h):
                if h == 0:
                    if not (isinstance(e, int) and e < EP):
                        for k in range(2):
                            pool.wait_ge(rows_in[i * 2 + k], (e - i) * (16 * HT // EP))
                        pass_wait()
                    pool.tensor_copy(idx_get[:, i, :], idx[:, bass.ds(e, 1), :].rearrange("p o r -> p (o r)")).then_inc(get_copied, 1)
                    pool.wait_ge(get_copied, e + 1)
                after(pool, turned, e * 2 + h - 2)
                after(pool, gates_copied, e * 2 + h - 2)
                pass_wait()
                for t in range(HT):
                    at = bass.IndirectOffsetOnAxis(ap=idx_get[:, i, h * HT + t:h * HT + t + 1], axis=0)
                    pool.indirect_dma_start(rows[:, i * 2 + h, t, :], None, x_normed, at, compute_op=ALU.bypass).then_inc(rows_in[i * 2 + h], 16)

            def add(e, i, h):
                for s in range(2):
                    pool.wait_ge(added[s], e * (16 * HT))
                if h == 0:
                    pass_wait()
                    pool.tensor_copy(idx_add[:, i, :], idx[:, bass.ds(e, 1), :].rearrange("p o r -> p (o r)")).then_inc(add_copied, 1)
                    pool.wait_ge(add_copied, e + 1)
                for t in range(HT):
                    pool.wait_ge(y_made, done(HT, e * 2 + h, t + 1))
                    pass_wait()
                    at = bass.IndirectOffsetOnAxis(ap=idx_add[:, i, h * HT + t:h * HT + t + 1], axis=0)
                    pool.indirect_dma_start(x, at, y[:, h, t, :], None, compute_op=ALU.add).then_inc(added[h], 16)

            def body(q, last):
                e = q * EP
                for h in range(2):
                    gather(e + 1, 1, h)
                for h in range(2):
                    if not last:
                        gather(e + EP, 0, h)
                    add(e, 0, h)
                for h in range(2):
                    add(e + 1, 1, h)

            for h in range(2):
                gather(0, 0, h)
            iterations(pool, body)
            for s in range(2):
                pool.wait_ge(added[s], E * 16 * HT)

        @block.tensor
        def _(pe):
            def turn(g, j, q):
                pe.wait_ge(rows_in[j], q * (16 * HT) + 16 * HT)
                after(pe, xT_ready, g)
                for c in range(KC):
                    for t in range(HT):
                        m = pe.transpose(psum[:, c, t * P:(t + 1) * P], rows[:, j, t, c * P:(c + 1) * P], const["ident"][:, :])
                m.then_inc(turned, 1)

            def up(g, p):
                pe.wait_ge(xT_ready, g + 1)
                for f in range(FC):
                    if f == 0:
                        pe.wait_ge(silu_made, g * FC)
                    if f >= 4:
                        pe.wait_ge(silu_made, done(FC, g, f - 3))
                    cols = slice(f * P, (f + 1) * P)
                    for c in range(KC):
                        m = three_passes(pe, psum[:, 2 + f % 4, :], wu_hi[:, c, cols], wu_lo[:, c, cols],
                                         xT_hi[:, p, c, :], xT_lo[:, p, c, :], c == 0, c == KC - 1)
                    m.then_inc(up_made, 1)

            def down(g, p, i):
                pe.wait_ge(y_made, g * HT)
                pe.wait_ge(lo_made, done(PAIRS + 1, g, PAIRS + 1))
                for t in range(HT):
                    rows_t = slice(t * P, (t + 1) * P)
                    for f in range(FC):
                        m = three_passes(pe, psum[:, 6 + t // 2, (t % 2) * D:(t % 2 + 1) * D], mid_hi[:, p, f, rows_t],
                                         mid_lo[:, p, f, rows_t], wd_hi[:, i, f, :], wd_lo[:, i, f, :], f == 0, f == FC - 1)
                    m.then_inc(down_made[p], 1)

            def body(q, last):
                g = q * GJ
                pe.wait_ge(wu_ready, q + 1)
                up(g, 0)
                for j in range(1, GJ):
                    turn(g + j, j, q)
                    up(g + j, j % 2)
                    if j >= 2:
                        if j % 2 == 0:
                            pe.wait_ge(wd_ready, q * EP + j // 2)
                        down(g + j - 2, j % 2, (j - 2) // 2)
                if not last:
                    turn(g + GJ, 0, q + 1)
                pe.wait_ge(wd_ready, q * EP + EP)
                for j in range(GJ - 2, GJ):
                    down(g + j, j % 2, j // 2)

            pe.wait_ge(cleared, 6)
            turn(0, 0, 0)
            iterations(pe, body)

        @block.scalar
        def _(act):
            def rows_hi(g, p):
                act.wait_ge(turned, g + 1)
                act.activation(xT_hi[:, p, :, :], psum[:, 0:KC, :], ACT.Copy).then_inc(xT_hi_made, 1)

            def up_weights(q):
                act.wait_ge(wu_in, q * 32 + 32)
                act.activation(wu_hi[:, :, :], wu[:, :, :], ACT.Copy).then_inc(wu_hi_made, 1)

            def down_weights(e, i):
                act.wait_ge(wd_in, e * 16 + 16)
                for f in range(0, FC, 3):
                    act.activation(wd_hi[:, i, f:f + 3, :], wd[:, f:f + 3, :], ACT.Copy).then_inc(wd_hi_made, 1)

            def hidden(g, p, u):
                act.wait_ge(lo_made, g * (PAIRS + 1))
                for f in range(FC):
                    act.wait_ge(up_made, done(FC, g, f + 1))
                    valid = slice(0, P if f < FC - 1 else BIAS_ROW)
                    act.activation(mid[valid, f, :], psum[valid, 2 + f % 4, :], ACT.Silu, bias=bu[valid, f:f + 1]).then_inc(silu_made, 1)
                    if f % 2:
                        if f == 1:
                            act.wait_ge(down_made[p], u * HT)
                        act.wait_ge(silu_made, done(FC, g, f + 1))
                        if f < FC - 1:
                            act.activation(mid_hi[:, p, f - 1:f + 1, :], mid[:, f - 1:f + 1, :], ACT.Copy).then_inc(hi_made, 1)
                        else:
                            act.activation(mid_hi[:, p, f - 1, :], mid[:, f - 1, :], ACT.Copy).then_inc(hi_made, 1)
                            act.activation(mid_hi[valid, p, f, :], mid[valid, f, :], ACT.Copy).then_inc(hi_made, 1)

            def body(q, last):
                act.wait_ge(wu_ready, q + 1)
                for j in range(GJ):
                    hidden(q * GJ + j, j % 2, q * EP + j // 2)
                    if j < GJ - 1:
                        rows_hi(q * GJ + j + 1, (j + 1) % 2)
                if not last:
                    rows_hi(q * GJ + GJ, 0)
                    up_weights(q + 1)
                    for i in range(EP):
                        act.wait_ge(down_made[1], q * (EP * HT) + (i + 1) * HT)
                        down_weights(q * EP + EP + i, i)

            up_weights(0)
            rows_hi(0, 0)
            for i in range(EP):
                down_weights(i, i)
            iterations(act, body)

        @block.vector
        def _(dve):
            def rows_lo(g, j, e, q):
                p = j % 2
                dve.wait_ge(rows_in[j], q * (16 * HT) + 16 * HT)
                dve.tensor_copy(gates[:, j, :], rows[:, j, :, bass.ds(e + D, 1)].rearrange("p t o -> p (t o)")).then_inc(gates_copied, 1)
                dve.wait_ge(xT_hi_made, g + 1)
                dve.tensor_tensor(xT_lo[:, p, :, :], psum[:, 0:KC, :], xT_hi[:, p, :, :].bitcast(F32), ALU.subtract).then_inc(xT_ready, 1)

            def up_weights(q):
                dve.wait_ge(wu_in, q * 32 + 32)
                dve.tensor_copy(bu[:, :], bu_in[:, :]).then_inc(bu_copied, 1)
                dve.wait_ge(wu_hi_made, q + 1)
                dve.wait_ge(bu_copied, q + 1)
                dve.tensor_tensor(wu_lo[:, :, :], wu[:, :, :], wu_hi[:, :, :].bitcast(F32), ALU.subtract).then_inc(wu_ready, 1)

            def down_weights(e, i):
                dve.wait_ge(wd_hi_made, e * 2 + 2)
                dve.tensor_tensor(wd_lo[:, i, :, :], wd[:, :, :], wd_hi[:, i, :, :].bitcast(F32), ALU.subtract).then_inc(wd_ready, 1)

            def hidden_lo(g, p, u):
                for k in range(PAIRS):
                    if k == 0:
                        dve.wait_ge(down_made[p], u * HT)
                    if k < PAIRS - 1:
                        dve.wait_ge(hi_made, done(PAIRS + 1, g, k + 1))
                        dve.tensor_tensor(mid_lo[:, p, 2 * k:2 * k + 2, :], mid[:, 2 * k:2 * k + 2, :],
                                          mid_hi[:, p, 2 * k:2 * k + 2, :].bitcast(F32), ALU.subtract).then_inc(lo_made, 1)
                    else:
                        dve.wait_ge(hi_made, done(PAIRS + 1, g, PAIRS + 1))
                        f, valid = FC - 1, slice(0, BIAS_ROW)
                        dve.tensor_tensor(mid_lo[:, p, f - 1, :], mid[:, f - 1, :], mid_hi[:, p, f - 1, :].bitcast(F32), ALU.subtract).then_inc(lo_made, 1)
                        dve.tensor_tensor(mid_lo[valid, p, f, :], mid[valid, f, :], mid_hi[valid, p, f, :].bitcast(F32), ALU.subtract).then_inc(lo_made, 1)

            def outputs(g, p, j, u):
                dve.wait_ge(gates_copied, g + 1)
                dve.wait_ge(added[p], u * (16 * HT))
                for t in range(HT):
                    dve.wait_ge(down_made[p], done(HT, u, t // 2 * 2 + 2))
                    dve.tensor_scalar(y[:, p, t, :], psum[:, 6 + t // 2, (t % 2) * D:(t % 2 + 1) * D],
                                      gates[:, j, t:t + 1], None, ALU.mult).then_inc(y_made, 1)

            def body(q, last):
                def out(j):
                    outputs(q * GJ + j, j % 2, j, q * EP + j // 2)
                for j in range(GJ):
                    hidden_lo(q * GJ + j, j % 2, q * EP + j // 2)
                    if j < GJ - 1:
                        rows_lo(q * GJ + j + 1, j + 1, q * EP + (j + 1) // 2, q)
                    if 2 <= j:
                        out(j - 2)
                if not last:
                    rows_lo(q * GJ + GJ, 0, q * EP + EP, q + 1)
                    dve.wait_ge(up_made, (q + 1) * (GJ * FC))
                    dve.wait_ge(silu_made, (q + 1) * (GJ * FC))
                    up_weights(q + 1)
                    dve.wait_ge(down_made[1], q * (EP * HT) + HT)
                    down_weights(q * EP + EP, 0)
                out(GJ - 2)
                out(GJ - 1)
                if not last:
                    down_weights(q * EP + EP + 1, 1)

            up_weights(0)
            rows_lo(0, 0, 0, 0)
            for i in range(EP):
                down_weights(i, i)
            iterations(dve, body)


GOLDEN_CENTER = 1.0 / math.e
GOLDEN_LOWER = 0.5 - math.log(4.0 / 3.0)
GOLDEN_UPPER = 0.5
I_FF = 256
IC = I_FF // P
TINY = 1e-8


def route_zone(nc, const, logits, temperature, weight):
    with ExitStack() as ctx:
        sc = Scope(nc, ctx, "zone", const)
        temp, order = sc.sb("temp", [P, 1]), sc.sb("order", [P, E])
        inh, dist, zone, near = (sc.sb(n, [P, NT, E]) for n in ("inh", "dist", "zone", "near"))
        key, hit, picked, flag = (sc.sb(n, [P, NT, E]) for n in ("key", "hit", "picked", "flag"))
        best, total, lone, keep = (sc.sb(n, [P, NT]) for n in ("best", "total", "lone", "keep"))
        temp_loaded, order_made, step = sc.sem("temp_loaded"), sc.sem("order_made"), sc.sem("step")
        block = ctx.enter_context(nc.Block())
        DIST_READY = 7
        exps, divided = sc.sem("exps"), sc.sem("divided")

        @block.sync
        def _(sp):
            sp.dma_start(temp[:, :], temperature.partition_broadcast(P)).then_inc(temp_loaded, 16)

        @block.gpsimd
        def _(pool):
            pool.iota(order[:, :], pattern=[[-1, E]], base=E, channel_multiplier=0, allow_small_or_imprecise_dtypes=True).then_inc(order_made, 1)
        @block.scalar
        def _(act):
            act.wait_ge(divided, 1)
            act.activation(inh[:, :, :], inh[:, :, :], ACT.Exp, scale=-1.0).then_inc(exps, 1)
            act.wait_ge(step, DIST_READY)
            act.activation(weight[:, :, :], dist[:, :, :], ACT.Exp, scale=-1.0 / 0.1).then_inc(exps, 1)
            act.activation(near[:, :, :], dist[:, :, :], ACT.Exp, scale=-1.0 / 0.3).then_inc(exps, 1)

        @block.vector
        def _(dve):
            n = 0

            def then(instruction):
                nonlocal n
                instruction.then_inc(step, 1)
                n += 1
                dve.wait_ge(step, n)

            def over_e(x):
                return x.unsqueeze(2).to_broadcast([P, NT, E])

            keys = order[:, :].unsqueeze(1).to_broadcast([P, NT, E])
            dve.wait_ge(temp_loaded, 16)
            then(dve.reciprocal(temp[:, :], temp[:, :]))
            dve.tensor_scalar(inh[:, :, :], logits[:, :, :], temp[:, 0:1], None, ALU.mult).then_inc(divided, 1)
            dve.wait_ge(exps, 1)
            then(dve.tensor_scalar(inh[:, :, :], inh[:, :, :], 1.0, None, ALU.add))
            then(dve.reciprocal(inh[:, :, :], inh[:, :, :]))
            then(dve.tensor_scalar(zone[:, :, :], inh[:, :, :], GOLDEN_LOWER, None, ALU.is_ge))
            then(dve.scalar_tensor_tensor(zone[:, :, :], inh[:, :, :], GOLDEN_UPPER, zone[:, :, :], ALU.is_le, ALU.mult))
            then(dve.tensor_scalar(inh[:, :, :], inh[:, :, :], GOLDEN_CENTER, None, ALU.subtract))
            then(dve.scalar_tensor_tensor(dist[:, :, :], inh[:, :, :], -1.0, inh[:, :, :], ALU.mult, ALU.max))
            assert n == DIST_READY
            dve.wait_ge(exps, 2)
            then(dve.tensor_tensor(weight[:, :, :], weight[:, :, :], zone[:, :, :], ALU.mult))
            then(dve.tensor_reduce(total[:, :], weight[:, :, :], AX.X, ALU.add))
            then(dve.tensor_scalar(lone[:, :], total[:, :], TINY, None, ALU.is_lt))
            then(dve.tensor_scalar(keep[:, :], lone[:, :], -1.0, 1.0, ALU.mult, ALU.add))
            dve.wait_ge(exps, 3)
            dve.wait_ge(order_made, 1)
            left = near
            for k in range(2):
                then(dve.tensor_reduce(best[:, :], left[:, :, :], AX.X, ALU.max))
                then(dve.tensor_tensor(key[:, :, :], left[:, :, :], over_e(best[:, :]), ALU.is_ge))
                then(dve.tensor_tensor(key[:, :, :], key[:, :, :], keys, ALU.mult))
                then(dve.tensor_reduce(best[:, :], key[:, :, :], AX.X, ALU.max))
                then(dve.tensor_tensor(flag[:, :, :], key[:, :, :], over_e(best[:, :]), ALU.is_equal))
                if k == 0:
                    then(dve.scalar_tensor_tensor(hit[:, :, :], flag[:, :, :], -2.0, near[:, :, :], ALU.mult, ALU.add))
                    then(dve.tensor_copy(picked[:, :, :], flag[:, :, :]))
                    left = hit
            then(dve.tensor_tensor(picked[:, :, :], picked[:, :, :], flag[:, :, :], ALU.add))
            then(dve.tensor_tensor(near[:, :, :], near[:, :, :], picked[:, :, :], ALU.mult))
            then(dve.tensor_reduce(total[:, :], near[:, :, :], AX.X, ALU.add))
            then(dve.tensor_scalar(total[:, :], total[:, :], TINY, None, ALU.max))
            then(dve.reciprocal(total[:, :], total[:, :]))
            then(dve.tensor_tensor(total[:, :], total[:, :], lone[:, :], ALU.mult))
            then(dve.tensor_tensor(near[:, :, :], near[:, :, :], over_e(total[:, :]), ALU.mult))
            then(dve.tensor_tensor(weight[:, :, :], weight[:, :, :], over_e(keep[:, :]), ALU.mult))
            then(dve.tensor_tensor(weight[:, :, :], weight[:, :, :], near[:, :, :], ALU.add))
            then(dve.tensor_reduce(total[:, :], weight[:, :, :], AX.X, ALU.add))
            then(dve.tensor_scalar(total[:, :], total[:, :], TINY, None, ALU.max))
            then(dve.reciprocal(total[:, :], total[:, :]))
            then(dve.tensor_tensor(weight[:, :, :], weight[:, :, :], over_e(total[:, :]), ALU.mult))


def zone_mixture(nc, const, psum, weight, x, x_normed, w_gate, w_up, w_down, out):
    with ExitStack() as ctx:
        sc = Scope(nc, ctx, "zmix", const)
        wg_hi, wg_lo = sc.sb("wg_hi", [P, E, KC, I_FF], F32R), sc.sb("wg_lo", [P, E, KC, I_FF], F32R)
        wu_hi, wu_lo = sc.sb("wu_hi", [P, E, KC, I_FF], F32R), sc.sb("wu_lo", [P, E, KC, I_FF], F32R)
        wd_hi, wd_lo = sc.sb("wd_hi", [P, E, IC, D], F32R), sc.sb("wd_lo", [P, E, IC, D], F32R)
        raw = sc.sb("raw", [P, 4, 512])
        acc = sc.sb("acc", [P, 2, TT, D])
        xn = sc.sb("xn", [P, 2, TT, D])
        xT_hi, xT_lo = sc.sb("xT_hi", [P, 2, KC, S], F32R), sc.sb("xT_lo", [P, 2, KC, S], F32R)
        act_gate = sc.sb("act_gate", [P, IC, S])
        hid = sc.sb("hid", [P, IC, S])
        hid_hi, hid_lo = sc.sb("hid_hi", [P, 2, IC, S], F32R), sc.sb("hid_lo", [P, 2, IC, S], F32R)

        raw_in = [sc.sem(f"raw_in{k}") for k in range(4)]
        w_hi, w_ready = sc.sem("w_hi"), sc.sem("w_ready")
        acc_in, xn_in = ([sc.sem(f"{n}{p}") for p in range(2)] for n in ("acc_in", "xn_in"))
        stored = [sc.sem(f"stored{p}") for p in range(2)]
        turned, xT_hi_made, xT_ready = sc.sem("turned"), sc.sem("xT_hi_made"), sc.sem("xT_ready")
        gate_made, up_made, gate_out, up_out = sc.sem("gate_made"), sc.sem("up_made"), sc.sem("gate_out"), sc.sem("up_out")
        hi_made, lo_made = sc.sem("hi_made"), sc.sem("lo_made")
        down_made = sc.sem("down_made")
        acc_made = sc.sem("acc_made")
        block = ctx.enter_context(nc.Block())
        STEPS = 2 * E
        LAST = B // 2 - 1
        matrices = [(w, e) for e in range(E) for w in range(3)]

        def iterations(eng, body):
            with eng.Fori(0, LAST) as r:
                body(r, False)
            body(LAST, True)

        def parts(w, e):
            hi, lo = ((wg_hi, wg_lo), (wu_hi, wu_lo), (wd_hi, wd_lo))[w]
            return hi[:, e, :, :].rearrange("p c f -> p (c f)"), lo[:, e, :, :].rearrange("p c f -> p (c f)")

        def weights_for(pe, e, count):
            pe.wait_ge(w_ready, 3 * e + count)

        @block.sync
        def _(sp):
            def load(b, p, r):
                after(sp, turned, b - 1)
                sp.dma_start(xn[:, p, :, :], x_normed[bass.ds(b, 1), :, :].rearrange("o (t p) d -> p (o t) d", p=P)).then_inc(xn_in[p], 16)
                after(sp, stored[p], r * 16)
                sp.dma_start(acc[:, p, :, :], x[bass.ds(b, 1), :, :].rearrange("o (t p) d -> p (o t) d", p=P)).then_inc(acc_in[p], 16)

            def body(r, last):
                for p in range(2):
                    b = r * 2 + p
                    sp.wait_ge(acc_made, (b + 1) * (E * TT))
                    sp.dma_start(out[bass.ds(b, 1), :, :].rearrange("o (t p) d -> p (o t) d", p=P), acc[:, p, :, :]).then_inc(stored[p], 16)
                    if not last:
                        load(b + 2, p, r + 1)
            for p in range(2):
                load(p, p, 0)
            iterations(sp, body)
            for p in range(2):
                sp.wait_ge(stored[p], 16 * (B // 2))

        @block.gpsimd
        def _(pool):
            for n, (w, e) in enumerate(matrices):
                after(pool, w_ready, n - 3)
                src = (w_gate, w_up, w_down)[w][e, :, :].rearrange("(c p) f -> p c f", p=P)
                pool.dma_start(raw[:, n % 4, :].rearrange("p (c f) -> p c f", c=2), src).then_inc(raw_in[n % 4], 16)

        @block.tensor
        def _(pe):
            def turn(b, p, r):
                pe.wait_ge(xn_in[p], r * 16 + 16)
                after(pe, xT_ready, b)
                for c in range(KC):
                    for t in range(TT):
                        m = pe.transpose(psum[:, 6 + c, t * P:(t + 1) * P], xn[:, p, t, c * P:(c + 1) * P], const["ident"][:, :])
                m.then_inc(turned, 1)

            def gate_up(b, p, e, first):
                n = b * E + e
                if e == 0:
                    pe.wait_ge(xT_ready, b + 1)
                for w, (hi, lo), bank, last_out, made in ((0, (wg_hi, wg_lo), 0, gate_out, gate_made), (1, (wu_hi, wu_lo), 2, up_out, up_made)):
                    if first:
                        pe.wait_ge(w_ready, 3 * e + w + 1)
                    after(pe, last_out, n)
                    for i in range(IC):
                        cols = slice(i * P, (i + 1) * P)
                        for c in range(KC):
                            m = three_passes(pe, psum[:, bank + i, :], hi[:, e, c, cols], lo[:, e, c, cols],
                                             xT_hi[:, p, c, :], xT_lo[:, p, c, :], c == 0, c == KC - 1)
                    m.then_inc(made, 1)

            def down(b, p, e, first):
                n = b * E + e
                if first:
                    pe.wait_ge(w_ready, 3 * e + 3)
                pe.wait_ge(lo_made, n + 1)
                for t in range(TT):
                    if t % 2 == 0:
                        after(pe, acc_made, n * TT - TT + t + 2)
                    rows = slice(t * P, (t + 1) * P)
                    for i in range(IC):
                        m = three_passes(pe, psum[:, 4 + t // 2, (t % 2) * D:(t % 2 + 1) * D], hid_hi[:, e % 2, i, rows],
                                         hid_lo[:, e % 2, i, rows], wd_hi[:, e, i, :], wd_lo[:, e, i, :], i == 0, i == IC - 1)
                    if t % 2:
                        m.then_inc(down_made, 1)

            def steps(r, last, first):
                for p in range(2):
                    b = r * 2 + p
                    for e in range(E):
                        if e < E - 1:
                            if e == 2 and not (last and p == 1):
                                turn(b + 1, 1 - p, r + p)
                            gate_up(b, p, e + 1, first and p == 0)
                        elif not (last and p == 1):
                            gate_up(b + 1, 1 - p, 0, False)
                        down(b, p, e, first and p == 0)

            turn(0, 0, 0)
            gate_up(0, 0, 0, True)
            steps(0, False, True)
            with pe.Fori(1, LAST) as r:
                steps(r, False, False)
            steps(LAST, True, False)

        @block.scalar
        def _(act):
            def rows_hi(b, p):
                act.wait_ge(turned, b + 1)
                after(act, gate_made, b * E - E)
                after(act, up_made, b * E - E)
                act.activation(xT_hi[:, p, :, :], psum[:, 6:8, :], ACT.Copy).then_inc(xT_hi_made, 1)

            def steps(r, last, first):
                for p in range(2):
                    b = r * 2 + p
                    for e in range(E):
                        n = b * E + e
                        act.wait_ge(gate_made, n + 1)
                        after(act, hi_ready_to_reuse, n)
                        act.activation(act_gate[:, :, :], psum[:, 0:2, :], ACT.Silu).then_inc(gate_out, 1)
                        if e == 3 and not (last and p == 1):
                            rows_hi(b + 1, 1 - p)
                        act.wait_ge(up_out, n + 1)
                        after(act, down_made, n * 2 - 2)
                        act.activation(hid_hi[:, e % 2, :, :], hid[:, :, :], ACT.Copy).then_inc(hi_made, 1)

            hi_ready_to_reuse = up_out
            for n, (w, e) in enumerate(matrices):
                act.wait_ge(raw_in[n % 4], n // 4 * 16 + 16)
                act.activation(parts(w, e)[0], raw[:, n % 4, :], ACT.Copy).then_inc(w_hi, 1)
                if n == 2:
                    rows_hi(0, 0)
            steps(0, False, True)
            with act.Fori(1, LAST) as r:
                steps(r, False, False)
            steps(LAST, True, False)

        @block.vector
        def _(dve):
            def rows_lo(b, p):
                dve.wait_ge(xT_hi_made, b + 1)
                dve.tensor_tensor(xT_lo[:, p, :, :], psum[:, 6:8, :], xT_hi[:, p, :, :].bitcast(F32), ALU.subtract).then_inc(xT_ready, 1)

            def add(b, p, e, r):
                n = b * E + e
                if e == 0:
                    dve.wait_ge(acc_in[p], r * 16 + 16)
                else:
                    dve.wait_ge(acc_made, n * TT)
                for t in range(TT):
                    if t % 2 == 0:
                        dve.wait_ge(down_made, n * 2 + t // 2 + 1)
                    dve.scalar_tensor_tensor(acc[:, p, t, :], psum[:, 4 + t // 2, (t % 2) * D:(t % 2 + 1) * D],
                                             weight[:, bass.ds(b * TT + t, 1), e], acc[:, p, t, :], ALU.mult, ALU.add).then_inc(acc_made, 1)

            def hidden(b, p, e):
                n = b * E + e
                dve.wait_ge(gate_out, n + 1)
                dve.wait_ge(up_made, n + 1)
                after(dve, lo_made, n)
                dve.tensor_tensor(hid[:, :, :], act_gate[:, :, :], psum[:, 2:4, :], ALU.mult).then_inc(up_out, 1)

            def hidden_lo(b, p, e):
                n = b * E + e
                dve.wait_ge(hi_made, n + 1)
                dve.tensor_tensor(hid_lo[:, e % 2, :, :], hid[:, :, :], hid_hi[:, e % 2, :, :].bitcast(F32), ALU.subtract).then_inc(lo_made, 1)

            def steps(r, last, first):
                for p in range(2):
                    b = r * 2 + p
                    for e in range(E):
                        if e < E - 1:
                            nb, np_, ne = b, p, e + 1
                        else:
                            nb, np_, ne = b + 1, 1 - p, 0
                        over = last and p == 1
                        if not (over and e == E - 1):
                            hidden(nb, np_, ne)
                        if e == 2 and not over:
                            rows_lo(b + 1, 1 - p)
                        if not (over and e == E - 1):
                            hidden_lo(nb, np_, ne)
                        add(b, p, e, r)

            for n, (w, e) in enumerate(matrices):
                dve.wait_ge(w_hi, n + 1)
                dve.wait_ge(raw_in[n % 4], n // 4 * 16 + 16)
                dve.tensor_tensor(parts(w, e)[1], raw[:, n % 4, :], parts(w, e)[0].bitcast(F32), ALU.subtract).then_inc(w_ready, 1)
                if n == 2:
                    rows_lo(0, 0)
            hidden(0, 0, 0)
            hidden_lo(0, 0, 0)
            steps(0, False, True)
            with dve.Fori(1, LAST) as r:
                steps(r, False, False)
            steps(LAST, True, False)


def attention_layer(nc, const, psum, masked, name, w, src, dst, dst_normed, logits):
    with ExitStack() as ctx:
        kv = alloc_layer(Scope(nc, ctx, name), masked)
        attention_setup(nc, const, kv, w, psum)
        attention(nc, const, kv, psum, src, dst, dst_normed, logits)


def two_layers(nc, a, out):
    x1 = nc.dram_tensor("x1", (N_TOK, D), F32, kind="Internal").ap()
    rows1 = nc.dram_tensor("rows1", (N_TOK, ROW), F32, kind="Internal").ap()
    x3 = nc.dram_tensor("x3", (B, S, D), F32, kind="Internal").ap()
    normed3 = nc.dram_tensor("normed3", (B, S, D), F32, kind="Internal").ap()
    thresholds = nc.dram_tensor("thresholds", (P,), F32, kind="Internal").ap()
    x1_by_batch = x1.rearrange("(b s) d -> b s d", s=S)
    with ExitStack() as ctx:
        sc = Scope(nc, ctx, "main")
        const = {"ident": sc.sb("ident", [P, P]), "headmask": sc.sb("headmask", [P, HH]),
                 "negsel": sc.sb("negsel", [P, NP, P], F32R), "keysel": sc.sb("keysel", [P, HH, SK], BF16)}
        psum = ctx.enter_context(nc.psum_tensor("psum", [P, 8, 512], F32))
        logits = sc.sb("logits", [P, NT, E])
        const["sems"] = Semaphores(nc)
        make_constants(nc, const)

        w0 = {k: a[k + "0"] for k in ("wq", "wk", "wv", "wo", "bq", "bk", "bv", "bo", "wr")}
        attention_layer(nc, const, psum, False, "att0", {**w0, "ctx": a["ctx"], "mask": None, "pad": None}, a["x"], x1_by_batch,
                        rows1.rearrange("(b s) r -> b s r", s=S)[:, :, 0:D], logits)
        const["sems"].give_back()
        const["sems"] = Semaphores(nc)
        with ExitStack() as mixture:
            idx = Scope(nc, mixture, "lists").sb("idx", [P, E, TOPK // P], I32)
            route_expert_choice(nc, const, psum, logits, a["br"], rows1, thresholds, idx)
            expert_choice_mixture(nc, const, psum, idx, x1, rows1, a["w_up"], a["b_up"], a["w_down"])

        w1 = {k: a[k + "1"] for k in ("wq", "wk", "wv", "wo", "bq", "bk", "bv", "bo", "wr")}
        attention_layer(nc, const, psum, True, "att1", {**w1, "ctx": a["ctx"], "mask": a["mask"], "pad": a["pad"]}, x1_by_batch, x3,
                        normed3, logits)
        weight = sc.sb("weight", [P, NT, E])
        route_zone(nc, const, logits, a["temperature"], weight)
        zone_mixture(nc, const, psum, weight, x3, normed3, a["wg"], a["wu"], a["wd"], out)


def kernel(**inputs):
    import numpy as _np
    import concourse.bacc as _bacc
    from concourse import mybir as _mybir
    from concourse.bass_utils import run_bass_kernel_spmd as _run

    i = {k: _np.asarray(v) for k, v in inputs.items()}

    def columns(v):
        return v.reshape(-1, P).T

    w_up = _np.zeros((GROUPS_UP, D, FP), i["L0_ffn_W_up"].dtype)
    w_up[:, :, :F] = i["L0_ffn_W_up"]
    b_up = _np.zeros((GROUPS_UP, FP), i["L0_ffn_b_up"].dtype)
    b_up[:, :F] = i["L0_ffn_b_up"]
    w_down = _np.zeros((E, FP, D), i["L0_ffn_W_down"].dtype)
    w_down[:, :F] = i["L0_ffn_W_down"]
    w_down[:, (FC - 1) * P + BIAS_ROW] = i["L0_ffn_b_down"]
    laid = {
        "x": i["x"], "ctx": i["ctx_1024"].reshape(B * SK, D),
        "wq0": i["L0_xattn_Wq"], "wk0": i["L0_xattn_Wk"], "wv0": i["L0_xattn_Wv"], "wo0": i["L0_xattn_Wo"],
        "bq0": columns(i["L0_xattn_bq"]), "bk0": columns(i["L0_xattn_bk"]), "bv0": i["L0_xattn_bv"], "bo0": i["L0_xattn_bo"],
        "wr0": i["L0_ffn_Wr"], "br": i["L0_ffn_br"],
        "w_up": w_up, "b_up": b_up.reshape(GROUPS_UP, FC, P).transpose(0, 2, 1), "w_down": w_down,
        "wq1": i["L1_xattn_wq"].T, "wk1": i["L1_xattn_wk"].T, "wv1": i["L1_xattn_wv"].T, "wo1": i["L1_xattn_wo"].T,
        "bq1": columns(i["L1_xattn_bq"]), "bk1": columns(i["L1_xattn_bk"]), "bv1": i["L1_xattn_bv"], "bo1": i["L1_xattn_bo"],
        "wr1": i["L1_ffn_Wr"], "temperature": i["L1_ffn_temperature"],
        "mask": i["mask_SxS2_bk0"].T, "pad": i["mask_BxS2_bk1"].T,
        "wg": i["L1_ffn_Wg"], "wu": i["L1_ffn_Wu"], "wd": i["L1_ffn_Wd"],
    }
    nc = _bacc.Bacc("TRN2", target_bir_lowering=False, num_devices=1)
    arrays, args = {}, {}
    for name, v in laid.items():
        v = _np.ascontiguousarray(v)
        if v.dtype == _np.bool_:
            v = v.view(_np.int32)
        arrays[f"in_{name}"] = v
        args[name] = nc.dram_tensor(f"in_{name}", v.shape, _mybir.dt.from_np(v.dtype), kind="ExternalInput").ap()
    out = nc.dram_tensor("out_x", (B, S, D), _mybir.dt.float32, kind="ExternalOutput").ap()
    two_layers(nc, args, out)
    r = _run(nc, [arrays], core_ids=[0])
    return r.results[0]["out_x"]
```

```python
import math
from contextlib import ExitStack

import numpy as np

import concourse.bass as bass
from concourse import mybir

F32 = mybir.dt.float32
F32R = mybir.dt.float32r
BF16 = mybir.dt.bfloat16
I32 = mybir.dt.int32
U8 = mybir.dt.uint8
ALU = mybir.AluOpType
ACT = mybir.ActivationFunctionType
AX = mybir.AxisListType

P = 128
B, S, D = 16, 512, 256
SK = 64
H, DH = 16, 16
KC = D // P
TT = S // P
HH = H // KC
NP = H // 2
NT = B * TT
VW = DH + 1
N_TOK = B * S
LN_EPS = 1e-5
BIG = float(2.0 ** 60)
PE_COLS = 96
RSQRT_MAGIC = float(0x5F3759DF)
NEWTON = 3


def done(count_per_batch, b, k):
    return b * count_per_batch + k


def ln_steps(n):
    return n * 2 * TT + 3 + 3 * NEWTON


def after(eng, sem, value):
    if not isinstance(value, int) or value > 0:
        eng.wait_ge(sem, value)


class Semaphores:

    def __init__(self, nc):
        self.nc, self.stack, self.taken = nc, ExitStack(), []

    def take(self, name):
        self.taken.append(self.stack.enter_context(self.nc.semaphore(name)))
        return self.taken[-1]

    def give_back(self):
        with self.nc.Block() as block:
            @block.gpsimd
            def _(pool):
                for sem in self.taken:
                    pool.sem_clear(sem)
        self.stack.close()


class Scope:

    def __init__(self, nc, ctx, phase, const=None):
        self.nc, self.ctx, self.phase, self.const = nc, ctx, phase, const

    def sb(self, name, shape, dt=F32):
        return self.ctx.enter_context(self.nc.sbuf_tensor(f"{self.phase}_{name}", shape, dt))

    def sem(self, name):
        return self.const["sems"].take(f"{self.phase}_{name}")


def layernorm_stats(dve, xs, parts, stats, mv, rstd, tmp, sem, start, passed, before=(), between=None):
    n = 0
    for i, (x, k) in enumerate(zip(xs, parts)):
        if before:
            before[i]()
        for t in range(TT):
            dve.bn_stats(stats[:, k * TT + t, :], x[:, t, :]).then_inc(sem, 1)
            n += 1
    dve.wait_ge(sem, start + n)
    dve.sem_inc(passed, 1)
    for k in parts:
        for t in range(TT):
            dve.bn_aggr(mv[:, k * TT + t, :], stats[:, k * TT + t, :]).then_inc(sem, 1)
            n += 1
    dve.wait_ge(sem, start + n)
    cols = slice(parts[0] * TT, (parts[-1] + 1) * TT)
    var, guess, y = tmp[:, 0, cols], tmp[:, 1, cols], rstd[:, cols]
    dve.tensor_scalar(var, mv[:, cols, 1], LN_EPS, None, ALU.add).then_inc(sem, 1)
    n += 1
    dve.wait_ge(sem, start + n)
    dve.tensor_scalar(guess.bitcast(I32), var.bitcast(I32), 1, None, ALU.logical_shift_right).then_inc(sem, 1)
    n += 1
    dve.wait_ge(sem, start + n)
    dve.tensor_scalar(y.bitcast(I32), guess.bitcast(I32), -1.0, RSQRT_MAGIC, ALU.mult, ALU.add).then_inc(sem, 1)
    n += 1
    for k in range(NEWTON):
        if k == 1 and between:
            between()
        dve.wait_ge(sem, start + n)
        dve.scalar_tensor_tensor(guess, y, -0.5, y, ALU.mult, ALU.mult).then_inc(sem, 1)
        n += 1
        dve.wait_ge(sem, start + n)
        dve.tensor_tensor(guess, guess, var, ALU.mult).then_inc(sem, 1)
        n += 1
        dve.wait_ge(sem, start + n)
        dve.scalar_tensor_tensor(y, guess, 1.5, y, ALU.add, ALU.mult).then_inc(sem, 1)
        n += 1
    assert n == ln_steps(len(xs))


def three_passes(pe, out, st_hi, st_lo, mv_hi, mv_lo, first, last):
    pe.matmul(out, st_hi, mv_hi, start=first, stop=False)
    pe.matmul(out, st_hi, mv_lo, start=False, stop=False)
    return pe.matmul(out, st_lo, mv_hi, start=False, stop=last)


def make_constants(nc, const):
    ident, headmask, negsel, keysel = const["ident"], const["headmask"], const["negsel"], const["keysel"]
    with ExitStack() as ctx:
        sc = Scope(nc, ctx, "const", const)
        made = sc.sem("const_made")
        negf = sc.sb("negsel_f", [P, NP, P])
        keyf = sc.sb("keysel_f", [P, H // 2, SK])
        block = ctx.enter_context(nc.Block())

        @block.gpsimd
        def _(pool):
            pool.memset(ident[:, :], 0.0).then_inc(made, 1)
            pool.memset(headmask[:, :], 1.0).then_inc(made, 1)
            pool.memset(negf[:, :, :], -1.0).then_inc(made, 1)
            pool.memset(keyf[:, :, :], 0.0).then_inc(made, 1)
            pool.wait_ge(made, 4)
            pool.affine_select(out=ident[:, :], in_=ident[:, :], compare_op=ALU.not_equal, fill=1.0, base=0,
                               pattern=[[-1, P]], channel_multiplier=1).then_inc(made, 1)
            pool.affine_select(out=headmask[:, :], in_=headmask[:, :], compare_op=ALU.is_ge, fill=0.0, base=0,
                               pattern=[[-DH, HH]], channel_multiplier=1).then_inc(made, 1)
            pool.affine_select(out=keyf[:, :, :], in_=keyf[:, :, :], compare_op=ALU.not_equal, fill=1.0, base=0,
                               pattern=[[0, HH], [-1, SK]], channel_multiplier=1).then_inc(made, 1)
            v = negf[:, :, :].rearrange("p j (a k) -> p j a k", a=2)
            pool.affine_select(out=v, in_=v, compare_op=ALU.is_equal, fill=0.0, base=0,
                               pattern=[[-2, NP], [-1, 2], [0, SK]], channel_multiplier=1).then_inc(made, 1)
            pool.wait_ge(made, 8)
            pool.affine_select(out=headmask[:, :], in_=headmask[:, :], compare_op=ALU.is_ge, fill=0.0, base=DH - 1,
                               pattern=[[DH, HH]], channel_multiplier=-1).then_inc(made, 1)
            pool.tensor_copy(negsel[:, :, :], negf[:, :, :]).then_inc(made, 1)
            pool.tensor_copy(keysel[:, :, :], keyf[:, :, :]).then_inc(made, 1)


def attention_setup(nc, const, kv, w, psum):
    V_BANKS, BH = 4, B // 2
    with ExitStack() as ctx:
        sc = Scope(nc, ctx, kv["name"] + "_setup", const)
        ctx_in = sc.sb("ctx_in", [P, B * SK // P, D])
        ctxT = sc.sb("ctxT", [P, KC, B, 2, SK])
        wk, wv = sc.sb("wk", [P, KC, D]), sc.sb("wv", [P, KC, D])
        bv = sc.sb("bv_bcast", [P, D])
        wq, wo = sc.sb("wq", [P, KC, D]), sc.sb("wo", [P, KC, D])
        loaded, qo_loaded = sc.sem("kv_loaded"), sc.sem("qo_loaded")
        small_loaded = sc.sem("small_loaded")
        turned, turned_out, turned_twice = sc.sem("ctx_turned"), sc.sem("ctx_turned_out"), sc.sem("ctx_turned_twice")
        k_made, k_hi, k_out = sc.sem("k_made"), sc.sem("k_hi"), sc.sem("k_out")
        v_made, v_out = sc.sem("v_made"), sc.sem("v_out")
        v_cleared, split_hi, split_lo = sc.sem("v_cleared"), sc.sem("split_hi"), sc.sem("split_lo")
        mask_loaded, wr_cleared = sc.sem("mask_loaded"), sc.sem("wr_cleared")
        NC8 = B * SK // P
        if w["mask"] is not None:
            mask32, pad32 = sc.sb("mask_u8", [SK, S // 4], I32), sc.sb("pad_u8", [SK, B // 4], I32)
        block = ctx.enter_context(nc.Block())

        @block.sync
        def _(sp):
            sp.dma_start(ctx_in[:, :, :], w["ctx"].rearrange("(n p) d -> p n d", p=P)).then_inc(loaded, 16)
            sp.dma_start(wk[:, :, :], w["wk"].rearrange("(c p) d -> p c d", p=P)).then_inc(loaded, 16)
            sp.dma_start(wv[:, :, :], w["wv"].rearrange("(c p) d -> p c d", p=P)).then_inc(loaded, 16)
            sp.dma_start(bv[:, :], w["bv"].partition_broadcast(P)).then_inc(small_loaded, 16)
            sp.dma_start(kv["bo"][:, :], w["bo"].partition_broadcast(P)).then_inc(small_loaded, 16)
            sp.dma_start(kv["bk"][:, :], w["bk"]).then_inc(small_loaded, 16)
            sp.dma_start(kv["bq"][:, :], w["bq"]).then_inc(small_loaded, 16)
            sp.dma_start(wq[:, :, :], w["wq"].rearrange("(c p) d -> p c d", p=P)).then_inc(qo_loaded, 16)
            sp.dma_start(wo[:, :, :], w["wo"].rearrange("(c p) d -> p c d", p=P)).then_inc(qo_loaded, 16)
            sp.wait_ge(wr_cleared, 1)
            sp.dma_start(kv["wr"][:, :, 0:8], w["wr"].rearrange("(c p) e -> p c e", p=P)).then_inc(small_loaded, 16)
            if w["mask"] is not None:
                sp.dma_start(mask32[:, :], w["mask"]).then_inc(mask_loaded, 16)
                sp.dma_start(pad32[:, :], w["pad"]).then_inc(mask_loaded, 16)
                sp.wait_ge(mask_loaded, 32)
            sp.wait_ge(small_loaded, 5 * 16)

        @block.gpsimd
        def _(pool):
            pool.memset(kv["wr"][:, :, :], 0.0).then_inc(wr_cleared, 1)
            pool.memset(kv["v"][:, :, :, :], 0.0).then_inc(v_cleared, 1)
            pool.wait_ge(v_cleared, 1)
            ones = kv["v"][:, :, :, :].rearrange("p b j (a c) -> p (b j) a c", a=2)
            pool.memset(ones[0:SK, :, 0, DH:VW], 1.0).then_inc(v_cleared, 1)
            pool.memset(ones[SK:P, :, 1, DH:VW], 1.0).then_inc(v_cleared, 1)
            pool.wait_ge(v_cleared, 3)

        @block.tensor
        def _(pe):
            pe.wait_ge(loaded, 48)
            for c in range(KC):
                for n in range(NC8):
                    t = pe.transpose(psum[:, 2 * c + n // 4, (n % 4) * P:(n % 4 + 1) * P], ctx_in[:, n, c * P:(c + 1) * P],
                                     const["ident"][:, :])
                    if n % 4 == 3:
                        t.then_inc(turned, 1)
            pe.wait_ge(turned_out, KC * 2)
            for m in range(KC):
                for n in range(2):
                    for c in range(KC):
                        k = pe.matmul(psum[:, 4 + 2 * m + n, :], wk[:, c, m * P:(m + 1) * P], ctxT[:, c, n * BH:(n + 1) * BH, 0, :],
                                      start=(c == 0), stop=(c == KC - 1))
                    k.then_inc(k_made, 1)
            pe.wait_ge(turned_twice, KC * 2)
            for b in range(B):
                if b >= V_BANKS:
                    pe.wait_ge(v_out, 2 * (b - V_BANKS + 1))
                for c in range(KC):
                    v = pe.matmul(psum[:, b % V_BANKS, 0:D], ctxT[:, c, b, :, :], wv[:, c, :], start=(c == 0), stop=(c == KC - 1))
                v.then_inc(v_made, 1)

        @block.scalar
        def _(act):
            for n in range(2 * KC):
                act.wait_ge(turned, n + 1)
                act.activation(ctxT[:, n // 2, (n % 2) * BH:(n % 2 + 1) * BH, 0, :],
                               psum[:, n, :].rearrange("p (b k) -> p b k", k=SK), ACT.Copy).then_inc(turned_out, 1)
            act.wait_ge(small_loaded, 5 * 16)
            for m in range(KC):
                for n in range(2):
                    act.wait_ge(k_made, 2 * m + n + 1)
                    act.activation(kv["kT_hi"][:, m, n * 512:(n + 1) * 512], psum[:, 4 + 2 * m + n, :], ACT.Identity,
                                   bias=kv["bk"][:, m:m + 1]).then_inc(k_hi, 1)
            act.wait_ge(qo_loaded, 32)
            act.activation(kv["wq_hi"][:, :, :], wq[:, :, :], ACT.Copy).then_inc(split_hi, 1)
            act.activation(kv["wo_hi"][:, :, :], wo[:, :, :], ACT.Copy).then_inc(split_hi, 1)

        @block.vector
        def _(dve):
            for n in range(2 * KC):
                dve.wait_ge(turned_out, n + 1)
                dve.tensor_copy(ctxT[:, n // 2, (n % 2) * BH:(n % 2 + 1) * BH, 1, :],
                                psum[:, n, :].rearrange("p (b k) -> p b k", k=SK)).then_inc(turned_twice, 1)
            dve.wait_ge(small_loaded, 5 * 16)
            for m in range(KC):
                for n in range(2):
                    dve.wait_ge(k_hi, 2 * m + n + 1)
                    cols = slice(n * 512, (n + 1) * 512)
                    dve.scalar_tensor_tensor(kv["kT_lo"][:, m, cols], psum[:, 4 + 2 * m + n, :], kv["bk"][:, m:m + 1],
                                             kv["kT_hi"][:, m, cols].bitcast(F32), ALU.add, ALU.subtract).then_inc(k_out, 1)
            dve.wait_ge(split_hi, 2)
            dve.wait_ge(qo_loaded, 32)
            dve.tensor_tensor(kv["wq_lo"][:, :, :], wq[:, :, :], kv["wq_hi"][:, :, :].bitcast(F32), ALU.subtract).then_inc(split_lo, 1)
            dve.tensor_tensor(kv["wo_lo"][:, :, :], wo[:, :, :], kv["wo_hi"][:, :, :].bitcast(F32), ALU.subtract).then_inc(split_lo, 1)
            if w["mask"] is not None:
                dve.wait_ge(mask_loaded, 32)
                dve.tensor_copy(kv["mask"][:, :], mask32[:, :].bitcast(U8))
                dve.tensor_scalar(kv["pad"][:, :], pad32[:, :].bitcast(U8), BIG, None, ALU.mult)
            dve.wait_ge(v_cleared, 3)
            for b in range(B):
                dve.wait_ge(v_made, b + 1)
                for a in range(2):
                    rows = slice(a * SK, (a + 1) * SK)
                    heads = psum[rows, b % V_BANKS, 0:D].rearrange("p (j a c) -> p j a c", a=2, c=DH)[:, :, a, :]
                    bias = bv[rows, :].rearrange("p (j a c) -> p j a c", a=2, c=DH)[:, :, a, :]
                    dve.tensor_tensor(kv["v"][rows, b, :, a * VW:a * VW + DH], heads, bias, ALU.add).then_inc(v_out, 1)


def attention(nc, const, kv, psum, src, dst, dst_normed, logits_all):
    masked = kv["masked"]
    ident = const["ident"]
    STORES = 2
    with ExitStack() as ctx:
        sc = Scope(nc, ctx, kv["name"], const)
        x_in = sc.sb("x_in", [P, 2, TT, D])
        x_bias = sc.sb("x_bias", [P, 2, TT, D])
        x_new = sc.sb("x_new", [P, 2, TT, D])
        normed = sc.sb("normed", [P, TT, D])
        normed_new = sc.sb("normed_new", [P, 2, TT, D])
        nT_hi, nT_lo = sc.sb("nT_hi", [P, KC, S], F32R), sc.sb("nT_lo", [P, KC, S], F32R)
        newT = sc.sb("newT", [P, KC, S])
        qT_hi, qT_lo = sc.sb("qT_hi", [P, 2, KC, S], F32R), sc.sb("qT_lo", [P, 2, KC, S], F32R)
        kb_hi, kb_lo = sc.sb("kb_hi", [P, 2, KC, HH, SK], F32R), sc.sb("kb_lo", [P, 2, KC, HH, SK], F32R)
        v_cur = sc.sb("v_cur", [P, 2, (NP - 1) * 2 * VW + PE_COLS])
        s_max = sc.sb("s_max", [P, TT, H])
        maxT = sc.sb("maxT", [P, S], F32R)
        probs = sc.sb("probs", [P, NP, S])
        recip = sc.sb("recip", [P, TT, H])
        att = sc.sb("att", [P, TT, D])
        aT_hi, aT_lo = sc.sb("aT_hi", [P, KC, S], F32R), sc.sb("aT_lo", [P, KC, S], F32R)
        stats, mv = sc.sb("stats", [P, 2 * TT, 6]), sc.sb("mv", [P, 2 * TT, 2])
        rstd, shift2 = sc.sb("rstd", [P, 2 * TT]), sc.sb("shift2", [P, TT])
        tmp = sc.sb("ln_tmp", [P, 2, 2 * TT])
        mask_cur = sc.sb("mask_cur", [P, 2, S], BF16) if masked else None

        x_loaded = [sc.sem(f"x_loaded{p}") for p in range(2)]
        stored = [sc.sem(f"stored{p}") for p in range(2)]
        ln = sc.sem("ln")
        shifted = sc.sem("shifted")
        norm_in, norm_out = sc.sem("norm_in"), sc.sem("norm_out")
        bias_done = sc.sem("bias_done")
        v_ready = sc.sem("v_ready")
        kb_ready = sc.sem("kb_ready")
        mask_ready = sc.sem("mask_ready")
        turned, turned_hi, turned_lo = sc.sem("turned"), sc.sem("turned_hi"), sc.sem("turned_lo")
        q_made, q_hi, q_lo = sc.sem("q_made"), sc.sem("q_hi"), sc.sem("q_lo")
        s_made, s_taken = sc.sem("s_made"), sc.sem("s_taken")
        max_turned, max_ready = sc.sem("max_turned"), sc.sem("max_ready")
        st_made, exp_done = sc.sem("st_made"), sc.sem("exp_done")
        av_made, av_recip, av_taken = sc.sem("av_made"), sc.sem("av_recip"), sc.sem("av_taken")
        a_turned, a_hi, a_lo = sc.sem("a_turned"), sc.sem("a_hi"), sc.sem("a_lo")
        o_made, x_ready = sc.sem("o_made"), sc.sem("x_ready")
        new_turned, new_out = sc.sem("new_turned"), sc.sem("new_out")
        lg_made, lg_out = sc.sem("lg_made"), sc.sem("lg_out")
        cleared, passed = sc.sem("cleared"), sc.sem("passed")
        block = ctx.enter_context(nc.Block())

        def batches(eng, body, close=None):
            body(0, 0, 0)
            with eng.Fori(0, (B - 4) // 2) as r:
                body(r * 2 + 1, 1, r)
                body(r * 2 + 2, 0, r + 1)
            for b in range(B - 3, B):
                body(b, b % 2, b // 2)
            if close:
                close(B)

        def there(b):
            return not isinstance(b, int) or 0 <= b < B

        def ln_start(b):
            both = 3 * ln_steps(1)
            if isinstance(b, int) and b < 1:
                return (2 + b) * ln_steps(1)
            if isinstance(b, int) and b > B - 2:
                return both + (B - 3) * ln_steps(2) + (b - (B - 2)) * ln_steps(1)
            return b * ln_steps(2) + (both - ln_steps(2))

        @block.sync
        def _(sp):
            def load(b, p, half):
                after(sp, norm_in, done(TT, b - 1, 0))
                after(sp, bias_done, b - 1)
                sp.dma_start(x_in[:, p, :, :], src[bass.ds(b, 1), :, :].rearrange("o (t p) d -> p (o t) d", p=P)).then_inc(x_loaded[p], 16)

            def store_x(b, p, half):
                sp.wait_ge(x_ready, done(KC, b, KC))
                sp.dma_start(dst[bass.ds(b, 1), :, :].rearrange("o (t p) d -> p (o t) d", p=P), x_new[:, p, :, :]).then_inc(stored[p], 16)

            def store_normed(b, p, half):
                sp.wait_ge(norm_out, done(TT, b, TT))
                sp.dma_start(dst_normed[bass.ds(b, 1), :, :].rearrange("o (t p) d -> p (o t) d", p=P),
                             normed_new[:, p, :, :]).then_inc(stored[p], 16)

            def body(b, p, half):
                if there(b - 1):
                    store_x(b - 1, 1 - p, half + p - 1)
                if there(b + 3):
                    load(b + 3, 1 - p, half + 1 + p)
                if there(b - 1):
                    store_normed(b - 1, 1 - p, half + p - 1)

            def close(n):
                store_x(n - 1, 1, B // 2 - 1)
                store_normed(n - 1, 1, B // 2 - 1)
            for b in range(3):
                load(b, b % 2, b // 2)
            batches(sp, body, close)
            for p in range(2):
                sp.wait_ge(stored[p], 16 * STORES * (B // 2))

        @block.gpsimd
        def _(pool):
            pool.memset(maxT[:, :].bitcast(F32), 0.0).then_inc(cleared, 1)
            pool.memset(v_cur[:, :, NP * 2 * VW:], 0.0).then_inc(cleared, 1)
            if masked:
                pool.memset(mask_cur[:, :, :], 0.0).then_inc(cleared, 1)

            def input_side(b, p, half):
                after(pool, av_made, done(TT, b - 1, 0))
                pool.sem_inc(passed, 1)
                pool.tensor_copy(v_cur[:, p, 0:NP * 2 * VW], kv["v"][:, bass.ds(b, 1), :, :].rearrange("p o j c -> p (o j c)")).then_inc(v_ready, 1)
                after(pool, st_made, done(NP, b - 1, 0))
                hm = const["headmask"][:, :].unsqueeze(2).to_broadcast([P, HH, SK])
                for c in range(KC):
                    for out, k in ((kb_hi, kv["kT_hi"]), (kb_lo, kv["kT_lo"])):
                        cols = k[:, c, bass.ds(b * SK, SK)].bitcast(F32).unsqueeze(1).to_broadcast([P, HH, SK])
                        pool.tensor_tensor(out[:, p, c, :, :], cols, hm, ALU.mult).then_inc(kb_ready, 1)
                pool.wait_ge(x_loaded[p], 16 * (half + 1))
                after(pool, x_ready, done(KC, b - 1, 0))
                bo = kv["bo"][:, :].unsqueeze(1).to_broadcast([P, TT, D])
                pool.tensor_tensor(x_bias[:, p, :, :], x_in[:, p, :, :], bo, ALU.add).then_inc(bias_done, 1)

            def body(b, p, half):
                if there(b + 1):
                    input_side(b + 1, 1 - p, half + p)
            input_side(0, 0, 0)
            batches(pool, body)

        @block.tensor
        def _(pe):
            def turn_input(b, p):
                pe.wait_ge(norm_in, done(TT, b, TT))
                after(pe, a_lo, b - 1)
                for c in range(KC):
                    for t in range(TT):
                        m = pe.transpose(psum[:, c, t * P:(t + 1) * P], normed[:, t, c * P:(c + 1) * P], ident[:, :])
                m.then_inc(turned, 1)

            def queries(b, p):
                pe.wait_ge(turned_lo, b + 1)
                for m in range(KC):
                    for c in range(KC):
                        cols = slice(m * P, (m + 1) * P)
                        q = three_passes(pe, psum[:, m, :], kv["wq_hi"][:, c, cols], kv["wq_lo"][:, c, cols],
                                         nT_hi[:, c, :], nT_lo[:, c, :], c == 0, c == KC - 1)
                    q.then_inc(q_made, 1)

            def maxima(b, p, tiles):
                if 0 in tiles:
                    pe.wait_ge(q_hi, done(KC, b, KC))
                    pe.wait_ge(kb_ready, done(2 * KC, b, 2 * KC))
                    after(pe, max_ready, b)
                    if masked:
                        pe.wait_ge(mask_ready, b + 1)
                for t in tiles:
                    for c in range(KC):
                        after(pe, s_taken, done(TT * KC, b, t * KC + c - 1))
                        m = pe.matmul(psum[:, 2 + c, :], qT_hi[:, p, c, t * P:(t + 1) * P], kb_hi[:, p, c, :, :],
                                      start=True, stop=not masked)
                        if masked:
                            m = pe.matmul(psum[:, 2 + c, :], mask_cur[:, p, t * P:(t + 1) * P], const["keysel"][:, :, :],
                                          start=False, stop=True)
                        m.then_inc(s_made, 1)

            def turn_maxima(b):
                pe.wait_ge(s_taken, done(TT * KC, b, TT * KC))
                for t in range(TT):
                    m = pe.transpose(psum[0:H, 3, t * P:(t + 1) * P], s_max[:, t, :], ident[:, :])
                m.then_inc(max_turned, 1)

            def scores(b, p, pairs):
                if 0 in pairs:
                    pe.wait_ge(q_lo, done(KC, b, KC))
                    pe.wait_ge(max_ready, b + 1)
                    after(pe, lg_out, b - 1)
                for j in pairs:
                    after(pe, exp_done, done(NP, b, j - 1))
                    c, heads = j // (NP // KC), slice(2 * (j % (NP // KC)), 2 * (j % (NP // KC)) + 2)
                    out = psum[:, 4 + j % 2, :]
                    three_passes(pe, out, kb_hi[:, p, c, heads, :], kb_lo[:, p, c, heads, :],
                                 qT_hi[:, p, c, :], qT_lo[:, p, c, :], True, False)
                    if masked:
                        pe.matmul(out, const["keysel"][:, 0:2, :], mask_cur[:, p, :], start=False, stop=False)
                    pe.matmul(out, const["negsel"][:, j, :], maxT[:, :], start=False, stop=True).then_inc(st_made, 1)

            def weighted_values(b, p, t):
                if t == 0:
                    pe.wait_ge(exp_done, done(NP, b, NP))
                    pe.wait_ge(v_ready, b + 1)
                    after(pe, x_ready, done(KC, b, 0))
                if t >= 2:
                    pe.wait_ge(av_taken, done(TT, b, t - 1))
                for j in range(NP):
                    cols = slice(j * 2 * VW, j * 2 * VW + PE_COLS)
                    m = pe.matmul(psum[:, 6 + t % 2, cols], probs[:, j, t * P:(t + 1) * P], v_cur[:, p, cols],
                                  start=True, stop=True)
                m.then_inc(av_made, 1)

            def turn_attention(b):
                pe.wait_ge(av_taken, done(TT, b, TT))
                if there(b - 1):
                    pe.wait_ge(new_out, b)
                else:
                    pe.wait_ge(q_lo, 2 * KC)
                for c in range(KC):
                    for t in range(TT):
                        m = pe.transpose(psum[:, c, t * P:(t + 1) * P], att[:, t, c * P:(c + 1) * P], ident[:, :])
                m.then_inc(a_turned, 1)

            def outputs(b):
                pe.wait_ge(a_lo, b + 1)
                for t in range(TT):
                    for c in range(KC):
                        rows = slice(t * P, (t + 1) * P)
                        m = three_passes(pe, psum[:, 6 + t // 2, (t % 2) * D:(t % 2 + 1) * D], aT_hi[:, c, rows], aT_lo[:, c, rows],
                                         kv["wo_hi"][:, c, :], kv["wo_lo"][:, c, :], c == 0, c == KC - 1)
                    if t % 2:
                        m.then_inc(o_made, 1)

            def route(b, last):
                pe.wait_ge(new_out, b + 1)
                if not last:
                    pe.wait_ge(exp_done, done(NP, b + 1, NP))
                for t in range(TT):
                    for c in range(KC):
                        m = pe.matmul(psum[:, 4, t * PE_COLS:(t + 1) * PE_COLS], newT[:, c, t * P:(t + 1) * P], kv["wr"][:, c, :],
                                      start=(c == 0), stop=(c == KC - 1))
                m.then_inc(lg_made, 1)

            pe.wait_ge(cleared, 3 if masked else 2)

            def body(b, p, half):
                nxt = there(b + 1)
                scores(b, p, range(0, 2))
                if there(b - 1):
                    outputs(b - 1)
                if nxt:
                    turn_input(b + 1, 1 - p)
                scores(b, p, range(2, 5))
                if nxt:
                    queries(b + 1, 1 - p)
                scores(b, p, range(5, 8))
                for t in range(TT):
                    if nxt:
                        maxima(b + 1, 1 - p, [t])
                    weighted_values(b, p, t)
                    if t == 1 and there(b - 1):
                        if nxt:
                            pe.wait_ge(q_lo, done(KC, b + 1, KC))
                        else:
                            pe.wait_ge(a_lo, b)
                        turn_new(b - 1, 1 - p)
                if there(b - 1):
                    route(b - 1, not nxt)
                if nxt:
                    turn_maxima(b + 1)
                turn_attention(b)

            def turn_new(b, p):
                pe.wait_ge(norm_out, done(TT, b, TT))
                new_transposes(b, p)

            def new_transposes(b, p):
                for c in range(KC):
                    for t in range(TT):
                        m = pe.transpose(psum[:, c, t * P:(t + 1) * P], normed_new[:, p, t, c * P:(c + 1) * P], ident[:, :])
                m.then_inc(new_turned, 1)

            def close(n):
                outputs(n - 1)
                turn_new(n - 1, 1)
                route(n - 1, True)
            turn_input(0, 0)
            queries(0, 0)
            maxima(0, 0, range(TT))
            turn_maxima(0)
            batches(pe, body, close)

        @block.scalar
        def _(act):
            def input_hi(b, p):
                act.wait_ge(turned, b + 1)
                after(act, q_made, done(KC, b, 0))
                act.activation(nT_hi[:, :, :], psum[:, 0:KC, :], ACT.Copy).then_inc(turned_hi, 1)

            def queries_hi(b, p):
                for m in range(KC):
                    act.wait_ge(q_made, done(KC, b, m + 1))
                    act.activation(qT_hi[:, p, m, :], psum[:, m, :], ACT.Identity, bias=kv["bq"][:, m:m + 1]).then_inc(q_hi, 1)

            def exps(b, pairs):
                if 0 in pairs:
                    after(act, av_made, done(TT, b, 0))
                for j in pairs:
                    act.wait_ge(st_made, done(NP, b, j + 1))
                    act.activation(probs[:, j, :], psum[:, 4 + j % 2, :], ACT.Exp, scale=DH ** -0.5).then_inc(exp_done, 1)

            def new_copy(b):
                act.wait_ge(new_turned, b + 1)
                after(act, lg_made, b)
                act.activation(newT[:, :, :], psum[:, 0:KC, :], ACT.Copy).then_inc(new_out, 1)

            def new_norm(b, p, half):
                act.wait_ge(shifted, b + 1)
                after(act, stored[p], half * (16 * STORES))
                after(act, new_turned, b)
                for t in range(TT):
                    act.activation(normed_new[:, p, t, :], x_new[:, p, t, :], ACT.Identity, bias=shift2[:, t:t + 1],
                                   scale=rstd[:, TT + t:TT + t + 1]).then_inc(norm_out, 1)

            def attention_hi(b):
                act.wait_ge(a_turned, b + 1)
                after(act, o_made, done(KC, b, 0))
                act.activation(aT_hi[:, :, :], psum[:, 0:KC, :], ACT.Copy).then_inc(a_hi, 1)

            def body(b, p, half):
                exps(b, range(0, 2))
                if there(b + 1):
                    input_hi(b + 1, 1 - p)
                exps(b, range(2, 5))
                if there(b + 1):
                    queries_hi(b + 1, 1 - p)
                exps(b, range(5, 8))
                if there(b - 1):
                    new_norm(b - 1, 1 - p, half + p - 1)
                    new_copy(b - 1)
                attention_hi(b)

            def close(n):
                new_norm(n - 1, 1, B // 2 - 1)
                new_copy(n - 1)
            input_hi(0, 0)
            queries_hi(0, 0)
            batches(act, body, close)

        @block.vector
        def _(dve):
            dve.wait_ge(cleared, 3 if masked else 2)

            def mask_of(b, p):
                after(dve, st_made, done(NP, b - 1, 0))
                dve.tensor_scalar(mask_cur[0:SK, p, :], kv["mask"][:, :], kv["pad"][:, bass.ds(b, 1)], -BIG,
                                  ALU.mult, ALU.add).then_inc(mask_ready, 1)

            def layernorms(b, p, half, ahead_of_new=None, between=None):
                ahead, new = there(b + 2), there(b - 1)

                def before_input():
                    dve.wait_ge(x_loaded[p], half * 16 + 32)
                    after(dve, norm_in, done(TT, b + 2, 0))

                def before_new():
                    ahead_of_new()
                    dve.wait_ge(x_ready, done(KC, b - 1, KC))
                    after(dve, norm_out, done(TT, b - 1, 0))

                kinds = [(x_in[:, p, :, :], 0, before_input)] * ahead + [(x_new[:, 1 - p, :, :], 1, before_new)] * new
                xs, parts, before = zip(*kinds)
                steps = ln_steps(len(xs))
                layernorm_stats(dve, xs, parts, stats, mv, rstd, tmp, ln, ln_start(b), passed, before, between)
                dve.wait_ge(ln, ln_start(b) + steps)
                if new:
                    dve.scalar_tensor_tensor(shift2[:, :], mv[:, TT:, 0], -1.0, rstd[:, TT:], ALU.mult, ALU.mult).then_inc(shifted, 1)

            def input_norm(b, p, tiles=range(TT)):
                if 0 in tiles:
                    after(dve, turned, b)
                for t in tiles:
                    dve.tensor_scalar(normed[:, t, :], x_in[:, p, t, :], mv[:, t, 0:1], rstd[:, t:t + 1],
                                      ALU.subtract, ALU.mult).then_inc(norm_in, 1)

            def input_lo(b):
                dve.wait_ge(turned_hi, b + 1)
                dve.tensor_tensor(nT_lo[:, :, :], psum[:, 0:KC, :], nT_hi[:, :, :].bitcast(F32), ALU.subtract).then_inc(turned_lo, 1)

            def queries_lo(b, p):
                for m in range(KC):
                    dve.wait_ge(q_hi, done(KC, b, m + 1))
                    dve.scalar_tensor_tensor(qT_lo[:, p, m, :], psum[:, m, :], kv["bq"][:, m:m + 1],
                                             qT_hi[:, p, m, :].bitcast(F32), ALU.add, ALU.subtract).then_inc(q_lo, 1)

            def maxima(b, tiles):
                if 0 in tiles:
                    after(dve, max_turned, b)
                for t in tiles:
                    for c in range(KC):
                        dve.wait_ge(s_made, done(TT * KC, b, t * KC + c + 1))
                        s = psum[:, 2 + c, :].rearrange("p (h k) -> p h k", k=SK)
                        dve.tensor_reduce(s_max[:, t, c * HH:(c + 1) * HH], s, AX.X, ALU.max).then_inc(s_taken, 1)

            def maxima_copy(b):
                dve.wait_ge(max_turned, b + 1)
                after(dve, st_made, done(NP, b, 0))
                dve.tensor_copy(maxT[0:H, :], psum[0:H, 3, :]).then_inc(max_ready, 1)

            def normalise(b, t):
                if t == 0:
                    after(dve, a_turned, b)
                dve.wait_ge(av_made, done(TT, b, t + 1))
                av = psum[:, 6 + t % 2, 0:H * VW].rearrange("p (h c) -> p h c", c=VW)
                dve.reciprocal(recip[:, t, :], av[:, :, DH]).then_inc(av_recip, 1)
                dve.wait_ge(av_recip, done(TT, b, t + 1))
                dve.tensor_tensor(att[:, t, :].rearrange("p (h c) -> p h c", c=DH), av[:, :, 0:DH],
                                  recip[:, t, :].unsqueeze(2).to_broadcast([P, H, DH]), ALU.mult).then_inc(av_taken, 1)

            def router_copy(b):
                dve.wait_ge(lg_made, b + 1)
                dve.tensor_copy(logits_all[:, bass.ds(b * TT, TT), :], psum[:, 4, 0:TT * PE_COLS].rearrange("p (t e) -> p t e", e=PE_COLS)[:, :, 0:8]).then_inc(lg_out, 1)

            def attention_lo(b):
                dve.wait_ge(a_hi, b + 1)
                dve.tensor_tensor(aT_lo[:, :, :], psum[:, 0:KC, :], aT_hi[:, :, :].bitcast(F32), ALU.subtract).then_inc(a_lo, 1)

            def residual(b, p, half):
                dve.wait_ge(bias_done, b + 1)
                after(dve, stored[p], half * (16 * STORES))
                after(dve, norm_out, done(TT, b, 0))
                for n in range(KC):
                    dve.wait_ge(o_made, done(KC, b, n + 1))
                    tiles = slice(2 * n, 2 * n + 2)
                    dve.tensor_tensor(x_new[:, p, tiles, :], psum[:, 6 + n, :].rearrange("p (t d) -> p t d", d=D),
                                      x_bias[:, p, tiles, :], ALU.add).then_inc(x_ready, 1)

            def body(b, p, half):
                nxt = there(b + 1)
                if masked and nxt:
                    mask_of(b + 1, 1 - p)

                def ahead_of_new():
                    if there(b - 1):
                        residual(b - 1, 1 - p, half + p - 1)
                    if nxt:
                        input_lo(b + 1)

                def between():
                    if nxt:
                        queries_lo(b + 1, 1 - p)
                if there(b - 1):
                    layernorms(b, p, half, ahead_of_new, between)
                else:
                    layernorms(b, p, half)
                    ahead_of_new()
                    between()
                for t in range(TT):
                    if nxt:
                        maxima(b + 1, [t])
                    normalise(b, t)
                    if there(b + 2):
                        input_norm(b + 2, p, [t])
                if nxt:
                    maxima_copy(b + 1)
                if there(b - 1):
                    router_copy(b - 1)
                attention_lo(b)

            def close(n):
                layernorms(n, 0, B // 2, lambda: residual(n - 1, 1, B // 2 - 1))
                router_copy(n - 1)

            if masked:
                mask_of(0, 0)
            layernorms(-2, 0, -1)
            input_norm(0, 0)
            input_lo(0)
            queries_lo(0, 0)
            layernorms(-1, 1, -1)
            input_norm(1, 1)
            maxima(0, range(TT))
            maxima_copy(0)
            batches(dve, body, close)


def alloc_layer(sc, masked):
    kv = {"masked": masked, "name": sc.phase}
    for n in ("kT_hi", "kT_lo"):
        kv[n] = sc.sb(n, [P, KC, B * SK], F32R)
    for n in ("wq_hi", "wq_lo", "wo_hi", "wo_lo"):
        kv[n] = sc.sb(n, [P, KC, D], F32R)
    kv["v"] = sc.sb("v_aug", [P, B, NP, 2 * VW])
    kv["bo"] = sc.sb("bo_bcast", [P, D])
    kv["bk"], kv["bq"] = sc.sb("bk_col", [P, KC]), sc.sb("bq_col", [P, KC])
    kv["wr"] = sc.sb("wr_sb", [P, KC, PE_COLS])
    if masked:
        kv["mask"], kv["pad"] = sc.sb("mask_keep", [SK, S], BF16), sc.sb("pad_keep", [SK, B])
    return kv


E = 8
TOPK = N_TOK // E
SLOT = 32
TOP_BIT = 29
F = 682
GROUPS_UP = 4
FC = -(-F // P)
FR = F - (FC - 1) * P
ROW = D + E
CHUNKS = P // E


def route_expert_choice(nc, const, psum, logits, br, rows_dram, thresh_dram, idx):
    with ExitStack() as ctx:
        sc = Scope(nc, ctx, "choice", const)
        bias = sc.sb("bias", [P, E])
        top, total = sc.sb("top", [P, NT]), sc.sb("total", [P, NT])
        score = sc.sb("score", [P, NT, E])
        by_e = sc.sb("by_e", [P, E, NT])
        turned = sc.sb("turned", [P, 4, P])
        hits = sc.sb("hits", [P, 4 * P], BF16)
        count, found, bit, cand, add = (sc.sb(n, [P, 1], d) for n, d in
                                        (("count", F32), ("found", I32), ("bit", I32), ("cand", I32), ("add", I32)))
        limits = sc.sb("limits", [P, 1], I32)
        same_e, before, ones = sc.sb("same_e", [P, E, CHUNKS]), sc.sb("before", [P, P], BF16), sc.sb("ones", [P, P], BF16)
        thresh = sc.sb("thresh", [P, P])
        above, equal, chosen = sc.sb("above", [P, E, NT], BF16), sc.sb("equal", [P, E, NT], BF16), sc.sb("chosen", [P, E, NT], BF16)
        keep_on = sc.sb("keep_on", [P, E, NT])
        run, rank, want = sc.sb("run", [P, E, NT]), sc.sb("rank", [P, E, NT]), sc.sb("want", [P, E])
        pos, part = sc.sb("pos", [P, E, NT], I32), sc.sb("part", [P, E, NT], I32)
        high, low = sc.sb("high", [P, E, NT]), sc.sb("low", [P, E, NT])
        slot_no, tile_no = sc.sb("slot_no", [P, SLOT]), sc.sb("tile_no", [P, NT])
        lane_no = sc.sb("lane_no", [P, 1])
        one_high = sc.sb("one_high", [P, 2, NT, SLOT], BF16)
        one_low = sc.sb("one_low", [P, 2, NT, SLOT], BF16)
        coded = sc.sb("coded", [P, 2, NT, 2, SLOT], BF16)
        listed = sc.sb("listed", [SLOT, E, 2, SLOT])

        made = sc.sem("made")
        bias_loaded, scores_stored = sc.sem("bias_loaded"), sc.sem("scores_stored")
        th_stored, th_loaded = sc.sem("th_stored"), sc.sem("th_loaded")
        step, exps, sums = sc.sem("step"), sc.sem("exps"), sc.sem("sums")
        t_made, counted = sc.sem("t_made"), sc.sem("counted")
        hit, decided = sc.sem("hit"), sc.sem("decided")
        found_all = sc.sem("found_all")
        high_made, low_made, lane_made, tile_made, list_made = (sc.sem(n) for n in ("high_made", "low_made", "lane_made", "tile_made", "list_made"))
        block = ctx.enter_context(nc.Block())

        @block.sync
        def _(sp):
            sp.dma_start(bias[:, :], br.partition_broadcast(P)).then_inc(bias_loaded, 16)
            sp.wait_ge(step, 6)
            sp.dma_start(rows_dram.rearrange("(t p) r -> p t r", p=P)[:, :, D:ROW], score[:, :, :]).then_inc(scores_stored, 16)
            sp.wait_ge(found_all, 1)
            sp.dma_start(thresh_dram.rearrange("(p o) -> p o", o=1), limits[:, :].bitcast(F32)).then_inc(th_stored, 16)
            sp.wait_ge(th_stored, 16)
            sp.dma_start(thresh[:, :], thresh_dram.partition_broadcast(P)).then_inc(th_loaded, 16)
            sp.wait_ge(scores_stored, 16)
            sp.wait_ge(th_loaded, 16)

        @block.gpsimd
        def _(pool):
            pool.memset(same_e[:, :, :], 1.0).then_inc(made, 1)
            pool.memset(before[:, :], 1.0).then_inc(made, 1)
            pool.memset(ones[:, :], 1.0).then_inc(made, 1)
            pool.memset(keep_on[:, :, :], 1.0).then_inc(made, 1)
            pool.iota(slot_no[:, :], pattern=[[1, SLOT]], base=0, channel_multiplier=0, allow_small_or_imprecise_dtypes=True).then_inc(made, 1)
            pool.iota(tile_no[:, :], pattern=[[1, NT]], base=0, channel_multiplier=0, allow_small_or_imprecise_dtypes=True).then_inc(made, 1)
            pool.iota(lane_no[:, :], pattern=[[0, 1]], base=0, channel_multiplier=1, allow_small_or_imprecise_dtypes=True).then_inc(made, 1)
            pool.wait_ge(made, 7)
            pool.memset(keep_on[:, :, 0:1], 0.0).then_inc(made, 1)
            pool.affine_select(out=before[:, :], in_=before[:, :], compare_op=ALU.is_gt, fill=0.0, base=0,
                               pattern=[[1, P]], channel_multiplier=-1).then_inc(made, 1)
            pool.affine_select(out=same_e[:, :, :], in_=same_e[:, :, :], compare_op=ALU.is_ge, fill=0.0, base=0,
                               pattern=[[-CHUNKS, E], [0, CHUNKS]], channel_multiplier=1).then_inc(made, 1)
            pool.wait_ge(made, 10)
            pool.affine_select(out=same_e[:, :, :], in_=same_e[:, :, :], compare_op=ALU.is_ge, fill=0.0, base=CHUNKS - 1,
                               pattern=[[CHUNKS, E], [0, CHUNKS]], channel_multiplier=-1).then_inc(made, 1)
            tiles = tile_no[:, :].unsqueeze(2).to_broadcast([P, NT, SLOT])
            for e in range(E):
                pool.wait_ge(low_made, e + 1)
                if e >= 2:
                    pool.wait_ge(list_made, e - 1)
                pool.tensor_tensor(coded[:, e % 2, :, 1, :], one_low[:, e % 2, :, :], tiles, ALU.mult).then_inc(tile_made, 1)

        @block.scalar
        def _(act):
            act.wait_ge(step, 3)
            act.activation(score[:, :, :], score[:, :, :], ACT.Exp).then_inc(exps, 1)
            for e in range(E):
                act.wait_ge(low_made, e + 1)
                if e >= 2:
                    act.wait_ge(list_made, e - 1)
                act.activation(coded[:, e % 2, :, 0, :], one_low[:, e % 2, :, :], ACT.Copy, scale=lane_no[:, 0:1]).then_inc(lane_made, 1)

        @block.tensor
        def _(pe):
            pe.wait_ge(step, 7)
            for r in range(4):
                t = pe.transpose(psum[:, 0, r * P:(r + 1) * P], by_e[:, :, r::4], const["ident"][:, :])
            t.then_inc(t_made, 1)
            pe.wait_ge(made, 11)
            with pe.Fori(0, TOP_BIT + 1) as i:
                pe.wait_ge(hit, i + 1)
                pe.matmul(psum[:, 1, 0:1], same_e[:, :, :], count[:, :], start=True, stop=True).then_inc(counted, 1)
            for n, x in enumerate((above, equal, chosen)):
                pe.wait_ge(sums, n + 1)
                pe.matmul(psum[:, 2 + 2 * n, :], before[:, :], x[:, :, :], start=True, stop=True)
                pe.matmul(psum[:, 3 + 2 * n if n < 2 else 0, :], ones[:, :], x[:, :, :], start=True, stop=True).then_inc(counted, 1)
            for e in range(E):
                pe.wait_ge(high_made, e + 1)
                pe.wait_ge(lane_made, e + 1)
                pe.wait_ge(tile_made, e + 1)
                for t in range(NT):
                    m = pe.matmul(psum[0:SLOT, 1, e * 2 * SLOT:(e + 1) * 2 * SLOT], one_high[:, e % 2, t, :],
                                  coded[:, e % 2, t, :, :], start=(t == 0), stop=(t == NT - 1))
                m.then_inc(list_made, 1)

        @block.vector
        def _(dve):
            n = 0

            def then(instruction):
                nonlocal n
                instruction.then_inc(step, 1)
                n += 1
                dve.wait_ge(step, n)

            def over_e(x):
                return x.unsqueeze(2).to_broadcast([P, NT, E])

            def over_t(x):
                return x.unsqueeze(2).to_broadcast([P, E, NT])

            dve.wait_ge(bias_loaded, 16)
            then(dve.tensor_tensor(score[:, :, :], logits[:, :, :], bias[:, :].unsqueeze(1).to_broadcast([P, NT, E]), ALU.add))
            then(dve.tensor_reduce(top[:, :], score[:, :, :], AX.X, ALU.max))
            then(dve.tensor_tensor(score[:, :, :], score[:, :, :], over_e(top[:, :]), ALU.subtract))
            dve.wait_ge(exps, 1)
            then(dve.tensor_reduce(total[:, :], score[:, :, :], AX.X, ALU.add))
            then(dve.reciprocal(total[:, :], total[:, :]))
            then(dve.tensor_tensor(score[:, :, :], score[:, :, :], over_e(total[:, :]), ALU.mult))
            then(dve.tensor_copy(by_e[:, :, :], score[:, :, :].rearrange("p t e -> p e t")))
            then(dve.memset(found[:, :], 0))
            then(dve.memset(bit[:, :], 1 << TOP_BIT))
            then(dve.memset(cand[:, :], 1 << TOP_BIT))
            dve.wait_ge(t_made, 1)
            then(dve.tensor_copy(turned[:, :, :], psum[:, 0, :].rearrange("p (r q) -> p r q", r=4)))
            with dve.Fori(0, TOP_BIT + 1) as i:
                dve.tensor_scalar(hits[:, :], turned[:, :, :].rearrange("p r q -> p (r q)"), cand[:, :].bitcast(F32), 0.0,
                                  ALU.is_ge, ALU.add, accum_out=count[:, :]).then_inc(hit, 1)
                dve.wait_ge(counted, i + 1)
                dve.scalar_tensor_tensor(add[:, :], psum[:, 1, 0:1], float(TOPK), bit[:, :], ALU.is_ge, ALU.mult).then_inc(decided, 1)
                dve.wait_ge(decided, i * 4 + 1)
                dve.tensor_tensor(found[:, :], found[:, :], add[:, :], ALU.bitwise_or).then_inc(decided, 1)
                dve.tensor_scalar(bit[:, :], bit[:, :], 1, None, ALU.logical_shift_right).then_inc(decided, 1)
                dve.wait_ge(decided, i * 4 + 3)
                dve.tensor_tensor(cand[:, :], found[:, :], bit[:, :], ALU.bitwise_or).then_inc(decided, 1)
                dve.wait_ge(decided, i * 4 + 4)
            dve.tensor_copy(limits[:, :], found[:, :]).then_inc(found_all, 1)
            dve.wait_ge(th_loaded, 16)
            dve.wait_ge(made, 11)
            limit = over_t(thresh[:, 0::CHUNKS])
            then(dve.tensor_tensor(above[:, :, :], by_e[:, :, :], limit, ALU.is_gt))
            dve.tensor_tensor(equal[:, :, :], by_e[:, :, :], limit, ALU.is_equal).then_inc(sums, 1)
            dve.wait_ge(sums, 1)
            dve.tensor_copy(add[:, :], found[:, :]).then_inc(sums, 1)
            dve.wait_ge(counted, TOP_BIT + 2)

            def flat(bank):
                return psum[:, bank, :].rearrange("p (e t) -> p e t", e=E)

            def ranks(within, totals):
                then(dve.tensor_copy(rank[:, :, :], flat(totals)))
                then(dve.tensor_tensor_scan(run[:, :, :].rearrange("p e t -> p (e t)"), keep_on[:, :, :].rearrange("p e t -> p (e t)"),
                                            rank[:, :, :].rearrange("p e t -> p (e t)"), 0.0, ALU.mult, ALU.add))
                then(dve.tensor_tensor(run[:, :, :], run[:, :, :], rank[:, :, :], ALU.subtract))
                then(dve.tensor_tensor(rank[:, :, :], flat(within), run[:, :, :], ALU.add))

            then(dve.tensor_reduce(want[:, :], flat(3), AX.X, ALU.add))
            then(dve.tensor_scalar(want[:, :], want[:, :], -1.0, float(TOPK), ALU.mult, ALU.add))
            dve.wait_ge(counted, TOP_BIT + 3)
            ranks(4, 5)
            then(dve.tensor_tensor(rank[:, :, :], rank[:, :, :], over_t(want[:, :]), ALU.is_lt))
            then(dve.tensor_tensor(rank[:, :, :], rank[:, :, :], equal[:, :, :], ALU.mult))
            then(dve.tensor_tensor(chosen[:, :, :], rank[:, :, :], above[:, :, :], ALU.add))
            dve.tensor_copy(add[:, :], found[:, :]).then_inc(sums, 1)
            dve.wait_ge(counted, TOP_BIT + 4)
            ranks(6, 0)
            then(dve.tensor_copy(pos[:, :, :], rank[:, :, :]))
            then(dve.tensor_scalar(part[:, :, :], pos[:, :, :], 5, None, ALU.logical_shift_right))
            then(dve.scalar_tensor_tensor(high[:, :, :], part[:, :, :], 1.0, chosen[:, :, :], ALU.add, ALU.mult))
            then(dve.tensor_scalar(high[:, :, :], high[:, :, :], -1.0, None, ALU.add))
            then(dve.tensor_scalar(part[:, :, :], pos[:, :, :], SLOT - 1, None, ALU.bitwise_and))
            then(dve.tensor_copy(low[:, :, :], part[:, :, :]))
            numbers = slot_no[:, :].unsqueeze(1).to_broadcast([P, NT, SLOT])
            for e in range(E):
                if e >= 2:
                    dve.wait_ge(list_made, e - 1)
                dve.tensor_tensor(one_low[:, e % 2, :, :], low[:, e, :].unsqueeze(2).to_broadcast([P, NT, SLOT]), numbers,
                                  ALU.is_equal).then_inc(low_made, 1)
                dve.tensor_tensor(one_high[:, e % 2, :, :], high[:, e, :].unsqueeze(2).to_broadcast([P, NT, SLOT]), numbers,
                                  ALU.is_equal).then_inc(high_made, 1)
            dve.wait_ge(list_made, E)
            then(dve.tensor_copy(listed[:, :, :, :], psum[0:SLOT, 1, :].rearrange("s (e c l) -> s e c l", e=E, c=2)))
            for q in range(P // SLOT):
                cols = slice(q * 8, (q + 1) * 8)
                then(dve.scalar_tensor_tensor(idx[q * SLOT:(q + 1) * SLOT, :, :], listed[:, :, 1, cols], float(P), listed[:, :, 0, cols],
                                              ALU.mult, ALU.add))


FP = FC * P
BIAS_ROW = 64
assert FR <= BIAS_ROW
EP = E // GROUPS_UP
HALF = TOPK // 2
HT = HALF // P
GJ = 2 * EP
PAIRS = FC // 2


def expert_choice_mixture(nc, const, psum, idx, x, x_normed, w_up, b_up, w_down):
    with ExitStack() as ctx:
        sc = Scope(nc, ctx, "moe", const)
        rows = sc.sb("rows", [P, GJ, HT, ROW])
        gates = sc.sb("gates", [P, GJ, HT])
        idx_get, idx_add = sc.sb("idx_get", [P, EP, 2 * HT], I32), sc.sb("idx_add", [P, EP, 2 * HT], I32)
        wu, wd = sc.sb("wu", [P, KC, FP]), sc.sb("wd", [P, FC, D])
        wu_hi, wu_lo = sc.sb("wu_hi", [P, KC, FP], F32R), sc.sb("wu_lo", [P, KC, FP], F32R)
        wd_hi, wd_lo = sc.sb("wd_hi", [P, EP, FC, D], F32R), sc.sb("wd_lo", [P, EP, FC, D], F32R)
        bu, bu_in = sc.sb("bu", [P, FC]), sc.sb("bu_in", [P, FC])
        xT_hi, xT_lo = sc.sb("xT_hi", [P, 2, KC, HALF], F32R), sc.sb("xT_lo", [P, 2, KC, HALF], F32R)
        mid = sc.sb("mid", [P, FC, HALF])
        mid_hi, mid_lo = sc.sb("mid_hi", [P, 2, FC, HALF], F32R), sc.sb("mid_lo", [P, 2, FC, HALF], F32R)
        y = sc.sb("y", [P, 2, HT, D])

        gates_copied = sc.sem("gates_copied")
        rows_in = [sc.sem(f"rows_in{j}") for j in range(GJ)]
        added = [sc.sem(f"added{p}") for p in range(2)]
        get_copied, add_copied = sc.sem("get_copied"), sc.sem("add_copied")
        wu_in, wd_in, wu_hi_made, wd_hi_made = sc.sem("wu_in"), sc.sem("wd_in"), sc.sem("wu_hi_made"), sc.sem("wd_hi_made")
        wu_ready, wd_ready = sc.sem("wu_ready"), sc.sem("wd_ready")
        turned, xT_hi_made, xT_ready = sc.sem("turned"), sc.sem("xT_hi_made"), sc.sem("xT_ready")
        up_made, silu_made = sc.sem("up_made"), sc.sem("silu_made")
        hi_made, lo_made = sc.sem("hi_made"), sc.sem("lo_made")
        down_made = [sc.sem(f"down_made{p}") for p in range(2)]
        y_made = sc.sem("y_made")
        cleared, passed, bu_copied = sc.sem("cleared"), sc.sem("passed"), sc.sem("bu_copied")
        block = ctx.enter_context(nc.Block())
        LAST = GROUPS_UP - 1

        def iterations(eng, body):
            with eng.Fori(0, LAST) as q:
                body(q, False)
            body(LAST, True)

        @block.sync
        def _(sp):
            def load_up(q):
                after(sp, wu_ready, q)
                sp.dma_start(wu[:, :, :], w_up[bass.ds(q, 1), :, :].rearrange("o (c p) f -> p (o c) f", p=P)).then_inc(wu_in, 16)
                sp.dma_start(bu_in[:, :], b_up[bass.ds(q, 1), :, :].rearrange("o p c -> p (o c)")).then_inc(wu_in, 16)

            def load_down(e):
                after(sp, wd_ready, e)
                sp.dma_start(wd[:, :, :], w_down[bass.ds(e, 1), :, :].rearrange("o (c p) d -> p (o c) d", p=P)).then_inc(wd_in, 16)
            with sp.Fori(0, GROUPS_UP) as q:
                load_up(q)
                for i in range(EP):
                    load_down(q * EP + i)

        @block.gpsimd
        def _(pool):
            for p in range(2):
                pool.memset(mid_lo[BIAS_ROW:, p, FC - 1, :].bitcast(F32), 0.0).then_inc(cleared, 1)
                pool.memset(mid_hi[BIAS_ROW:, p, FC - 1, :].bitcast(F32), 0.0).then_inc(cleared, 1)
            pool.wait_ge(cleared, 4)
            for p in range(2):
                pool.memset(mid_hi[BIAS_ROW:BIAS_ROW + 1, p, FC - 1, :].bitcast(F32), 1.0).then_inc(cleared, 1)
            pool.wait_ge(cleared, 6)

            def pass_wait():
                pool.sem_inc(passed, 1)

            def gather(e, i, h):
                if h == 0:
                    if not (isinstance(e, int) and e < EP):
                        for k in range(2):
                            pool.wait_ge(rows_in[i * 2 + k], (e - i) * (16 * HT // EP))
                        pass_wait()
                    pool.tensor_copy(idx_get[:, i, :], idx[:, bass.ds(e, 1), :].rearrange("p o r -> p (o r)")).then_inc(get_copied, 1)
                    pool.wait_ge(get_copied, e + 1)
                after(pool, turned, e * 2 + h - 2)
                after(pool, gates_copied, e * 2 + h - 2)
                pass_wait()
                for t in range(HT):
                    at = bass.IndirectOffsetOnAxis(ap=idx_get[:, i, h * HT + t:h * HT + t + 1], axis=0)
                    pool.indirect_dma_start(rows[:, i * 2 + h, t, :], None, x_normed, at, compute_op=ALU.bypass).then_inc(rows_in[i * 2 + h], 16)

            def add(e, i, h):
                for s in range(2):
                    pool.wait_ge(added[s], e * (16 * HT))
                if h == 0:
                    pass_wait()
                    pool.tensor_copy(idx_add[:, i, :], idx[:, bass.ds(e, 1), :].rearrange("p o r -> p (o r)")).then_inc(add_copied, 1)
                    pool.wait_ge(add_copied, e + 1)
                for t in range(HT):
                    pool.wait_ge(y_made, done(HT, e * 2 + h, t + 1))
                    pass_wait()
                    at = bass.IndirectOffsetOnAxis(ap=idx_add[:, i, h * HT + t:h * HT + t + 1], axis=0)
                    pool.indirect_dma_start(x, at, y[:, h, t, :], None, compute_op=ALU.add).then_inc(added[h], 16)

            def body(q, last):
                e = q * EP
                for h in range(2):
                    gather(e + 1, 1, h)
                for h in range(2):
                    if not last:
                        gather(e + EP, 0, h)
                    add(e, 0, h)
                for h in range(2):
                    add(e + 1, 1, h)

            for h in range(2):
                gather(0, 0, h)
            iterations(pool, body)
            for s in range(2):
                pool.wait_ge(added[s], E * 16 * HT)

        @block.tensor
        def _(pe):
            def turn(g, j, q):
                pe.wait_ge(rows_in[j], q * (16 * HT) + 16 * HT)
                after(pe, xT_ready, g)
                for c in range(KC):
                    for t in range(HT):
                        m = pe.transpose(psum[:, c, t * P:(t + 1) * P], rows[:, j, t, c * P:(c + 1) * P], const["ident"][:, :])
                m.then_inc(turned, 1)

            def up(g, p, turn_next):
                pe.wait_ge(xT_ready, g + 1)
                for f in range(FC):
                    if f == 3 and turn_next:
                        turn_next()
                    if f == 0:
                        pe.wait_ge(silu_made, g * FC)
                    if f >= 4:
                        pe.wait_ge(silu_made, done(FC, g, f - 3))
                    cols = slice(f * P, (f + 1) * P)
                    for c in range(KC):
                        m = three_passes(pe, psum[:, 2 + f % 4, :], wu_hi[:, c, cols], wu_lo[:, c, cols],
                                         xT_hi[:, p, c, :], xT_lo[:, p, c, :], c == 0, c == KC - 1)
                    m.then_inc(up_made, 1)

            def down(g, p, i):
                pe.wait_ge(y_made, g * HT)
                pe.wait_ge(lo_made, done(PAIRS + 1, g, PAIRS + 1))
                for t in range(HT):
                    rows_t = slice(t * P, (t + 1) * P)
                    for f in range(FC):
                        m = three_passes(pe, psum[:, 6 + t // 2, (t % 2) * D:(t % 2 + 1) * D], mid_hi[:, p, f, rows_t],
                                         mid_lo[:, p, f, rows_t], wd_hi[:, i, f, :], wd_lo[:, i, f, :], f == 0, f == FC - 1)
                    m.then_inc(down_made[p], 1)

            def body(q, last):
                g = q * GJ
                pe.wait_ge(wu_ready, q + 1)
                for j in range(GJ):
                    if j < GJ - 1:
                        up(g + j, j % 2, lambda: turn(g + j + 1, j + 1, q))
                    else:
                        up(g + j, j % 2, None if last else lambda: turn(g + GJ, 0, q + 1))
                    if j >= 1:
                        pe.wait_ge(wd_ready, q * EP + (j - 1) // 2 + 1)
                        down(g + j - 1, (j - 1) % 2, (j - 1) // 2)
                down(g + GJ - 1, 1, EP - 1)

            pe.wait_ge(cleared, 6)
            turn(0, 0, 0)
            iterations(pe, body)

        @block.scalar
        def _(act):
            def rows_hi(g, p):
                act.wait_ge(turned, g + 1)
                act.activation(xT_hi[:, p, :, :], psum[:, 0:KC, :], ACT.Copy).then_inc(xT_hi_made, 1)

            def up_weights(q):
                act.wait_ge(wu_in, q * 32 + 32)
                act.activation(wu_hi[:, :, :], wu[:, :, :], ACT.Copy).then_inc(wu_hi_made, 1)

            def down_weights(e, i):
                act.wait_ge(wd_in, e * 16 + 16)
                for f in range(0, FC, 3):
                    act.activation(wd_hi[:, i, f:f + 3, :], wd[:, f:f + 3, :], ACT.Copy).then_inc(wd_hi_made, 1)

            def hidden(g, p, u, rows_next):
                act.wait_ge(lo_made, g * (PAIRS + 1))
                for f in range(FC):
                    act.wait_ge(up_made, done(FC, g, f + 1))
                    valid = slice(0, P if f < FC - 1 else BIAS_ROW)
                    act.activation(mid[valid, f, :], psum[valid, 2 + f % 4, :], ACT.Silu, bias=bu[valid, f:f + 1]).then_inc(silu_made, 1)
                    if f % 2:
                        if f == 1:
                            act.wait_ge(down_made[p], u * HT)
                        act.wait_ge(silu_made, done(FC, g, f + 1))
                        if f < FC - 1:
                            act.activation(mid_hi[:, p, f - 1:f + 1, :], mid[:, f - 1:f + 1, :], ACT.Copy).then_inc(hi_made, 1)
                            if f == 3 and rows_next:
                                rows_next()
                        else:
                            act.activation(mid_hi[:, p, f - 1, :], mid[:, f - 1, :], ACT.Copy).then_inc(hi_made, 1)
                            act.activation(mid_hi[valid, p, f, :], mid[valid, f, :], ACT.Copy).then_inc(hi_made, 1)

            def body(q, last):
                act.wait_ge(wu_ready, q + 1)
                for j in range(GJ):
                    hidden(q * GJ + j, j % 2, q * EP + j // 2,
                           lambda: rows_hi(q * GJ + j + 1, (j + 1) % 2) if j < GJ - 1 or not last else None)
                if not last:
                    up_weights(q + 1)
                    for i in range(EP):
                        act.wait_ge(down_made[1], q * (EP * HT) + (i + 1) * HT)
                        down_weights(q * EP + EP + i, i)

            up_weights(0)
            down_weights(0, 0)
            rows_hi(0, 0)
            down_weights(1, 1)
            iterations(act, body)

        @block.vector
        def _(dve):
            def rows_lo(g, j, e, q):
                p = j % 2
                dve.wait_ge(rows_in[j], q * (16 * HT) + 16 * HT)
                dve.tensor_copy(gates[:, j, :], rows[:, j, :, bass.ds(e + D, 1)].rearrange("p t o -> p (t o)")).then_inc(gates_copied, 1)
                dve.wait_ge(xT_hi_made, g + 1)
                dve.tensor_tensor(xT_lo[:, p, :, :], psum[:, 0:KC, :], xT_hi[:, p, :, :].bitcast(F32), ALU.subtract).then_inc(xT_ready, 1)

            def up_weights(q):
                dve.wait_ge(wu_in, q * 32 + 32)
                dve.tensor_copy(bu[:, :], bu_in[:, :]).then_inc(bu_copied, 1)
                dve.wait_ge(wu_hi_made, q + 1)
                dve.wait_ge(bu_copied, q + 1)
                dve.tensor_tensor(wu_lo[:, :, :], wu[:, :, :], wu_hi[:, :, :].bitcast(F32), ALU.subtract).then_inc(wu_ready, 1)

            def down_weights(e, i):
                dve.wait_ge(wd_hi_made, e * 2 + 2)
                dve.tensor_tensor(wd_lo[:, i, :, :], wd[:, :, :], wd_hi[:, i, :, :].bitcast(F32), ALU.subtract).then_inc(wd_ready, 1)

            def hidden_lo(g, p, u, rows_next):
                for k in range(PAIRS):
                    if k == 2 and rows_next:
                        rows_next()
                    if k == 0:
                        dve.wait_ge(down_made[p], u * HT)
                    if k < PAIRS - 1:
                        dve.wait_ge(hi_made, done(PAIRS + 1, g, k + 1))
                        dve.tensor_tensor(mid_lo[:, p, 2 * k:2 * k + 2, :], mid[:, 2 * k:2 * k + 2, :],
                                          mid_hi[:, p, 2 * k:2 * k + 2, :].bitcast(F32), ALU.subtract).then_inc(lo_made, 1)
                    else:
                        dve.wait_ge(hi_made, done(PAIRS + 1, g, PAIRS + 1))
                        f, valid = FC - 1, slice(0, BIAS_ROW)
                        dve.tensor_tensor(mid_lo[:, p, f - 1, :], mid[:, f - 1, :], mid_hi[:, p, f - 1, :].bitcast(F32), ALU.subtract).then_inc(lo_made, 1)
                        dve.tensor_tensor(mid_lo[valid, p, f, :], mid[valid, f, :], mid_hi[valid, p, f, :].bitcast(F32), ALU.subtract).then_inc(lo_made, 1)

            def outputs(g, p, j, u):
                dve.wait_ge(gates_copied, g + 1)
                dve.wait_ge(added[p], u * (16 * HT))
                for t in range(HT):
                    dve.wait_ge(down_made[p], done(HT, u, t // 2 * 2 + 2))
                    dve.tensor_scalar(y[:, p, t, :], psum[:, 6 + t // 2, (t % 2) * D:(t % 2 + 1) * D],
                                      gates[:, j, t:t + 1], None, ALU.mult).then_inc(y_made, 1)

            def body(q, last):
                def out(j):
                    outputs(q * GJ + j, j % 2, j, q * EP + j // 2)
                for j in range(GJ):
                    if j < GJ - 1:
                        hidden_lo(q * GJ + j, j % 2, q * EP + j // 2, lambda: rows_lo(q * GJ + j + 1, j + 1, q * EP + (j + 1) // 2, q))
                    else:
                        hidden_lo(q * GJ + j, j % 2, q * EP + j // 2,
                                  None if last else lambda: rows_lo(q * GJ + GJ, 0, q * EP + EP, q + 1))
                    if j >= 1:
                        out(j - 1)
                if not last:
                    dve.wait_ge(up_made, (q + 1) * (GJ * FC))
                    dve.wait_ge(silu_made, (q + 1) * (GJ * FC))
                    up_weights(q + 1)
                    dve.wait_ge(down_made[1], q * (EP * HT) + HT)
                    down_weights(q * EP + EP, 0)
                out(GJ - 1)
                if not last:
                    down_weights(q * EP + EP + 1, 1)

            up_weights(0)
            down_weights(0, 0)
            rows_lo(0, 0, 0, 0)
            down_weights(1, 1)
            iterations(dve, body)


GOLDEN_CENTER = 1.0 / math.e
GOLDEN_LOWER = 0.5 - math.log(4.0 / 3.0)
GOLDEN_UPPER = 0.5
I_FF = 256
IC = I_FF // P
TINY = 1e-8


def route_zone(nc, const, logits, temperature, weight):
    with ExitStack() as ctx:
        sc = Scope(nc, ctx, "zone", const)
        temp, order = sc.sb("temp", [P, 1]), sc.sb("order", [P, E])
        inh, dist, zone, near = (sc.sb(n, [P, NT, E]) for n in ("inh", "dist", "zone", "near"))
        key, hit, picked, flag = (sc.sb(n, [P, NT, E]) for n in ("key", "hit", "picked", "flag"))
        best, total, lone, keep = (sc.sb(n, [P, NT]) for n in ("best", "total", "lone", "keep"))
        temp_loaded, order_made, step = sc.sem("temp_loaded"), sc.sem("order_made"), sc.sem("step")
        block = ctx.enter_context(nc.Block())
        DIST_READY = 7
        exps, divided = sc.sem("exps"), sc.sem("divided")

        @block.sync
        def _(sp):
            sp.dma_start(temp[:, :], temperature.partition_broadcast(P)).then_inc(temp_loaded, 16)

        @block.gpsimd
        def _(pool):
            pool.iota(order[:, :], pattern=[[-1, E]], base=E, channel_multiplier=0, allow_small_or_imprecise_dtypes=True).then_inc(order_made, 1)
        @block.scalar
        def _(act):
            act.wait_ge(divided, 1)
            act.activation(inh[:, :, :], inh[:, :, :], ACT.Exp, scale=-1.0).then_inc(exps, 1)
            act.wait_ge(step, DIST_READY)
            act.activation(weight[:, :, :], dist[:, :, :], ACT.Exp, scale=-1.0 / 0.1).then_inc(exps, 1)
            act.activation(near[:, :, :], dist[:, :, :], ACT.Exp, scale=-1.0 / 0.3).then_inc(exps, 1)

        @block.vector
        def _(dve):
            n = 0

            def then(instruction):
                nonlocal n
                instruction.then_inc(step, 1)
                n += 1
                dve.wait_ge(step, n)

            def over_e(x):
                return x.unsqueeze(2).to_broadcast([P, NT, E])

            keys = order[:, :].unsqueeze(1).to_broadcast([P, NT, E])
            dve.wait_ge(temp_loaded, 16)
            then(dve.reciprocal(temp[:, :], temp[:, :]))
            dve.tensor_scalar(inh[:, :, :], logits[:, :, :], temp[:, 0:1], None, ALU.mult).then_inc(divided, 1)
            dve.wait_ge(exps, 1)
            then(dve.tensor_scalar(inh[:, :, :], inh[:, :, :], 1.0, None, ALU.add))
            then(dve.reciprocal(inh[:, :, :], inh[:, :, :]))
            then(dve.tensor_scalar(zone[:, :, :], inh[:, :, :], GOLDEN_LOWER, None, ALU.is_ge))
            then(dve.scalar_tensor_tensor(zone[:, :, :], inh[:, :, :], GOLDEN_UPPER, zone[:, :, :], ALU.is_le, ALU.mult))
            then(dve.tensor_scalar(inh[:, :, :], inh[:, :, :], GOLDEN_CENTER, None, ALU.subtract))
            then(dve.scalar_tensor_tensor(dist[:, :, :], inh[:, :, :], -1.0, inh[:, :, :], ALU.mult, ALU.max))
            assert n == DIST_READY
            dve.wait_ge(exps, 2)
            then(dve.tensor_tensor(weight[:, :, :], weight[:, :, :], zone[:, :, :], ALU.mult))
            then(dve.tensor_reduce(total[:, :], weight[:, :, :], AX.X, ALU.add))
            then(dve.tensor_scalar(lone[:, :], total[:, :], TINY, None, ALU.is_lt))
            then(dve.tensor_scalar(keep[:, :], lone[:, :], -1.0, 1.0, ALU.mult, ALU.add))
            dve.wait_ge(exps, 3)
            dve.wait_ge(order_made, 1)
            left = near
            for k in range(2):
                then(dve.tensor_reduce(best[:, :], left[:, :, :], AX.X, ALU.max))
                then(dve.tensor_tensor(key[:, :, :], left[:, :, :], over_e(best[:, :]), ALU.is_ge))
                then(dve.tensor_tensor(key[:, :, :], key[:, :, :], keys, ALU.mult))
                then(dve.tensor_reduce(best[:, :], key[:, :, :], AX.X, ALU.max))
                then(dve.tensor_tensor(flag[:, :, :], key[:, :, :], over_e(best[:, :]), ALU.is_equal))
                if k == 0:
                    then(dve.scalar_tensor_tensor(hit[:, :, :], flag[:, :, :], -2.0, near[:, :, :], ALU.mult, ALU.add))
                    then(dve.tensor_copy(picked[:, :, :], flag[:, :, :]))
                    left = hit
            then(dve.tensor_tensor(picked[:, :, :], picked[:, :, :], flag[:, :, :], ALU.add))
            then(dve.tensor_tensor(near[:, :, :], near[:, :, :], picked[:, :, :], ALU.mult))
            then(dve.tensor_reduce(total[:, :], near[:, :, :], AX.X, ALU.add))
            then(dve.tensor_scalar(total[:, :], total[:, :], TINY, None, ALU.max))
            then(dve.reciprocal(total[:, :], total[:, :]))
            then(dve.tensor_tensor(total[:, :], total[:, :], lone[:, :], ALU.mult))
            then(dve.tensor_tensor(near[:, :, :], near[:, :, :], over_e(total[:, :]), ALU.mult))
            then(dve.tensor_tensor(weight[:, :, :], weight[:, :, :], over_e(keep[:, :]), ALU.mult))
            then(dve.tensor_tensor(weight[:, :, :], weight[:, :, :], near[:, :, :], ALU.add))
            then(dve.tensor_reduce(total[:, :], weight[:, :, :], AX.X, ALU.add))
            then(dve.tensor_scalar(total[:, :], total[:, :], TINY, None, ALU.max))
            then(dve.reciprocal(total[:, :], total[:, :]))
            then(dve.tensor_tensor(weight[:, :, :], weight[:, :, :], over_e(total[:, :]), ALU.mult))


def zone_mixture(nc, const, psum, weight, x, x_normed, w_gate, w_up, w_down, out):
    with ExitStack() as ctx:
        sc = Scope(nc, ctx, "zmix", const)
        wg_hi, wg_lo = sc.sb("wg_hi", [P, E, KC, I_FF], F32R), sc.sb("wg_lo", [P, E, KC, I_FF], F32R)
        wu_hi, wu_lo = sc.sb("wu_hi", [P, E, KC, I_FF], F32R), sc.sb("wu_lo", [P, E, KC, I_FF], F32R)
        wd_hi, wd_lo = sc.sb("wd_hi", [P, E, IC, D], F32R), sc.sb("wd_lo", [P, E, IC, D], F32R)
        raw = sc.sb("raw", [P, 4, 512])
        acc = sc.sb("acc", [P, 2, TT, D])
        xn = sc.sb("xn", [P, 2, TT, D])
        xT_hi, xT_lo = sc.sb("xT_hi", [P, 2, KC, S], F32R), sc.sb("xT_lo", [P, 2, KC, S], F32R)
        act_gate = sc.sb("act_gate", [P, IC, S])
        hid = sc.sb("hid", [P, IC, S])
        hid_hi, hid_lo = sc.sb("hid_hi", [P, 2, IC, S], F32R), sc.sb("hid_lo", [P, 2, IC, S], F32R)

        raw_in = [sc.sem(f"raw_in{k}") for k in range(4)]
        w_hi, w_ready = sc.sem("w_hi"), sc.sem("w_ready")
        acc_in, xn_in = ([sc.sem(f"{n}{p}") for p in range(2)] for n in ("acc_in", "xn_in"))
        stored = [sc.sem(f"stored{p}") for p in range(2)]
        turned, xT_hi_made, xT_ready = sc.sem("turned"), sc.sem("xT_hi_made"), sc.sem("xT_ready")
        gate_made, up_made, gate_out, up_out = sc.sem("gate_made"), sc.sem("up_made"), sc.sem("gate_out"), sc.sem("up_out")
        hi_made, lo_made = sc.sem("hi_made"), sc.sem("lo_made")
        down_made = sc.sem("down_made")
        acc_made = sc.sem("acc_made")
        block = ctx.enter_context(nc.Block())
        STEPS = 2 * E
        LAST = B // 2 - 1
        matrices = [(w, e) for e in range(E) for w in range(3)]

        def iterations(eng, body):
            with eng.Fori(0, LAST) as r:
                body(r, False)
            body(LAST, True)

        def parts(w, e):
            hi, lo = ((wg_hi, wg_lo), (wu_hi, wu_lo), (wd_hi, wd_lo))[w]
            return hi[:, e, :, :].rearrange("p c f -> p (c f)"), lo[:, e, :, :].rearrange("p c f -> p (c f)")

        def weights_for(pe, e, count):
            pe.wait_ge(w_ready, 3 * e + count)

        @block.sync
        def _(sp):
            def load(b, p, r):
                after(sp, turned, b - 1)
                sp.dma_start(xn[:, p, :, :], x_normed[bass.ds(b, 1), :, :].rearrange("o (t p) d -> p (o t) d", p=P)).then_inc(xn_in[p], 16)
                after(sp, stored[p], r * 16)
                sp.dma_start(acc[:, p, :, :], x[bass.ds(b, 1), :, :].rearrange("o (t p) d -> p (o t) d", p=P)).then_inc(acc_in[p], 16)

            def body(r, last):
                for p in range(2):
                    b = r * 2 + p
                    sp.wait_ge(acc_made, (b + 1) * (E * TT))
                    sp.dma_start(out[bass.ds(b, 1), :, :].rearrange("o (t p) d -> p (o t) d", p=P), acc[:, p, :, :]).then_inc(stored[p], 16)
                    if not last:
                        load(b + 2, p, r + 1)
            for p in range(2):
                load(p, p, 0)
            iterations(sp, body)
            for p in range(2):
                sp.wait_ge(stored[p], 16 * (B // 2))

        @block.gpsimd
        def _(pool):
            for n, (w, e) in enumerate(matrices):
                after(pool, w_ready, n - 3)
                src = (w_gate, w_up, w_down)[w][e, :, :].rearrange("(c p) f -> p c f", p=P)
                pool.dma_start(raw[:, n % 4, :].rearrange("p (c f) -> p c f", c=2), src).then_inc(raw_in[n % 4], 16)

        @block.tensor
        def _(pe):
            def turn(b, p, r):
                pe.wait_ge(xn_in[p], r * 16 + 16)
                after(pe, xT_ready, b)
                for c in range(KC):
                    for t in range(TT):
                        m = pe.transpose(psum[:, 6 + c, t * P:(t + 1) * P], xn[:, p, t, c * P:(c + 1) * P], const["ident"][:, :])
                m.then_inc(turned, 1)

            def gate_up(b, p, e, first):
                n = b * E + e
                if e == 0:
                    pe.wait_ge(xT_ready, b + 1)
                for w, (hi, lo), bank, last_out, made in ((0, (wg_hi, wg_lo), 0, gate_out, gate_made), (1, (wu_hi, wu_lo), 2, up_out, up_made)):
                    if first:
                        pe.wait_ge(w_ready, 3 * e + w + 1)
                    after(pe, last_out, n)
                    for i in range(IC):
                        cols = slice(i * P, (i + 1) * P)
                        for c in range(KC):
                            m = three_passes(pe, psum[:, bank + i, :], hi[:, e, c, cols], lo[:, e, c, cols],
                                             xT_hi[:, p, c, :], xT_lo[:, p, c, :], c == 0, c == KC - 1)
                    m.then_inc(made, 1)

            def down(b, p, e, first):
                n = b * E + e
                if first:
                    pe.wait_ge(w_ready, 3 * e + 3)
                pe.wait_ge(lo_made, n + 1)
                for t in range(TT):
                    if t % 2 == 0:
                        after(pe, acc_made, n * TT - TT + t + 2)
                    rows = slice(t * P, (t + 1) * P)
                    for i in range(IC):
                        m = three_passes(pe, psum[:, 4 + t // 2, (t % 2) * D:(t % 2 + 1) * D], hid_hi[:, e % 2, i, rows],
                                         hid_lo[:, e % 2, i, rows], wd_hi[:, e, i, :], wd_lo[:, e, i, :], i == 0, i == IC - 1)
                    if t % 2:
                        m.then_inc(down_made, 1)

            def steps(r, last, first):
                for p in range(2):
                    b = r * 2 + p
                    for e in range(E):
                        if e < E - 1:
                            if e == 2 and not (last and p == 1):
                                turn(b + 1, 1 - p, r + p)
                            gate_up(b, p, e + 1, first and p == 0)
                        elif not (last and p == 1):
                            gate_up(b + 1, 1 - p, 0, False)
                        down(b, p, e, first and p == 0)

            turn(0, 0, 0)
            gate_up(0, 0, 0, True)
            steps(0, False, True)
            with pe.Fori(1, LAST) as r:
                steps(r, False, False)
            steps(LAST, True, False)

        @block.scalar
        def _(act):
            def rows_hi(b, p):
                act.wait_ge(turned, b + 1)
                after(act, gate_made, b * E - E)
                after(act, up_made, b * E - E)
                act.activation(xT_hi[:, p, :, :], psum[:, 6:8, :], ACT.Copy).then_inc(xT_hi_made, 1)

            def steps(r, last, first):
                for p in range(2):
                    b = r * 2 + p
                    for e in range(E):
                        n = b * E + e
                        act.wait_ge(gate_made, n + 1)
                        after(act, hi_ready_to_reuse, n)
                        act.activation(act_gate[:, :, :], psum[:, 0:2, :], ACT.Silu).then_inc(gate_out, 1)
                        if e == 3 and not (last and p == 1):
                            rows_hi(b + 1, 1 - p)
                        act.wait_ge(up_out, n + 1)
                        after(act, down_made, n * 2 - 2)
                        act.activation(hid_hi[:, e % 2, :, :], hid[:, :, :], ACT.Copy).then_inc(hi_made, 1)

            hi_ready_to_reuse = up_out
            for n, (w, e) in enumerate(matrices):
                act.wait_ge(raw_in[n % 4], n // 4 * 16 + 16)
                act.activation(parts(w, e)[0], raw[:, n % 4, :], ACT.Copy).then_inc(w_hi, 1)
                if n == 2:
                    rows_hi(0, 0)
            steps(0, False, True)
            with act.Fori(1, LAST) as r:
                steps(r, False, False)
            steps(LAST, True, False)

        @block.vector
        def _(dve):
            def rows_lo(b, p):
                dve.wait_ge(xT_hi_made, b + 1)
                dve.tensor_tensor(xT_lo[:, p, :, :], psum[:, 6:8, :], xT_hi[:, p, :, :].bitcast(F32), ALU.subtract).then_inc(xT_ready, 1)

            def add(b, p, e, r):
                n = b * E + e
                if e == 0:
                    dve.wait_ge(acc_in[p], r * 16 + 16)
                else:
                    dve.wait_ge(acc_made, n * TT)
                for t in range(TT):
                    if t % 2 == 0:
                        dve.wait_ge(down_made, n * 2 + t // 2 + 1)
                    dve.scalar_tensor_tensor(acc[:, p, t, :], psum[:, 4 + t // 2, (t % 2) * D:(t % 2 + 1) * D],
                                             weight[:, bass.ds(b * TT + t, 1), e], acc[:, p, t, :], ALU.mult, ALU.add).then_inc(acc_made, 1)

            def hidden(b, p, e):
                n = b * E + e
                dve.wait_ge(gate_out, n + 1)
                dve.wait_ge(up_made, n + 1)
                after(dve, lo_made, n)
                dve.tensor_tensor(hid[:, :, :], act_gate[:, :, :], psum[:, 2:4, :], ALU.mult).then_inc(up_out, 1)

            def hidden_lo(b, p, e):
                n = b * E + e
                dve.wait_ge(hi_made, n + 1)
                dve.tensor_tensor(hid_lo[:, e % 2, :, :], hid[:, :, :], hid_hi[:, e % 2, :, :].bitcast(F32), ALU.subtract).then_inc(lo_made, 1)

            def steps(r, last, first):
                for p in range(2):
                    b = r * 2 + p
                    for e in range(E):
                        if e < E - 1:
                            nb, np_, ne = b, p, e + 1
                        else:
                            nb, np_, ne = b + 1, 1 - p, 0
                        over = last and p == 1
                        if not (over and e == E - 1):
                            hidden(nb, np_, ne)
                        if e == 2 and not over:
                            rows_lo(b + 1, 1 - p)
                        if not (over and e == E - 1):
                            hidden_lo(nb, np_, ne)
                        add(b, p, e, r)

            for n, (w, e) in enumerate(matrices):
                dve.wait_ge(w_hi, n + 1)
                dve.wait_ge(raw_in[n % 4], n // 4 * 16 + 16)
                dve.tensor_tensor(parts(w, e)[1], raw[:, n % 4, :], parts(w, e)[0].bitcast(F32), ALU.subtract).then_inc(w_ready, 1)
                if n == 2:
                    rows_lo(0, 0)
            hidden(0, 0, 0)
            hidden_lo(0, 0, 0)
            steps(0, False, True)
            with dve.Fori(1, LAST) as r:
                steps(r, False, False)
            steps(LAST, True, False)


def attention_layer(nc, const, psum, masked, name, w, src, dst, dst_normed, logits):
    with ExitStack() as ctx:
        kv = alloc_layer(Scope(nc, ctx, name), masked)
        attention_setup(nc, const, kv, w, psum)
        attention(nc, const, kv, psum, src, dst, dst_normed, logits)


def two_layers(nc, a, out):
    x1 = nc.dram_tensor("x1", (N_TOK, D), F32, kind="Internal").ap()
    rows1 = nc.dram_tensor("rows1", (N_TOK, ROW), F32, kind="Internal").ap()
    x3 = nc.dram_tensor("x3", (B, S, D), F32, kind="Internal").ap()
    normed3 = nc.dram_tensor("normed3", (B, S, D), F32, kind="Internal").ap()
    thresholds = nc.dram_tensor("thresholds", (P,), F32, kind="Internal").ap()
    x1_by_batch = x1.rearrange("(b s) d -> b s d", s=S)
    with ExitStack() as ctx:
        sc = Scope(nc, ctx, "main")
        const = {"ident": sc.sb("ident", [P, P]), "headmask": sc.sb("headmask", [P, HH]),
                 "negsel": sc.sb("negsel", [P, NP, P], F32R), "keysel": sc.sb("keysel", [P, HH, SK], BF16)}
        psum = ctx.enter_context(nc.psum_tensor("psum", [P, 8, 512], F32))
        logits = sc.sb("logits", [P, NT, E])
        const["sems"] = Semaphores(nc)
        make_constants(nc, const)

        w0 = {k: a[k + "0"] for k in ("wq", "wk", "wv", "wo", "bq", "bk", "bv", "bo", "wr")}
        attention_layer(nc, const, psum, False, "att0", {**w0, "ctx": a["ctx"], "mask": None, "pad": None}, a["x"], x1_by_batch,
                        rows1.rearrange("(b s) r -> b s r", s=S)[:, :, 0:D], logits)
        const["sems"].give_back()
        const["sems"] = Semaphores(nc)
        with ExitStack() as mixture:
            idx = Scope(nc, mixture, "lists").sb("idx", [P, E, TOPK // P], I32)
            route_expert_choice(nc, const, psum, logits, a["br"], rows1, thresholds, idx)
            expert_choice_mixture(nc, const, psum, idx, x1, rows1, a["w_up"], a["b_up"], a["w_down"])

        w1 = {k: a[k + "1"] for k in ("wq", "wk", "wv", "wo", "bq", "bk", "bv", "bo", "wr")}
        attention_layer(nc, const, psum, True, "att1", {**w1, "ctx": a["ctx"], "mask": a["mask"], "pad": a["pad"]}, x1_by_batch, x3,
                        normed3, logits)
        weight = sc.sb("weight", [P, NT, E])
        route_zone(nc, const, logits, a["temperature"], weight)
        zone_mixture(nc, const, psum, weight, x3, normed3, a["wg"], a["wu"], a["wd"], out)


def kernel(**inputs):
    import numpy as _np
    import concourse.bacc as _bacc
    from concourse import mybir as _mybir
    from concourse.bass_utils import run_bass_kernel_spmd as _run

    i = {k: _np.asarray(v) for k, v in inputs.items()}

    def columns(v):
        return v.reshape(-1, P).T

    w_up = _np.zeros((GROUPS_UP, D, FP), i["L0_ffn_W_up"].dtype)
    w_up[:, :, :F] = i["L0_ffn_W_up"]
    b_up = _np.zeros((GROUPS_UP, FP), i["L0_ffn_b_up"].dtype)
    b_up[:, :F] = i["L0_ffn_b_up"]
    w_down = _np.zeros((E, FP, D), i["L0_ffn_W_down"].dtype)
    w_down[:, :F] = i["L0_ffn_W_down"]
    w_down[:, (FC - 1) * P + BIAS_ROW] = i["L0_ffn_b_down"]
    laid = {
        "x": i["x"], "ctx": i["ctx_1024"].reshape(B * SK, D),
        "wq0": i["L0_xattn_Wq"], "wk0": i["L0_xattn_Wk"], "wv0": i["L0_xattn_Wv"], "wo0": i["L0_xattn_Wo"],
        "bq0": columns(i["L0_xattn_bq"]), "bk0": columns(i["L0_xattn_bk"]), "bv0": i["L0_xattn_bv"], "bo0": i["L0_xattn_bo"],
        "wr0": i["L0_ffn_Wr"], "br": i["L0_ffn_br"],
        "w_up": w_up, "b_up": b_up.reshape(GROUPS_UP, FC, P).transpose(0, 2, 1), "w_down": w_down,
        "wq1": i["L1_xattn_wq"].T, "wk1": i["L1_xattn_wk"].T, "wv1": i["L1_xattn_wv"].T, "wo1": i["L1_xattn_wo"].T,
        "bq1": columns(i["L1_xattn_bq"]), "bk1": columns(i["L1_xattn_bk"]), "bv1": i["L1_xattn_bv"], "bo1": i["L1_xattn_bo"],
        "wr1": i["L1_ffn_Wr"], "temperature": i["L1_ffn_temperature"],
        "mask": i["mask_SxS2_bk0"].T, "pad": i["mask_BxS2_bk1"].T,
        "wg": i["L1_ffn_Wg"], "wu": i["L1_ffn_Wu"], "wd": i["L1_ffn_Wd"],
    }
    nc = _bacc.Bacc("TRN2", target_bir_lowering=False, num_devices=1)
    arrays, args = {}, {}
    for name, v in laid.items():
        v = _np.ascontiguousarray(v)
        if v.dtype == _np.bool_:
            v = v.view(_np.int32)
        arrays[f"in_{name}"] = v
        args[name] = nc.dram_tensor(f"in_{name}", v.shape, _mybir.dt.from_np(v.dtype), kind="ExternalInput").ap()
    out = nc.dram_tensor("out_x", (B, S, D), _mybir.dt.float32, kind="ExternalOutput").ap()
    two_layers(nc, args, out)
    r = _run(nc, [arrays], core_ids=[0])
    return r.results[0]["out_x"]
```

```python
import math
from contextlib import ExitStack

import numpy as np

import concourse.bass as bass
from concourse import mybir

F32 = mybir.dt.float32
F32R = mybir.dt.float32r
BF16 = mybir.dt.bfloat16
I32 = mybir.dt.int32
U8 = mybir.dt.uint8
ALU = mybir.AluOpType
ACT = mybir.ActivationFunctionType
AX = mybir.AxisListType

P = 128
B, S, D = 16, 512, 256
SK = 64
H, DH = 16, 16
KC = D // P
TT = S // P
HH = H // KC
NP = H // 2
NT = B * TT
VW = DH + 1
N_TOK = B * S
LN_EPS = 1e-5
BIG = float(2.0 ** 60)
PE_COLS = 96
RSQRT_MAGIC = float(0x5F3759DF)
NEWTON = 3


def done(count_per_batch, b, k):
    return b * count_per_batch + k


def ln_steps(n):
    return n * 2 * TT + 3 + 3 * NEWTON


def after(eng, sem, value):
    if not isinstance(value, int) or value > 0:
        eng.wait_ge(sem, value)


class Semaphores:

    def __init__(self, nc):
        self.nc, self.stack, self.taken = nc, ExitStack(), []

    def take(self, name):
        self.taken.append(self.stack.enter_context(self.nc.semaphore(name)))
        return self.taken[-1]

    def give_back(self):
        with self.nc.Block() as block:
            @block.gpsimd
            def _(pool):
                for sem in self.taken:
                    pool.sem_clear(sem)
        self.stack.close()


class Scope:

    def __init__(self, nc, ctx, phase, const=None):
        self.nc, self.ctx, self.phase, self.const = nc, ctx, phase, const

    def sb(self, name, shape, dt=F32):
        return self.ctx.enter_context(self.nc.sbuf_tensor(f"{self.phase}_{name}", shape, dt))

    def sem(self, name):
        return self.const["sems"].take(f"{self.phase}_{name}")


def layernorm_stats(dve, xs, parts, stats, mv, rstd, tmp, sem, start, passed, before=(), between=None):
    n = 0
    for i, (x, k) in enumerate(zip(xs, parts)):
        if before:
            before[i]()
        for t in range(TT):
            dve.bn_stats(stats[:, k * TT + t, :], x[:, t, :]).then_inc(sem, 1)
            n += 1
    dve.wait_ge(sem, start + n)
    dve.sem_inc(passed, 1)
    for k in parts:
        for t in range(TT):
            dve.bn_aggr(mv[:, k * TT + t, :], stats[:, k * TT + t, :]).then_inc(sem, 1)
            n += 1
    dve.wait_ge(sem, start + n)
    cols = slice(parts[0] * TT, (parts[-1] + 1) * TT)
    var, guess, y = tmp[:, 0, cols], tmp[:, 1, cols], rstd[:, cols]
    dve.tensor_scalar(var, mv[:, cols, 1], LN_EPS, None, ALU.add).then_inc(sem, 1)
    n += 1
    dve.wait_ge(sem, start + n)
    dve.tensor_scalar(guess.bitcast(I32), var.bitcast(I32), 1, None, ALU.logical_shift_right).then_inc(sem, 1)
    n += 1
    dve.wait_ge(sem, start + n)
    dve.tensor_scalar(y.bitcast(I32), guess.bitcast(I32), -1.0, RSQRT_MAGIC, ALU.mult, ALU.add).then_inc(sem, 1)
    n += 1
    for k in range(NEWTON):
        if k == 1 and between:
            between()
        dve.wait_ge(sem, start + n)
        dve.scalar_tensor_tensor(guess, y, -0.5, y, ALU.mult, ALU.mult).then_inc(sem, 1)
        n += 1
        dve.wait_ge(sem, start + n)
        dve.tensor_tensor(guess, guess, var, ALU.mult).then_inc(sem, 1)
        n += 1
        dve.wait_ge(sem, start + n)
        dve.scalar_tensor_tensor(y, guess, 1.5, y, ALU.add, ALU.mult).then_inc(sem, 1)
        n += 1
    assert n == ln_steps(len(xs))


def three_passes(pe, out, st_hi, st_lo, mv_hi, mv_lo, first, last):
    pe.matmul(out, st_hi, mv_hi, start=first, stop=False)
    pe.matmul(out, st_hi, mv_lo, start=False, stop=False)
    return pe.matmul(out, st_lo, mv_hi, start=False, stop=last)


def constant_parts(sc, const):
    ident, headmask, negsel, keysel = const["ident"], const["headmask"], const["negsel"], const["keysel"]
    made, ident_made = sc.sem("const_made"), sc.sem("ident_made")
    negf = sc.sb("negsel_f", [P, NP, P])
    keyf = sc.sb("keysel_f", [P, H // 2, SK])

    def identity(pool):
        pool.memset(ident[:, :], 0.0).then_inc(ident_made, 1)
        pool.wait_ge(ident_made, 1)
        pool.affine_select(out=ident[:, :], in_=ident[:, :], compare_op=ALU.not_equal, fill=1.0, base=0,
                           pattern=[[-1, P]], channel_multiplier=1).then_inc(ident_made, 1)

    def selectors(pool):
        pool.memset(headmask[:, :], 1.0).then_inc(made, 1)
        pool.memset(negf[:, :, :], -1.0).then_inc(made, 1)
        pool.memset(keyf[:, :, :], 0.0).then_inc(made, 1)
        pool.wait_ge(made, 3)
        pool.affine_select(out=headmask[:, :], in_=headmask[:, :], compare_op=ALU.is_ge, fill=0.0, base=0,
                           pattern=[[-DH, HH]], channel_multiplier=1).then_inc(made, 1)
        pool.affine_select(out=keyf[:, :, :], in_=keyf[:, :, :], compare_op=ALU.not_equal, fill=1.0, base=0,
                           pattern=[[0, HH], [-1, SK]], channel_multiplier=1).then_inc(made, 1)
        v = negf[:, :, :].rearrange("p j (a k) -> p j a k", a=2)
        pool.affine_select(out=v, in_=v, compare_op=ALU.is_equal, fill=0.0, base=0,
                           pattern=[[-2, NP], [-1, 2], [0, SK]], channel_multiplier=1).then_inc(made, 1)
        pool.wait_ge(made, 6)
        pool.affine_select(out=headmask[:, :], in_=headmask[:, :], compare_op=ALU.is_ge, fill=0.0, base=DH - 1,
                           pattern=[[DH, HH]], channel_multiplier=-1).then_inc(made, 1)
        pool.tensor_copy(negsel[:, :, :], negf[:, :, :]).then_inc(made, 1)
        pool.tensor_copy(keysel[:, :, :], keyf[:, :, :]).then_inc(made, 1)

    return identity, selectors, ident_made


def setup_parts(sc, const, kv, w, psum, v_bank):
    V_BANKS, BH = 4, B // 2
    ctx_in = sc.sb("ctx_in", [P, B * SK // P, D])
    ctxT = sc.sb("ctxT", [P, KC, B, 2, SK])
    wk, wv = sc.sb("wk", [P, KC, D]), sc.sb("wv", [P, KC, D])
    bv = sc.sb("bv_bcast", [P, D])
    wq, wo = sc.sb("wq", [P, KC, D]), sc.sb("wo", [P, KC, D])
    loaded, qo_loaded = sc.sem("kv_loaded"), sc.sem("qo_loaded")
    small_loaded = sc.sem("small_loaded")
    turned, turned_out, turned_twice = sc.sem("ctx_turned"), sc.sem("ctx_turned_out"), sc.sem("ctx_turned_twice")
    k_made, k_hi, k_out = sc.sem("k_made"), sc.sem("k_hi"), sc.sem("k_out")
    v_made, v_out = sc.sem("v_made"), sc.sem("v_out")
    v_cleared, split_hi, split_lo = sc.sem("v_cleared"), sc.sem("split_hi"), sc.sem("split_lo")
    mask_loaded, wr_cleared = sc.sem("mask_loaded"), sc.sem("wr_cleared")
    NC8 = B * SK // P
    if w["mask"] is not None:
        mask32, pad32 = sc.sb("mask_u8", [SK, S // 4], I32), sc.sb("pad_u8", [SK, B // 4], I32)

    def load(sp):
        sp.dma_start(ctx_in[:, :, :], w["ctx"].rearrange("(n p) d -> p n d", p=P)).then_inc(loaded, 16)
        sp.dma_start(wk[:, :, :], w["wk"].rearrange("(c p) d -> p c d", p=P)).then_inc(loaded, 16)
        sp.dma_start(wv[:, :, :], w["wv"].rearrange("(c p) d -> p c d", p=P)).then_inc(loaded, 16)
        sp.dma_start(bv[:, :], w["bv"].partition_broadcast(P)).then_inc(small_loaded, 16)
        sp.dma_start(kv["bo"][:, :], w["bo"].partition_broadcast(P)).then_inc(small_loaded, 16)
        sp.dma_start(kv["bk"][:, :], w["bk"]).then_inc(small_loaded, 16)
        sp.dma_start(kv["bq"][:, :], w["bq"]).then_inc(small_loaded, 16)
        sp.dma_start(wq[:, :, :], w["wq"].rearrange("(c p) d -> p c d", p=P)).then_inc(qo_loaded, 16)
        sp.dma_start(wo[:, :, :], w["wo"].rearrange("(c p) d -> p c d", p=P)).then_inc(qo_loaded, 16)
        sp.wait_ge(wr_cleared, 1)
        sp.dma_start(kv["wr"][:, :, 0:8], w["wr"].rearrange("(c p) e -> p c e", p=P)).then_inc(small_loaded, 16)
        if w["mask"] is not None:
            sp.dma_start(mask32[:, :], w["mask"]).then_inc(mask_loaded, 16)
            sp.dma_start(pad32[:, :], w["pad"]).then_inc(mask_loaded, 16)
            sp.wait_ge(mask_loaded, 32)
        sp.wait_ge(small_loaded, 5 * 16)

    def clear(pool):
        pool.memset(kv["wr"][:, :, :], 0.0).then_inc(wr_cleared, 1)
        pool.memset(kv["v"][:, :, :, :], 0.0).then_inc(v_cleared, 1)
        pool.wait_ge(v_cleared, 1)
        ones = kv["v"][:, :, :, :].rearrange("p b j (a c) -> p (b j) a c", a=2)
        pool.memset(ones[0:SK, :, 0, DH:VW], 1.0).then_inc(v_cleared, 1)
        pool.memset(ones[SK:P, :, 1, DH:VW], 1.0).then_inc(v_cleared, 1)
        pool.wait_ge(v_cleared, 3)

    def turn_context(pe):
        pe.wait_ge(loaded, 48)
        for c in range(KC):
            for n in range(NC8):
                t = pe.transpose(psum[:, 2 * c + n // 4, (n % 4) * P:(n % 4 + 1) * P], ctx_in[:, n, c * P:(c + 1) * P],
                                 const["ident"][:, :])
                if n % 4 == 3:
                    t.then_inc(turned, 1)

    def keys(pe, i):
        if i == 0:
            pe.wait_ge(turned_out, KC * 2)
        m, n = i // 2, i % 2
        for c in range(KC):
            k = pe.matmul(psum[:, 4 + i, :], wk[:, c, m * P:(m + 1) * P], ctxT[:, c, n * BH:(n + 1) * BH, 0, :],
                          start=(c == 0), stop=(c == KC - 1))
        k.then_inc(k_made, 1)

    def values(pe, b):
        if b == 0:
            pe.wait_ge(turned_twice, KC * 2)
        if v_bank == 4 and b < V_BANKS:
            pe.wait_ge(k_out, b + 1)
        if b >= V_BANKS:
            pe.wait_ge(v_out, 2 * (b - V_BANKS + 1))
        for c in range(KC):
            v = pe.matmul(psum[:, v_bank + b % V_BANKS, 0:D], ctxT[:, c, b, :, :], wv[:, c, :], start=(c == 0), stop=(c == KC - 1))
        v.then_inc(v_made, 1)

    def context_out(act):
        for n in range(2 * KC):
            act.wait_ge(turned, n + 1)
            act.activation(ctxT[:, n // 2, (n % 2) * BH:(n % 2 + 1) * BH, 0, :],
                           psum[:, n, :].rearrange("p (b k) -> p b k", k=SK), ACT.Copy).then_inc(turned_out, 1)

    def high_parts(act):
        act.wait_ge(small_loaded, 5 * 16)
        for m in range(KC):
            for n in range(2):
                act.wait_ge(k_made, 2 * m + n + 1)
                act.activation(kv["kT_hi"][:, m, n * 512:(n + 1) * 512], psum[:, 4 + 2 * m + n, :], ACT.Identity,
                               bias=kv["bk"][:, m:m + 1]).then_inc(k_hi, 1)
        act.wait_ge(qo_loaded, 32)
        act.activation(kv["wq_hi"][:, :, :], wq[:, :, :], ACT.Copy).then_inc(split_hi, 1)
        act.activation(kv["wo_hi"][:, :, :], wo[:, :, :], ACT.Copy).then_inc(split_hi, 1)

    def context_twice(dve):
        for n in range(2 * KC):
            dve.wait_ge(turned_out, n + 1)
            dve.tensor_copy(ctxT[:, n // 2, (n % 2) * BH:(n % 2 + 1) * BH, 1, :],
                            psum[:, n, :].rearrange("p (b k) -> p b k", k=SK)).then_inc(turned_twice, 1)

    def keys_out(dve, i):
        if i == 0:
            dve.wait_ge(small_loaded, 5 * 16)
        dve.wait_ge(k_hi, i + 1)
        m, cols = i // 2, slice(i % 2 * 512, (i % 2 + 1) * 512)
        dve.scalar_tensor_tensor(kv["kT_lo"][:, m, cols], psum[:, 4 + i, :], kv["bk"][:, m:m + 1],
                                 kv["kT_hi"][:, m, cols].bitcast(F32), ALU.add, ALU.subtract).then_inc(k_out, 1)

    def rest(dve):
        dve.wait_ge(split_hi, 2)
        dve.wait_ge(qo_loaded, 32)
        dve.tensor_tensor(kv["wq_lo"][:, :, :], wq[:, :, :], kv["wq_hi"][:, :, :].bitcast(F32), ALU.subtract).then_inc(split_lo, 1)
        dve.tensor_tensor(kv["wo_lo"][:, :, :], wo[:, :, :], kv["wo_hi"][:, :, :].bitcast(F32), ALU.subtract).then_inc(split_lo, 1)
        if w["mask"] is not None:
            dve.wait_ge(mask_loaded, 32)
            dve.tensor_copy(kv["mask"][:, :], mask32[:, :].bitcast(U8))
            dve.tensor_scalar(kv["pad"][:, :], pad32[:, :].bitcast(U8), BIG, None, ALU.mult)

    def values_out(dve, b):
        if b == 0:
            dve.wait_ge(v_cleared, 3)
        dve.wait_ge(v_made, b + 1)
        for a in range(2):
            rows = slice(a * SK, (a + 1) * SK)
            heads = psum[rows, v_bank + b % V_BANKS, 0:D].rearrange("p (j a c) -> p j a c", a=2, c=DH)[:, :, a, :]
            bias = bv[rows, :].rearrange("p (j a c) -> p j a c", a=2, c=DH)[:, :, a, :]
            dve.tensor_tensor(kv["v"][rows, b, :, a * VW:a * VW + DH], heads, bias, ALU.add).then_inc(v_out, 1)

    return dict(load=load, clear=clear, turn_context=turn_context, keys=keys, values=values, context_out=context_out,
                           high_parts=high_parts, context_twice=context_twice, keys_out=keys_out, rest=rest, values_out=values_out, turned_twice=turned_twice, v_out=v_out)


def first_setup(nc, const, kv, w, psum):
    with ExitStack() as ctx:
        sc = Scope(nc, ctx, kv["name"] + "_setup", const)
        identity, selectors, ident_made = constant_parts(sc, const)
        parts = setup_parts(sc, const, kv, w, psum, 0)
        block = ctx.enter_context(nc.Block())

        @block.sync
        def _(sp):
            parts["load"](sp)

        @block.gpsimd
        def _(pool):
            identity(pool)
            parts["clear"](pool)
            selectors(pool)

        @block.tensor
        def _(pe):
            pe.wait_ge(ident_made, 2)
            parts["turn_context"](pe)
            for i in range(2 * KC):
                parts["keys"](pe, i)
            for b in range(B):
                parts["values"](pe, b)

        @block.scalar
        def _(act):
            parts["context_out"](act)
            parts["high_parts"](act)

        @block.vector
        def _(dve):
            parts["context_twice"](dve)
            for i in range(2 * KC):
                parts["keys_out"](dve, i)
            parts["rest"](dve)
            for b in range(B):
                parts["values_out"](dve, b)


def attention(nc, const, kv, psum, src, dst, dst_normed, logits_all):
    masked = kv["masked"]
    ident = const["ident"]
    STORES = 2
    with ExitStack() as ctx:
        sc = Scope(nc, ctx, kv["name"], const)
        x_in = sc.sb("x_in", [P, 2, TT, D])
        x_bias = sc.sb("x_bias", [P, 2, TT, D])
        x_new = sc.sb("x_new", [P, 2, TT, D])
        normed = sc.sb("normed", [P, TT, D])
        normed_new = sc.sb("normed_new", [P, 2, TT, D])
        nT_hi, nT_lo = sc.sb("nT_hi", [P, KC, S], F32R), sc.sb("nT_lo", [P, KC, S], F32R)
        newT = sc.sb("newT", [P, KC, S])
        qT_hi, qT_lo = sc.sb("qT_hi", [P, 2, KC, S], F32R), sc.sb("qT_lo", [P, 2, KC, S], F32R)
        kb_hi, kb_lo = sc.sb("kb_hi", [P, 2, KC, HH, SK], F32R), sc.sb("kb_lo", [P, 2, KC, HH, SK], F32R)
        v_cur = sc.sb("v_cur", [P, 2, (NP - 1) * 2 * VW + PE_COLS])
        s_max = sc.sb("s_max", [P, TT, H])
        maxT = sc.sb("maxT", [P, S], F32R)
        probs = sc.sb("probs", [P, NP, S])
        recip = sc.sb("recip", [P, TT, H])
        att = sc.sb("att", [P, TT, D])
        aT_hi, aT_lo = sc.sb("aT_hi", [P, KC, S], F32R), sc.sb("aT_lo", [P, KC, S], F32R)
        stats, mv = sc.sb("stats", [P, 2 * TT, 6]), sc.sb("mv", [P, 2 * TT, 2])
        rstd, shift2 = sc.sb("rstd", [P, 2 * TT]), sc.sb("shift2", [P, TT])
        tmp = sc.sb("ln_tmp", [P, 2, 2 * TT])
        mask_cur = sc.sb("mask_cur", [P, 2, S], BF16) if masked else None

        x_loaded = [sc.sem(f"x_loaded{p}") for p in range(2)]
        stored = [sc.sem(f"stored{p}") for p in range(2)]
        ln = sc.sem("ln")
        shifted = sc.sem("shifted")
        norm_in, norm_out = sc.sem("norm_in"), sc.sem("norm_out")
        bias_done = sc.sem("bias_done")
        v_ready = sc.sem("v_ready")
        kb_ready = sc.sem("kb_ready")
        mask_ready = sc.sem("mask_ready")
        turned, turned_hi, turned_lo = sc.sem("turned"), sc.sem("turned_hi"), sc.sem("turned_lo")
        q_made, q_hi, q_lo = sc.sem("q_made"), sc.sem("q_hi"), sc.sem("q_lo")
        s_made, s_taken = sc.sem("s_made"), sc.sem("s_taken")
        max_turned, max_ready = sc.sem("max_turned"), sc.sem("max_ready")
        st_made, exp_done = sc.sem("st_made"), sc.sem("exp_done")
        av_made, av_recip, av_taken = sc.sem("av_made"), sc.sem("av_recip"), sc.sem("av_taken")
        a_turned, a_hi, a_lo = sc.sem("a_turned"), sc.sem("a_hi"), sc.sem("a_lo")
        o_made, x_ready = sc.sem("o_made"), sc.sem("x_ready")
        new_turned, new_out = sc.sem("new_turned"), sc.sem("new_out")
        lg_made, lg_out = sc.sem("lg_made"), sc.sem("lg_out")
        cleared, passed = sc.sem("cleared"), sc.sem("passed")
        block = ctx.enter_context(nc.Block())

        def batches(eng, body, close=None):
            body(0, 0, 0)
            with eng.Fori(0, (B - 4) // 2) as r:
                body(r * 2 + 1, 1, r)
                body(r * 2 + 2, 0, r + 1)
            for b in range(B - 3, B):
                body(b, b % 2, b // 2)
            if close:
                close(B)

        def there(b):
            return not isinstance(b, int) or 0 <= b < B

        def ln_start(b):
            first = ln_steps(2) + ln_steps(1)
            if isinstance(b, int) and b < 1:
                return ln_steps(2)
            if isinstance(b, int) and b > B - 2:
                return first + (B - 3) * ln_steps(2) + (b - (B - 2)) * ln_steps(1)
            return b * ln_steps(2) + (first - ln_steps(2))

        @block.sync
        def _(sp):
            def load(b, p, half):
                after(sp, norm_in, done(TT, b - 1, 0))
                after(sp, bias_done, b - 1)
                sp.dma_start(x_in[:, p, :, :], src[bass.ds(b, 1), :, :].rearrange("o (t p) d -> p (o t) d", p=P)).then_inc(x_loaded[p], 16)

            def store_x(b, p, half):
                sp.wait_ge(x_ready, done(KC, b, KC))
                sp.dma_start(dst[bass.ds(b, 1), :, :].rearrange("o (t p) d -> p (o t) d", p=P), x_new[:, p, :, :]).then_inc(stored[p], 16)

            def store_normed(b, p, half):
                sp.wait_ge(norm_out, done(TT, b, TT))
                sp.dma_start(dst_normed[bass.ds(b, 1), :, :].rearrange("o (t p) d -> p (o t) d", p=P),
                             normed_new[:, p, :, :]).then_inc(stored[p], 16)

            def body(b, p, half):
                if there(b - 1):
                    store_x(b - 1, 1 - p, half + p - 1)
                if there(b + 3):
                    load(b + 3, 1 - p, half + 1 + p)
                if there(b - 1):
                    store_normed(b - 1, 1 - p, half + p - 1)

            def close(n):
                store_x(n - 1, 1, B // 2 - 1)
                store_normed(n - 1, 1, B // 2 - 1)
            for b in range(3):
                load(b, b % 2, b // 2)
            batches(sp, body, close)
            for p in range(2):
                sp.wait_ge(stored[p], 16 * STORES * (B // 2))

        @block.gpsimd
        def _(pool):
            pool.memset(maxT[:, :].bitcast(F32), 0.0).then_inc(cleared, 1)
            pool.memset(v_cur[:, :, NP * 2 * VW:], 0.0).then_inc(cleared, 1)
            if masked:
                pool.memset(mask_cur[:, :, :], 0.0).then_inc(cleared, 1)

            def input_side(b, p, half):
                after(pool, av_made, done(TT, b - 1, 0))
                pool.sem_inc(passed, 1)
                pool.tensor_copy(v_cur[:, p, 0:NP * 2 * VW], kv["v"][:, bass.ds(b, 1), :, :].rearrange("p o j c -> p (o j c)")).then_inc(v_ready, 1)
                after(pool, st_made, done(NP, b - 1, 0))
                hm = const["headmask"][:, :].unsqueeze(2).to_broadcast([P, HH, SK])
                for c in range(KC):
                    for out, k in ((kb_hi, kv["kT_hi"]), (kb_lo, kv["kT_lo"])):
                        cols = k[:, c, bass.ds(b * SK, SK)].bitcast(F32).unsqueeze(1).to_broadcast([P, HH, SK])
                        pool.tensor_tensor(out[:, p, c, :, :], cols, hm, ALU.mult).then_inc(kb_ready, 1)
                pool.wait_ge(x_loaded[p], 16 * (half + 1))
                after(pool, x_ready, done(KC, b - 1, 0))
                bo = kv["bo"][:, :].unsqueeze(1).to_broadcast([P, TT, D])
                pool.tensor_tensor(x_bias[:, p, :, :], x_in[:, p, :, :], bo, ALU.add).then_inc(bias_done, 1)

            def body(b, p, half):
                if there(b + 1):
                    input_side(b + 1, 1 - p, half + p)
            input_side(0, 0, 0)
            batches(pool, body)

        @block.tensor
        def _(pe):
            def turn_input(b, p):
                pe.wait_ge(norm_in, done(TT, b, TT))
                after(pe, a_lo, done(KC, b - 1, 0))
                for c in range(KC):
                    for t in range(TT):
                        m = pe.transpose(psum[:, c, t * P:(t + 1) * P], normed[:, t, c * P:(c + 1) * P], ident[:, :])
                m.then_inc(turned, 1)

            def queries(b, p):
                pe.wait_ge(turned_lo, b + 1)
                for m in range(KC):
                    for c in range(KC):
                        cols = slice(m * P, (m + 1) * P)
                        q = three_passes(pe, psum[:, m, :], kv["wq_hi"][:, c, cols], kv["wq_lo"][:, c, cols],
                                         nT_hi[:, c, :], nT_lo[:, c, :], c == 0, c == KC - 1)
                    q.then_inc(q_made, 1)

            def maxima(b, p, tiles):
                if 0 in tiles:
                    pe.wait_ge(q_hi, done(KC, b, KC))
                    pe.wait_ge(kb_ready, done(2 * KC, b, 2 * KC))
                    after(pe, max_ready, b)
                    if masked:
                        pe.wait_ge(mask_ready, b + 1)
                for t in tiles:
                    for c in range(KC):
                        after(pe, s_taken, done(TT * KC, b, t * KC + c - 1))
                        m = pe.matmul(psum[:, 2 + c, :], qT_hi[:, p, c, t * P:(t + 1) * P], kb_hi[:, p, c, :, :],
                                      start=True, stop=not masked)
                        if masked:
                            m = pe.matmul(psum[:, 2 + c, :], mask_cur[:, p, t * P:(t + 1) * P], const["keysel"][:, :, :],
                                          start=False, stop=True)
                        m.then_inc(s_made, 1)

            def turn_maxima(b):
                pe.wait_ge(s_taken, done(TT * KC, b, TT * KC))
                for t in range(TT):
                    m = pe.transpose(psum[0:H, 3, t * P:(t + 1) * P], s_max[:, t, :], ident[:, :])
                m.then_inc(max_turned, 1)

            def scores(b, p, pairs):
                if 0 in pairs:
                    pe.wait_ge(q_lo, done(KC, b, KC))
                    pe.wait_ge(max_ready, b + 1)
                    after(pe, lg_out, b - 1)
                for j in pairs:
                    after(pe, exp_done, done(NP, b, j - 1))
                    c, heads = j // (NP // KC), slice(2 * (j % (NP // KC)), 2 * (j % (NP // KC)) + 2)
                    out = psum[:, 4 + j % 2, :]
                    three_passes(pe, out, kb_hi[:, p, c, heads, :], kb_lo[:, p, c, heads, :],
                                 qT_hi[:, p, c, :], qT_lo[:, p, c, :], True, False)
                    if masked:
                        pe.matmul(out, const["keysel"][:, 0:2, :], mask_cur[:, p, :], start=False, stop=False)
                    pe.matmul(out, const["negsel"][:, j, :], maxT[:, :], start=False, stop=True).then_inc(st_made, 1)

            def weighted_values(b, p, t):
                if t == 0:
                    pe.wait_ge(exp_done, done(NP, b, NP - 1))
                    pe.wait_ge(v_ready, b + 1)
                    after(pe, x_ready, done(KC, b, 0))
                if t >= 2:
                    pe.wait_ge(av_taken, done(TT, b, t - 1))
                for j in range(NP):
                    if t == 0 and j == NP - 1:
                        pe.wait_ge(exp_done, done(NP, b, NP))
                    cols = slice(j * 2 * VW, j * 2 * VW + PE_COLS)
                    m = pe.matmul(psum[:, 6 + t % 2, cols], probs[:, j, t * P:(t + 1) * P], v_cur[:, p, cols],
                                  start=True, stop=True)
                m.then_inc(av_made, 1)

            def turn_attention(b):
                pe.wait_ge(av_taken, done(TT, b, TT))
                if there(b - 1):
                    pe.wait_ge(new_out, b)
                else:
                    pe.wait_ge(q_lo, 2 * KC)
                for c in range(KC):
                    for t in range(TT):
                        m = pe.transpose(psum[:, c, t * P:(t + 1) * P], att[:, t, c * P:(c + 1) * P], ident[:, :])
                m.then_inc(a_turned, 1)

            def outputs(b):
                pe.wait_ge(a_lo, done(KC, b, KC))
                for t in range(TT):
                    for c in range(KC):
                        rows = slice(t * P, (t + 1) * P)
                        m = three_passes(pe, psum[:, 6 + t // 2, (t % 2) * D:(t % 2 + 1) * D], aT_hi[:, c, rows], aT_lo[:, c, rows],
                                         kv["wo_hi"][:, c, :], kv["wo_lo"][:, c, :], c == 0, c == KC - 1)
                    if t % 2:
                        m.then_inc(o_made, 1)

            def route(b, last):
                pe.wait_ge(new_out, b + 1)
                if not last:
                    pe.wait_ge(exp_done, done(NP, b + 1, NP))
                for t in range(TT):
                    for c in range(KC):
                        m = pe.matmul(psum[:, 4, t * PE_COLS:(t + 1) * PE_COLS], newT[:, c, t * P:(t + 1) * P], kv["wr"][:, c, :],
                                      start=(c == 0), stop=(c == KC - 1))
                m.then_inc(lg_made, 1)

            pe.wait_ge(cleared, 3 if masked else 2)

            def body(b, p, half):
                nxt = there(b + 1)
                scores(b, p, range(0, 2))
                if there(b - 1):
                    outputs(b - 1)
                if nxt:
                    turn_input(b + 1, 1 - p)
                scores(b, p, range(2, 5))
                if nxt:
                    queries(b + 1, 1 - p)
                scores(b, p, range(5, 8))
                for t in range(TT):
                    if nxt:
                        maxima(b + 1, 1 - p, [t])
                    weighted_values(b, p, t)
                    if t == 1 and there(b - 1):
                        if nxt:
                            pe.wait_ge(q_lo, done(KC, b + 1, KC))
                        else:
                            pe.wait_ge(a_lo, done(KC, b, 0))
                        turn_new(b - 1, 1 - p)
                if there(b - 1):
                    route(b - 1, not nxt)
                if nxt:
                    turn_maxima(b + 1)
                turn_attention(b)

            def turn_new(b, p):
                pe.wait_ge(norm_out, done(TT, b, TT))
                new_transposes(b, p)

            def new_transposes(b, p):
                for c in range(KC):
                    for t in range(TT):
                        m = pe.transpose(psum[:, c, t * P:(t + 1) * P], normed_new[:, p, t, c * P:(c + 1) * P], ident[:, :])
                m.then_inc(new_turned, 1)

            def close(n):
                outputs(n - 1)
                turn_new(n - 1, 1)
                route(n - 1, True)
            turn_input(0, 0)
            queries(0, 0)
            maxima(0, 0, range(TT))
            turn_maxima(0)
            batches(pe, body, close)

        @block.scalar
        def _(act):
            def input_hi(b, p):
                act.wait_ge(turned, b + 1)
                after(act, q_made, done(KC, b, 0))
                act.activation(nT_hi[:, :, :], psum[:, 0:KC, :], ACT.Copy).then_inc(turned_hi, 1)

            def queries_hi(b, p):
                for m in range(KC):
                    act.wait_ge(q_made, done(KC, b, m + 1))
                    act.activation(qT_hi[:, p, m, :], psum[:, m, :], ACT.Identity, bias=kv["bq"][:, m:m + 1]).then_inc(q_hi, 1)

            def exps(b, pairs):
                if 0 in pairs:
                    after(act, av_made, done(TT, b, 0))
                for j in pairs:
                    act.wait_ge(st_made, done(NP, b, j + 1))
                    act.activation(probs[:, j, :], psum[:, 4 + j % 2, :], ACT.Exp, scale=DH ** -0.5).then_inc(exp_done, 1)

            def new_copy(b):
                act.wait_ge(new_turned, b + 1)
                after(act, lg_made, b)
                act.activation(newT[:, :, :], psum[:, 0:KC, :], ACT.Copy).then_inc(new_out, 1)

            def new_norm(b, p, half):
                act.wait_ge(shifted, b + 1)
                after(act, stored[p], half * (16 * STORES))
                after(act, new_turned, b)
                for t in range(TT):
                    act.activation(normed_new[:, p, t, :], x_new[:, p, t, :], ACT.Identity, bias=shift2[:, t:t + 1],
                                   scale=rstd[:, TT + t:TT + t + 1]).then_inc(norm_out, 1)

            def attention_hi(b):
                act.wait_ge(a_turned, b + 1)
                after(act, o_made, done(KC, b, 0))
                for c in range(KC):
                    act.activation(aT_hi[:, c, :], psum[:, c, :], ACT.Copy).then_inc(a_hi, 1)

            def body(b, p, half):
                exps(b, range(0, 2))
                if there(b + 1):
                    input_hi(b + 1, 1 - p)
                exps(b, range(2, 5))
                if there(b + 1):
                    queries_hi(b + 1, 1 - p)
                exps(b, range(5, 8))
                if there(b - 1):
                    new_norm(b - 1, 1 - p, half + p - 1)
                    new_copy(b - 1)
                attention_hi(b)

            def close(n):
                new_norm(n - 1, 1, B // 2 - 1)
                new_copy(n - 1)
            input_hi(0, 0)
            queries_hi(0, 0)
            batches(act, body, close)

        @block.vector
        def _(dve):
            dve.wait_ge(cleared, 3 if masked else 2)

            def mask_of(b, p):
                after(dve, st_made, done(NP, b - 1, 0))
                dve.tensor_scalar(mask_cur[0:SK, p, :], kv["mask"][:, :], kv["pad"][:, bass.ds(b, 1)], -BIG,
                                  ALU.mult, ALU.add).then_inc(mask_ready, 1)

            def layernorms(b, p, half, ahead_of_new=None, between=None):
                ahead, new = there(b + 2), there(b - 1)

                def before_input():
                    dve.wait_ge(x_loaded[p], half * 16 + 32)
                    after(dve, norm_in, done(TT, b + 2, 0))

                def before_new():
                    ahead_of_new()
                    dve.wait_ge(x_ready, done(KC, b - 1, KC))
                    after(dve, norm_out, done(TT, b - 1, 0))

                kinds = [(x_in[:, p, :, :], 0, before_input)] * ahead + [(x_new[:, 1 - p, :, :], 1, before_new)] * new
                xs, parts, before = zip(*kinds)
                steps = ln_steps(len(xs))
                layernorm_stats(dve, xs, parts, stats, mv, rstd, tmp, ln, ln_start(b), passed, before, between)
                dve.wait_ge(ln, ln_start(b) + steps)
                if new:
                    dve.scalar_tensor_tensor(shift2[:, :], mv[:, TT:, 0], -1.0, rstd[:, TT:], ALU.mult, ALU.mult).then_inc(shifted, 1)

            def input_norm(b, p, tiles=range(TT), col=0):
                if 0 in tiles:
                    after(dve, turned, b)
                for t in tiles:
                    dve.tensor_scalar(normed[:, t, :], x_in[:, p, t, :], mv[:, col + t, 0:1], rstd[:, col + t:col + t + 1],
                                      ALU.subtract, ALU.mult).then_inc(norm_in, 1)

            def input_lo(b):
                dve.wait_ge(turned_hi, b + 1)
                dve.tensor_tensor(nT_lo[:, :, :], psum[:, 0:KC, :], nT_hi[:, :, :].bitcast(F32), ALU.subtract).then_inc(turned_lo, 1)

            def queries_lo(b, p):
                for m in range(KC):
                    dve.wait_ge(q_hi, done(KC, b, m + 1))
                    dve.scalar_tensor_tensor(qT_lo[:, p, m, :], psum[:, m, :], kv["bq"][:, m:m + 1],
                                             qT_hi[:, p, m, :].bitcast(F32), ALU.add, ALU.subtract).then_inc(q_lo, 1)

            def maxima(b, tiles):
                if 0 in tiles:
                    after(dve, max_turned, b)
                for t in tiles:
                    for c in range(KC):
                        dve.wait_ge(s_made, done(TT * KC, b, t * KC + c + 1))
                        s = psum[:, 2 + c, :].rearrange("p (h k) -> p h k", k=SK)
                        dve.tensor_reduce(s_max[:, t, c * HH:(c + 1) * HH], s, AX.X, ALU.max).then_inc(s_taken, 1)

            def maxima_copy(b):
                dve.wait_ge(max_turned, b + 1)
                after(dve, st_made, done(NP, b, 0))
                dve.tensor_copy(maxT[0:H, :], psum[0:H, 3, :]).then_inc(max_ready, 1)

            def normalise(b, t):
                if t == 0:
                    after(dve, a_turned, b)
                dve.wait_ge(av_made, done(TT, b, t + 1))
                av = psum[:, 6 + t % 2, 0:H * VW].rearrange("p (h c) -> p h c", c=VW)
                dve.reciprocal(recip[:, t, :], av[:, :, DH]).then_inc(av_recip, 1)
                dve.wait_ge(av_recip, done(TT, b, t + 1))
                dve.tensor_tensor(att[:, t, :].rearrange("p (h c) -> p h c", c=DH), av[:, :, 0:DH],
                                  recip[:, t, :].unsqueeze(2).to_broadcast([P, H, DH]), ALU.mult).then_inc(av_taken, 1)

            def router_copy(b):
                dve.wait_ge(lg_made, b + 1)
                dve.tensor_copy(logits_all[:, bass.ds(b * TT, TT), :], psum[:, 4, 0:TT * PE_COLS].rearrange("p (t e) -> p t e", e=PE_COLS)[:, :, 0:8]).then_inc(lg_out, 1)

            def attention_lo(b):
                for c in range(KC):
                    dve.wait_ge(a_hi, done(KC, b, c + 1))
                    dve.tensor_tensor(aT_lo[:, c, :], psum[:, c, :], aT_hi[:, c, :].bitcast(F32), ALU.subtract).then_inc(a_lo, 1)

            def residual(b, p, half):
                dve.wait_ge(bias_done, b + 1)
                after(dve, stored[p], half * (16 * STORES))
                after(dve, norm_out, done(TT, b, 0))
                for n in range(KC):
                    dve.wait_ge(o_made, done(KC, b, n + 1))
                    tiles = slice(2 * n, 2 * n + 2)
                    dve.tensor_tensor(x_new[:, p, tiles, :], psum[:, 6 + n, :].rearrange("p (t d) -> p t d", d=D),
                                      x_bias[:, p, tiles, :], ALU.add).then_inc(x_ready, 1)

            def body(b, p, half):
                nxt = there(b + 1)
                if masked and nxt:
                    mask_of(b + 1, 1 - p)

                def ahead_of_new():
                    if there(b - 1):
                        residual(b - 1, 1 - p, half + p - 1)
                    if nxt:
                        input_lo(b + 1)

                def between():
                    if nxt:
                        queries_lo(b + 1, 1 - p)
                if there(b - 1):
                    layernorms(b, p, half, ahead_of_new, between)
                else:
                    layernorms(b, p, half)
                    ahead_of_new()
                    between()
                for t in range(TT):
                    if nxt:
                        maxima(b + 1, [t])
                    normalise(b, t)
                    if there(b + 2):
                        input_norm(b + 2, p, [t])
                if there(b - 1):
                    router_copy(b - 1)
                if nxt:
                    maxima_copy(b + 1)
                attention_lo(b)

            def close(n):
                layernorms(n, 0, B // 2, lambda: residual(n - 1, 1, B // 2 - 1))
                router_copy(n - 1)

            if masked:
                mask_of(0, 0)
            layernorm_stats(dve, [x_in[:, p, :, :] for p in range(2)], [0, 1], stats, mv, rstd, tmp, ln, 0, passed,
                            [lambda: dve.wait_ge(x_loaded[0], 16), lambda: dve.wait_ge(x_loaded[1], 16)])
            dve.wait_ge(ln, ln_steps(2))
            input_norm(0, 0)
            input_lo(0)
            input_norm(1, 1, col=TT)
            queries_lo(0, 0)
            maxima(0, range(TT))
            maxima_copy(0)
            batches(dve, body, close)


def alloc_layer(sc, masked):
    kv = {"masked": masked, "name": sc.phase}
    for n in ("kT_hi", "kT_lo"):
        kv[n] = sc.sb(n, [P, KC, B * SK], F32R)
    for n in ("wq_hi", "wq_lo", "wo_hi", "wo_lo"):
        kv[n] = sc.sb(n, [P, KC, D], F32R)
    kv["v"] = sc.sb("v_aug", [P, B, NP, 2 * VW])
    kv["bo"] = sc.sb("bo_bcast", [P, D])
    kv["bk"], kv["bq"] = sc.sb("bk_col", [P, KC]), sc.sb("bq_col", [P, KC])
    kv["wr"] = sc.sb("wr_sb", [P, KC, PE_COLS])
    if masked:
        kv["mask"], kv["pad"] = sc.sb("mask_keep", [SK, S], BF16), sc.sb("pad_keep", [SK, B])
    return kv


E = 8
TOPK = N_TOK // E
TOP_BIT = 29
LIST_BUFS = 3
SETUP_LAG = 2
SLOT = 32
F = 682
GROUPS_UP = 4
FC = -(-F // P)
FR = F - (FC - 1) * P
ROW = D + E
CHUNKS = P // E


def route_expert_choice(nc, const, psum, logits, br, rows_dram, idx, setup_of):
    with ExitStack() as ctx:
        sc = Scope(nc, ctx, "choice", const)
        bias = sc.sb("bias", [P, E])
        top, total = sc.sb("top", [P, NT]), sc.sb("total", [P, NT])
        score = sc.sb("score", [P, NT, E])
        by_e = sc.sb("by_e", [P, E, NT])
        turned = sc.sb("turned", [P, 4, P])
        hits = sc.sb("hits", [P, 4 * P], BF16)
        count = sc.sb("count", [P, 1])
        cand, drop = sc.sb("cand", [P, 1], I32), sc.sb("drop", [P, 1], I32)
        limits = sc.sb("limits", [P, P])
        same_e, before, ones = sc.sb("same_e", [P, E, CHUNKS]), sc.sb("before", [P, P], BF16), sc.sb("ones", [P, P], BF16)
        thresh = sc.sb("thresh", [P, P])
        above, equal, chosen = sc.sb("above", [P, E, NT], BF16), sc.sb("equal", [P, E, NT], BF16), sc.sb("chosen", [P, E, NT], BF16)
        keep_on = sc.sb("keep_on", [P, E, NT])
        run, rank, want = sc.sb("run", [P, E, NT]), sc.sb("rank", [P, E, NT]), sc.sb("want", [P, E])
        pos, part = sc.sb("pos", [P, E, NT], I32), sc.sb("part", [P, E, NT], I32)
        high, low = sc.sb("high", [P, E, NT]), sc.sb("low", [P, E, NT])
        slot_no, tile_no = sc.sb("slot_no", [P, SLOT]), sc.sb("tile_no", [P, NT])
        lane_no = sc.sb("lane_no", [P, 1])
        one_high = sc.sb("one_high", [P, LIST_BUFS, NT, SLOT], BF16)
        one_low = sc.sb("one_low", [P, LIST_BUFS, NT, SLOT], BF16)
        coded = sc.sb("coded", [P, LIST_BUFS, NT, 2, SLOT], BF16)
        listed = sc.sb("listed", [SLOT, E, 2, SLOT])

        setup = setup_of(sc)
        SETUP_ITEMS = 2 * KC + B
        made = sc.sem("made")
        bias_loaded, scores_stored = sc.sem("bias_loaded"), sc.sem("scores_stored")
        limits_turned = sc.sem("limits_turned")
        step, exps, flagged = sc.sem("step"), sc.sem("exps"), sc.sem("flagged")
        t_made, counted = sc.sem("t_made"), sc.sem("counted")
        hit, decided = sc.sem("hit"), sc.sem("decided")
        found_all = sc.sem("found_all")
        high_made, low_made, lane_made, tile_made, list_made = (sc.sem(n) for n in ("high_made", "low_made", "lane_made", "tile_made", "list_made"))
        block = ctx.enter_context(nc.Block())

        @block.sync
        def _(sp):
            sp.dma_start(bias[:, :], br.partition_broadcast(P)).then_inc(bias_loaded, 16)
            setup["load"](sp)
            sp.wait_ge(step, 6)
            sp.dma_start(rows_dram.rearrange("(t p) r -> p t r", p=P)[:, :, D:ROW], score[:, :, :]).then_inc(scores_stored, 16)
            sp.wait_ge(scores_stored, 16)

        @block.gpsimd
        def _(pool):
            pool.memset(same_e[:, :, :], 1.0).then_inc(made, 1)
            pool.memset(before[:, :], 1.0).then_inc(made, 1)
            pool.memset(ones[:, :], 1.0).then_inc(made, 1)
            pool.memset(keep_on[:, :, :], 1.0).then_inc(made, 1)
            pool.iota(slot_no[:, :], pattern=[[1, SLOT]], base=0, channel_multiplier=0, allow_small_or_imprecise_dtypes=True).then_inc(made, 1)
            pool.iota(tile_no[:, :], pattern=[[1, NT]], base=0, channel_multiplier=0, allow_small_or_imprecise_dtypes=True).then_inc(made, 1)
            pool.iota(lane_no[:, :], pattern=[[0, 1]], base=0, channel_multiplier=1, allow_small_or_imprecise_dtypes=True).then_inc(made, 1)
            pool.wait_ge(made, 7)
            pool.memset(keep_on[:, :, 0:1], 0.0).then_inc(made, 1)
            pool.affine_select(out=before[:, :], in_=before[:, :], compare_op=ALU.is_gt, fill=0.0, base=0,
                               pattern=[[1, P]], channel_multiplier=-1).then_inc(made, 1)
            pool.affine_select(out=same_e[:, :, :], in_=same_e[:, :, :], compare_op=ALU.is_ge, fill=0.0, base=0,
                               pattern=[[-CHUNKS, E], [0, CHUNKS]], channel_multiplier=1).then_inc(made, 1)
            pool.wait_ge(made, 10)
            pool.affine_select(out=same_e[:, :, :], in_=same_e[:, :, :], compare_op=ALU.is_ge, fill=0.0, base=CHUNKS - 1,
                               pattern=[[CHUNKS, E], [0, CHUNKS]], channel_multiplier=-1).then_inc(made, 1)
            setup["clear"](pool)
            tiles = tile_no[:, :].unsqueeze(2).to_broadcast([P, NT, SLOT])
            for e in range(E):
                pool.wait_ge(low_made, e + 1)
                if e >= LIST_BUFS:
                    pool.wait_ge(list_made, e - LIST_BUFS + 1)
                pool.tensor_tensor(coded[:, e % LIST_BUFS, :, 1, :], one_low[:, e % LIST_BUFS, :, :], tiles, ALU.mult).then_inc(tile_made, 1)

        @block.scalar
        def _(act):
            act.wait_ge(step, 3)
            act.activation(score[:, :, :], score[:, :, :], ACT.Exp).then_inc(exps, 1)
            setup["context_out"](act)
            setup["high_parts"](act)
            for e in range(E):
                act.wait_ge(low_made, e + 1)
                if e >= LIST_BUFS:
                    act.wait_ge(list_made, e - LIST_BUFS + 1)
                act.activation(coded[:, e % LIST_BUFS, :, 0, :], one_low[:, e % LIST_BUFS, :, :], ACT.Copy, scale=lane_no[:, 0:1]).then_inc(lane_made, 1)

        @block.tensor
        def _(pe):
            setup["turn_context"](pe)
            pe.wait_ge(step, 7)
            pe.wait_ge(setup["turned_twice"], 2 * KC)
            for r in range(4):
                t = pe.transpose(psum[:, 0, r * P:(r + 1) * P], by_e[:, :, r::4], const["ident"][:, :])
            t.then_inc(t_made, 1)
            pe.wait_ge(made, 11)
            for i in range(TOP_BIT + 1):
                pe.wait_ge(hit, i + 1)
                pe.matmul(psum[:, 1, 0:1], same_e[:, :, :], count[:, :], start=True, stop=True).then_inc(counted, 1)
                if i < 2 * KC:
                    setup["keys"](pe, i)
                elif i < SETUP_ITEMS:
                    setup["values"](pe, i - 2 * KC)
            pe.wait_ge(found_all, 1)
            pe.transpose(psum[:, 1, 0:P], limits[:, :], const["ident"][:, :]).then_inc(limits_turned, 1)
            pe.wait_ge(setup["v_out"], 2 * B)
            for n, x in enumerate((above, equal, chosen)):
                pe.wait_ge(flagged, n + 1)
                pe.matmul(psum[:, 2 + 2 * n, :], before[:, :], x[:, :, :], start=True, stop=True)
                pe.matmul(psum[:, 3 + 2 * n if n < 2 else 0, :], ones[:, :], x[:, :, :], start=True, stop=True).then_inc(counted, 1)
            for e in range(E):
                pe.wait_ge(high_made, e + 1)
                pe.wait_ge(lane_made, e + 1)
                pe.wait_ge(tile_made, e + 1)
                for t in range(NT):
                    m = pe.matmul(psum[0:SLOT, 1, e * 2 * SLOT:(e + 1) * 2 * SLOT], one_high[:, e % LIST_BUFS, t, :],
                                  coded[:, e % LIST_BUFS, t, :, :], start=(t == 0), stop=(t == NT - 1))
                m.then_inc(list_made, 1)

        @block.vector
        def _(dve):
            n = 0

            def then(instruction):
                nonlocal n
                instruction.then_inc(step, 1)
                n += 1
                dve.wait_ge(step, n)

            def over_e(x):
                return x.unsqueeze(2).to_broadcast([P, NT, E])

            def over_t(x):
                return x.unsqueeze(2).to_broadcast([P, E, NT])

            dve.wait_ge(bias_loaded, 16)
            then(dve.tensor_tensor(score[:, :, :], logits[:, :, :], bias[:, :].unsqueeze(1).to_broadcast([P, NT, E]), ALU.add))
            then(dve.tensor_reduce(top[:, :], score[:, :, :], AX.X, ALU.max))
            then(dve.tensor_tensor(score[:, :, :], score[:, :, :], over_e(top[:, :]), ALU.subtract))
            dve.wait_ge(exps, 1)
            then(dve.tensor_reduce(total[:, :], score[:, :, :], AX.X, ALU.add))
            then(dve.reciprocal(total[:, :], total[:, :]))
            then(dve.tensor_tensor(score[:, :, :], score[:, :, :], over_e(total[:, :]), ALU.mult))
            then(dve.tensor_copy(by_e[:, :, :], score[:, :, :].rearrange("p t e -> p e t")))
            then(dve.memset(cand[:, :], 1 << TOP_BIT))
            setup["context_twice"](dve)
            dve.wait_ge(t_made, 1)
            then(dve.tensor_copy(turned[:, :, :], psum[:, 0, :].rearrange("p (r q) -> p r q", r=4)))
            for i in range(TOP_BIT + 1):
                dve.tensor_scalar(hits[:, :], turned[:, :, :].rearrange("p r q -> p (r q)"), cand[:, :].bitcast(F32), 0.0,
                                  ALU.is_ge, ALU.add, accum_out=count[:, :]).then_inc(hit, 1)
                item = i - SETUP_LAG
                if 0 <= item < 2 * KC:
                    setup["keys_out"](dve, item)
                elif 0 <= item < SETUP_ITEMS:
                    setup["values_out"](dve, item - 2 * KC)
                dve.wait_ge(counted, i + 1)
                tried = 1 << (TOP_BIT - i)
                dve.tensor_scalar(drop[:, :], psum[:, 1, 0:1], float(TOPK), float(tried), ALU.is_lt, ALU.mult).then_inc(decided, 1)
                dve.wait_ge(decided, i * 2 + 1)
                dve.scalar_tensor_tensor(cand[:, :], cand[:, :], tried >> 1, drop[:, :], ALU.bitwise_or, ALU.bitwise_xor).then_inc(decided, 1)
                dve.wait_ge(decided, i * 2 + 2)
            dve.tensor_copy(limits[:, :], cand[:, :].bitcast(F32).to_broadcast([P, P])).then_inc(found_all, 1)
            setup["rest"](dve)
            dve.wait_ge(limits_turned, 1)
            then(dve.tensor_copy(thresh[:, :], psum[:, 1, 0:P]))
            dve.wait_ge(made, 11)
            limit = over_t(thresh[:, 0::CHUNKS])
            dve.tensor_tensor(above[:, :, :], by_e[:, :, :], limit, ALU.is_gt).then_inc(flagged, 1)
            dve.tensor_tensor(equal[:, :, :], by_e[:, :, :], limit, ALU.is_equal).then_inc(flagged, 1)
            dve.wait_ge(flagged, 2)
            dve.wait_ge(counted, TOP_BIT + 2)

            def flat(bank):
                return psum[:, bank, :].rearrange("p (e t) -> p e t", e=E)

            def ranks(within, totals):
                then(dve.tensor_copy(rank[:, :, :], flat(totals)))
                then(dve.tensor_tensor_scan(run[:, :, :].rearrange("p e t -> p (e t)"), keep_on[:, :, :].rearrange("p e t -> p (e t)"),
                                            rank[:, :, :].rearrange("p e t -> p (e t)"), 0.0, ALU.mult, ALU.add))
                then(dve.tensor_tensor(run[:, :, :], run[:, :, :], rank[:, :, :], ALU.subtract))
                then(dve.tensor_tensor(rank[:, :, :], flat(within), run[:, :, :], ALU.add))

            then(dve.tensor_reduce(want[:, :], flat(3), AX.X, ALU.add))
            then(dve.tensor_scalar(want[:, :], want[:, :], -1.0, float(TOPK), ALU.mult, ALU.add))
            dve.wait_ge(counted, TOP_BIT + 3)
            ranks(4, 5)
            then(dve.tensor_tensor(rank[:, :, :], rank[:, :, :], over_t(want[:, :]), ALU.is_lt))
            then(dve.tensor_tensor(rank[:, :, :], rank[:, :, :], equal[:, :, :], ALU.mult))
            dve.tensor_tensor(chosen[:, :, :], rank[:, :, :], above[:, :, :], ALU.add).then_inc(flagged, 1)
            dve.wait_ge(flagged, 3)
            dve.wait_ge(counted, TOP_BIT + 4)
            ranks(6, 0)
            then(dve.tensor_copy(pos[:, :, :], rank[:, :, :]))
            then(dve.tensor_scalar(part[:, :, :], pos[:, :, :], 5, None, ALU.logical_shift_right))
            then(dve.scalar_tensor_tensor(high[:, :, :], part[:, :, :], 1.0, chosen[:, :, :], ALU.add, ALU.mult))
            then(dve.tensor_scalar(high[:, :, :], high[:, :, :], -1.0, None, ALU.add))
            then(dve.tensor_scalar(part[:, :, :], pos[:, :, :], SLOT - 1, None, ALU.bitwise_and))
            then(dve.tensor_copy(low[:, :, :], part[:, :, :]))
            numbers = slot_no[:, :].unsqueeze(1).to_broadcast([P, NT, SLOT])
            for e in range(E):
                if e >= LIST_BUFS:
                    dve.wait_ge(list_made, e - LIST_BUFS + 1)
                dve.tensor_tensor(one_low[:, e % LIST_BUFS, :, :], low[:, e, :].unsqueeze(2).to_broadcast([P, NT, SLOT]), numbers,
                                  ALU.is_equal).then_inc(low_made, 1)
                dve.tensor_tensor(one_high[:, e % LIST_BUFS, :, :], high[:, e, :].unsqueeze(2).to_broadcast([P, NT, SLOT]), numbers,
                                  ALU.is_equal).then_inc(high_made, 1)
            dve.wait_ge(list_made, E)
            then(dve.tensor_copy(listed[:, :, :, :], psum[0:SLOT, 1, :].rearrange("s (e c l) -> s e c l", e=E, c=2)))
            for q in range(P // SLOT):
                cols = slice(q * 8, (q + 1) * 8)
                then(dve.scalar_tensor_tensor(idx[q * SLOT:(q + 1) * SLOT, :, :], listed[:, :, 1, cols], float(P), listed[:, :, 0, cols],
                                              ALU.mult, ALU.add))


FP = FC * P
BIAS_ROW = 64
assert FR <= BIAS_ROW
EP = E // GROUPS_UP
HALF = TOPK // 2
HT = HALF // P
GJ = 2 * EP
PAIRS = FC // 2


def expert_choice_mixture(nc, const, psum, idx, x, x_normed, w_up, b_up, w_down):
    with ExitStack() as ctx:
        sc = Scope(nc, ctx, "moe", const)
        rows = sc.sb("rows", [P, GJ, HT, ROW])
        gates = sc.sb("gates", [P, GJ, HT])
        idx_get, idx_add = sc.sb("idx_get", [P, EP, 2 * HT], I32), sc.sb("idx_add", [P, EP, 2 * HT], I32)
        wu, wd = sc.sb("wu", [P, KC, FP]), sc.sb("wd", [P, FC, D])
        wu_hi, wu_lo = sc.sb("wu_hi", [P, KC, FP], F32R), sc.sb("wu_lo", [P, KC, FP], F32R)
        wd_hi, wd_lo = sc.sb("wd_hi", [P, EP, FC, D], F32R), sc.sb("wd_lo", [P, EP, FC, D], F32R)
        bu, bu_in = sc.sb("bu", [P, FC]), sc.sb("bu_in", [P, FC])
        xT_hi, xT_lo = sc.sb("xT_hi", [P, 2, KC, HALF], F32R), sc.sb("xT_lo", [P, 2, KC, HALF], F32R)
        mid = sc.sb("mid", [P, FC, HALF])
        mid_hi, mid_lo = sc.sb("mid_hi", [P, 2, FC, HALF], F32R), sc.sb("mid_lo", [P, 2, FC, HALF], F32R)
        y = sc.sb("y", [P, 2, HT, D])

        gates_copied = sc.sem("gates_copied")
        rows_in = [sc.sem(f"rows_in{j}") for j in range(GJ)]
        added = [sc.sem(f"added{p}") for p in range(2)]
        get_copied, add_copied = sc.sem("get_copied"), sc.sem("add_copied")
        wu_in, wd_in, wu_hi_made, wd_hi_made = sc.sem("wu_in"), sc.sem("wd_in"), sc.sem("wu_hi_made"), sc.sem("wd_hi_made")
        wu_ready, wd_ready = sc.sem("wu_ready"), sc.sem("wd_ready")
        turned, xT_hi_made, xT_ready = sc.sem("turned"), sc.sem("xT_hi_made"), sc.sem("xT_ready")
        up_made, silu_made = sc.sem("up_made"), sc.sem("silu_made")
        hi_made, lo_made = sc.sem("hi_made"), sc.sem("lo_made")
        down_made = [sc.sem(f"down_made{p}") for p in range(2)]
        y_made = sc.sem("y_made")
        cleared, passed, bu_copied = sc.sem("cleared"), sc.sem("passed"), sc.sem("bu_copied")
        block = ctx.enter_context(nc.Block())
        LAST = GROUPS_UP - 1

        def iterations(eng, body):
            with eng.Fori(0, LAST) as q:
                body(q, False)
            body(LAST, True)

        @block.sync
        def _(sp):
            def load_up(q):
                after(sp, wu_ready, q)
                sp.dma_start(wu[:, :, :], w_up[bass.ds(q, 1), :, :].rearrange("o (c p) f -> p (o c) f", p=P)).then_inc(wu_in, 16)
                sp.dma_start(bu_in[:, :], b_up[bass.ds(q, 1), :, :].rearrange("o p c -> p (o c)")).then_inc(wu_in, 16)

            def load_down(e):
                after(sp, wd_ready, e)
                sp.dma_start(wd[:, :, :], w_down[bass.ds(e, 1), :, :].rearrange("o (c p) d -> p (o c) d", p=P)).then_inc(wd_in, 16)
            with sp.Fori(0, GROUPS_UP) as q:
                load_up(q)
                for i in range(EP):
                    load_down(q * EP + i)

        @block.gpsimd
        def _(pool):
            def pass_wait():
                pool.sem_inc(passed, 1)

            def gather(e, i, h):
                if h == 0:
                    if not (isinstance(e, int) and e < EP):
                        for k in range(2):
                            pool.wait_ge(rows_in[i * 2 + k], (e - i) * (16 * HT // EP))
                        pass_wait()
                    pool.tensor_copy(idx_get[:, i, :], idx[:, bass.ds(e, 1), :].rearrange("p o r -> p (o r)")).then_inc(get_copied, 1)
                    pool.wait_ge(get_copied, e + 1)
                after(pool, turned, e * 2 + h - 2)
                after(pool, gates_copied, e * 2 + h - 2)
                pass_wait()
                for t in range(HT):
                    at = bass.IndirectOffsetOnAxis(ap=idx_get[:, i, h * HT + t:h * HT + t + 1], axis=0)
                    pool.indirect_dma_start(rows[:, i * 2 + h, t, :], None, x_normed, at, compute_op=ALU.bypass).then_inc(rows_in[i * 2 + h], 16)

            def add(e, i, h):
                for s in range(2):
                    pool.wait_ge(added[s], e * (16 * HT))
                if h == 0:
                    pass_wait()
                    pool.tensor_copy(idx_add[:, i, :], idx[:, bass.ds(e, 1), :].rearrange("p o r -> p (o r)")).then_inc(add_copied, 1)
                    pool.wait_ge(add_copied, e + 1)
                for t in range(HT):
                    pool.wait_ge(y_made, done(HT, e * 2 + h, t + 1))
                    pass_wait()
                    at = bass.IndirectOffsetOnAxis(ap=idx_add[:, i, h * HT + t:h * HT + t + 1], axis=0)
                    pool.indirect_dma_start(x, at, y[:, h, t, :], None, compute_op=ALU.add).then_inc(added[h], 16)

            def body(q, last):
                e = q * EP
                for h in range(2):
                    gather(e + 1, 1, h)
                for h in range(2):
                    if not last:
                        gather(e + EP, 0, h)
                    add(e, 0, h)
                for h in range(2):
                    add(e + 1, 1, h)

            for h in range(2):
                gather(0, 0, h)
            for p in range(2):
                pool.memset(mid_lo[BIAS_ROW:, p, FC - 1, :].bitcast(F32), 0.0).then_inc(cleared, 1)
                pool.memset(mid_hi[BIAS_ROW:, p, FC - 1, :].bitcast(F32), 0.0).then_inc(cleared, 1)
            pool.wait_ge(cleared, 4)
            for p in range(2):
                pool.memset(mid_hi[BIAS_ROW:BIAS_ROW + 1, p, FC - 1, :].bitcast(F32), 1.0).then_inc(cleared, 1)
            pool.wait_ge(cleared, 6)
            iterations(pool, body)
            for s in range(2):
                pool.wait_ge(added[s], E * 16 * HT)

        @block.tensor
        def _(pe):
            def turn(g, j, q):
                pe.wait_ge(rows_in[j], q * (16 * HT) + 16 * HT)
                after(pe, xT_ready, g)
                for c in range(KC):
                    for t in range(HT):
                        m = pe.transpose(psum[:, c, t * P:(t + 1) * P], rows[:, j, t, c * P:(c + 1) * P], const["ident"][:, :])
                m.then_inc(turned, 1)

            def up(g, j, turn_next):
                p = j % 2
                pe.wait_ge(xT_ready, g + 1)
                for f in range(FC):
                    if f == 2 and turn_next:
                        turn_next()
                    if f < 2:
                        pe.wait_ge(silu_made, g * FC - (1 if f == 0 and j else 0))
                    if f >= 4:
                        pe.wait_ge(silu_made, done(FC, g, f - 3))
                    cols = slice(f * P, (f + 1) * P)
                    for c in range(KC):
                        m = three_passes(pe, psum[:, 2 + f % 4, :], wu_hi[:, c, cols], wu_lo[:, c, cols],
                                         xT_hi[:, p, c, :], xT_lo[:, p, c, :], c == 0, c == KC - 1)
                    m.then_inc(up_made, 1)

            def down(g, j):
                p, i = j % 2, j // 2
                pe.wait_ge(lo_made, done(PAIRS + 1, g, PAIRS + 1))
                for t in range(HT):
                    if t % 2 == 0:
                        pe.wait_ge(y_made, g * HT - (2 if t == 0 and j else 0))
                    rows_t = slice(t * P, (t + 1) * P)
                    for f in range(FC):
                        m = three_passes(pe, psum[:, 6 + t // 2, (t % 2) * D:(t % 2 + 1) * D], mid_hi[:, p, f, rows_t],
                                         mid_lo[:, p, f, rows_t], wd_hi[:, i, f, :], wd_lo[:, i, f, :], f == 0, f == FC - 1)
                    m.then_inc(down_made[p], 1)

            def body(q, last):
                g = q * GJ
                pe.wait_ge(wu_ready, q + 1)
                for j in range(GJ):
                    if j < GJ - 1:
                        up(g + j, j, lambda: turn(g + j + 1, j + 1, q))
                    else:
                        up(g + j, j, None if last else lambda: turn(g + GJ, 0, q + 1))
                    if j >= 1:
                        pe.wait_ge(wd_ready, q * EP + (j - 1) // 2 + 1)
                        down(g + j - 1, j - 1)
                down(g + GJ - 1, GJ - 1)

            pe.wait_ge(cleared, 6)
            turn(0, 0, 0)
            iterations(pe, body)

        @block.scalar
        def _(act):
            def up_weights(q):
                act.wait_ge(wu_in, q * 32 + 32)
                act.activation(wu_hi[:, :, :], wu[:, :, :], ACT.Copy).then_inc(wu_hi_made, 1)

            def down_weights(e, i):
                act.wait_ge(wd_in, e * 16 + 16)
                for f in range(0, FC, 3):
                    act.activation(wd_hi[:, i, f:f + 3, :], wd[:, f:f + 3, :], ACT.Copy).then_inc(wd_hi_made, 1)

            def hidden(g, p, u):
                act.wait_ge(lo_made, g * (PAIRS + 1))
                for f in range(FC):
                    act.wait_ge(up_made, done(FC, g, f + 1))
                    valid = slice(0, P if f < FC - 1 else BIAS_ROW)
                    act.activation(mid[valid, f, :], psum[valid, 2 + f % 4, :], ACT.Silu, bias=bu[valid, f:f + 1]).then_inc(silu_made, 1)
                    if f % 2:
                        if f == 1:
                            act.wait_ge(down_made[p], u * HT)
                        act.wait_ge(silu_made, done(FC, g, f + 1))
                        if f < FC - 1:
                            act.activation(mid_hi[:, p, f - 1:f + 1, :], mid[:, f - 1:f + 1, :], ACT.Copy).then_inc(hi_made, 1)
                        else:
                            act.activation(mid_hi[:, p, f - 1, :], mid[:, f - 1, :], ACT.Copy).then_inc(hi_made, 1)
                            act.activation(mid_hi[valid, p, f, :], mid[valid, f, :], ACT.Copy).then_inc(hi_made, 1)

            def body(q, last):
                act.wait_ge(wu_ready, q + 1)
                for j in range(GJ):
                    hidden(q * GJ + j, j % 2, q * EP + j // 2)
                if not last:
                    up_weights(q + 1)
                    for i in range(EP):
                        act.wait_ge(down_made[1], q * (EP * HT) + (i + 1) * HT)
                        down_weights(q * EP + EP + i, i)

            up_weights(0)
            down_weights(0, 0)
            down_weights(1, 1)
            iterations(act, body)

        @block.vector
        def _(dve):
            def rows_lo(g, j, e, q):
                p = j % 2
                dve.wait_ge(rows_in[j], q * (16 * HT) + 16 * HT)
                dve.tensor_copy(gates[:, j, :], rows[:, j, :, bass.ds(e + D, 1)].rearrange("p t o -> p (t o)")).then_inc(gates_copied, 1)
                dve.wait_ge(turned, g + 1)
                dve.tensor_copy(xT_hi[:, p, :, :], psum[:, 0:KC, :]).then_inc(xT_hi_made, 1)
                dve.wait_ge(xT_hi_made, g + 1)
                dve.tensor_tensor(xT_lo[:, p, :, :], psum[:, 0:KC, :], xT_hi[:, p, :, :].bitcast(F32), ALU.subtract).then_inc(xT_ready, 1)

            def up_weights(q):
                dve.wait_ge(wu_in, q * 32 + 32)
                dve.tensor_copy(bu[:, :], bu_in[:, :]).then_inc(bu_copied, 1)
                dve.wait_ge(wu_hi_made, q + 1)
                dve.wait_ge(bu_copied, q + 1)
                dve.tensor_tensor(wu_lo[:, :, :], wu[:, :, :], wu_hi[:, :, :].bitcast(F32), ALU.subtract).then_inc(wu_ready, 1)

            def down_weights(e, i):
                dve.wait_ge(wd_hi_made, e * 2 + 2)
                dve.tensor_tensor(wd_lo[:, i, :, :], wd[:, :, :], wd_hi[:, i, :, :].bitcast(F32), ALU.subtract).then_inc(wd_ready, 1)

            def hidden_lo(g, p, u, rows_next):
                for k in range(PAIRS):
                    if k == 1 and rows_next:
                        rows_next()
                    if k == 0:
                        dve.wait_ge(down_made[p], u * HT)
                    if k < PAIRS - 1:
                        dve.wait_ge(hi_made, done(PAIRS + 1, g, k + 1))
                        dve.tensor_tensor(mid_lo[:, p, 2 * k:2 * k + 2, :], mid[:, 2 * k:2 * k + 2, :],
                                          mid_hi[:, p, 2 * k:2 * k + 2, :].bitcast(F32), ALU.subtract).then_inc(lo_made, 1)
                    else:
                        dve.wait_ge(hi_made, done(PAIRS + 1, g, PAIRS + 1))
                        f, valid = FC - 1, slice(0, BIAS_ROW)
                        dve.tensor_tensor(mid_lo[:, p, f - 1, :], mid[:, f - 1, :], mid_hi[:, p, f - 1, :].bitcast(F32), ALU.subtract).then_inc(lo_made, 1)
                        dve.tensor_tensor(mid_lo[valid, p, f, :], mid[valid, f, :], mid_hi[valid, p, f, :].bitcast(F32), ALU.subtract).then_inc(lo_made, 1)

            def outputs(g, p, j, u):
                dve.wait_ge(gates_copied, g + 1)
                dve.wait_ge(added[p], u * (16 * HT))
                for t in range(HT):
                    dve.wait_ge(down_made[p], done(HT, u, t // 2 * 2 + 2))
                    dve.tensor_scalar(y[:, p, t, :], psum[:, 6 + t // 2, (t % 2) * D:(t % 2 + 1) * D],
                                      gates[:, j, t:t + 1], None, ALU.mult).then_inc(y_made, 1)

            def body(q, last):
                def out(j):
                    outputs(q * GJ + j, j % 2, j, q * EP + j // 2)
                for j in range(GJ):
                    if j < GJ - 1:
                        hidden_lo(q * GJ + j, j % 2, q * EP + j // 2, lambda: rows_lo(q * GJ + j + 1, j + 1, q * EP + (j + 1) // 2, q))
                    else:
                        hidden_lo(q * GJ + j, j % 2, q * EP + j // 2,
                                  None if last else lambda: rows_lo(q * GJ + GJ, 0, q * EP + EP, q + 1))
                    if j >= 1:
                        out(j - 1)
                if not last:
                    dve.wait_ge(up_made, (q + 1) * (GJ * FC))
                    dve.wait_ge(silu_made, (q + 1) * (GJ * FC))
                    up_weights(q + 1)
                    dve.wait_ge(down_made[1], q * (EP * HT) + HT)
                    down_weights(q * EP + EP, 0)
                out(GJ - 1)
                if not last:
                    down_weights(q * EP + EP + 1, 1)

            up_weights(0)
            down_weights(0, 0)
            rows_lo(0, 0, 0, 0)
            down_weights(1, 1)
            iterations(dve, body)


GOLDEN_CENTER = 1.0 / math.e
GOLDEN_LOWER = 0.5 - math.log(4.0 / 3.0)
GOLDEN_UPPER = 0.5
I_FF = 256
IC = I_FF // P
TINY = 1e-8


ZONE_STEPS = 36


def zone_router(sc, logits, temperature, weight):
    temp, order = sc.sb("temp", [P, 1]), sc.sb("order", [P, E])
    inh, dist, zone, near = (sc.sb(n, [P, NT, E]) for n in ("inh", "dist", "zone", "near"))
    key, hit, picked, flag = (sc.sb(n, [P, NT, E]) for n in ("key", "hit", "picked", "flag"))
    best, total, lone, keep = (sc.sb(n, [P, NT]) for n in ("best", "total", "lone", "keep"))
    temp_loaded, order_made, step = sc.sem("temp_loaded"), sc.sem("order_made"), sc.sem("step")
    DIST_READY = 7
    exps, divided = sc.sem("exps"), sc.sem("divided")

    def load_temperature(sp):
        sp.dma_start(temp[:, :], temperature.partition_broadcast(P)).then_inc(temp_loaded, 16)

    def expert_order(pool):
        pool.iota(order[:, :], pattern=[[-1, E]], base=E, channel_multiplier=0, allow_small_or_imprecise_dtypes=True).then_inc(order_made, 1)

    def sigmoid_exp(act):
        act.wait_ge(divided, 1)
        act.activation(inh[:, :, :], inh[:, :, :], ACT.Exp, scale=-1.0).then_inc(exps, 1)

    def distance_exps(act):
        act.wait_ge(step, DIST_READY)
        act.activation(weight[:, :, :], dist[:, :, :], ACT.Exp, scale=-1.0 / 0.1).then_inc(exps, 1)
        act.activation(near[:, :, :], dist[:, :, :], ACT.Exp, scale=-1.0 / 0.3).then_inc(exps, 1)

    def weights(dve, midway):
        n = 0

        def then(instruction):
            nonlocal n
            instruction.then_inc(step, 1)
            n += 1
            dve.wait_ge(step, n)

        def over_e(x):
            return x.unsqueeze(2).to_broadcast([P, NT, E])

        keys = order[:, :].unsqueeze(1).to_broadcast([P, NT, E])
        dve.wait_ge(temp_loaded, 16)
        then(dve.reciprocal(temp[:, :], temp[:, :]))
        dve.tensor_scalar(inh[:, :, :], logits[:, :, :], temp[:, 0:1], None, ALU.mult).then_inc(divided, 1)
        dve.wait_ge(exps, 1)
        then(dve.tensor_scalar(inh[:, :, :], inh[:, :, :], 1.0, None, ALU.add))
        then(dve.reciprocal(inh[:, :, :], inh[:, :, :]))
        then(dve.tensor_scalar(zone[:, :, :], inh[:, :, :], GOLDEN_LOWER, None, ALU.is_ge))
        then(dve.scalar_tensor_tensor(zone[:, :, :], inh[:, :, :], GOLDEN_UPPER, zone[:, :, :], ALU.is_le, ALU.mult))
        then(dve.tensor_scalar(inh[:, :, :], inh[:, :, :], GOLDEN_CENTER, None, ALU.subtract))
        then(dve.scalar_tensor_tensor(dist[:, :, :], inh[:, :, :], -1.0, inh[:, :, :], ALU.mult, ALU.max))
        assert n == DIST_READY
        dve.wait_ge(exps, 2)
        then(dve.tensor_tensor(weight[:, :, :], weight[:, :, :], zone[:, :, :], ALU.mult))
        then(dve.tensor_reduce(total[:, :], weight[:, :, :], AX.X, ALU.add))
        then(dve.tensor_scalar(lone[:, :], total[:, :], TINY, None, ALU.is_lt))
        then(dve.tensor_scalar(keep[:, :], lone[:, :], -1.0, 1.0, ALU.mult, ALU.add))
        dve.wait_ge(exps, 3)
        dve.wait_ge(order_made, 1)
        left = near
        for k in range(2):
            then(dve.tensor_reduce(best[:, :], left[:, :, :], AX.X, ALU.max))
            then(dve.tensor_tensor(key[:, :, :], left[:, :, :], over_e(best[:, :]), ALU.is_ge))
            then(dve.tensor_tensor(key[:, :, :], key[:, :, :], keys, ALU.mult))
            then(dve.tensor_reduce(best[:, :], key[:, :, :], AX.X, ALU.max))
            then(dve.tensor_tensor(flag[:, :, :], key[:, :, :], over_e(best[:, :]), ALU.is_equal))
            if k == 0:
                then(dve.scalar_tensor_tensor(hit[:, :, :], flag[:, :, :], -2.0, near[:, :, :], ALU.mult, ALU.add))
                then(dve.tensor_copy(picked[:, :, :], flag[:, :, :]))
                left = hit
                midway()
        then(dve.tensor_tensor(picked[:, :, :], picked[:, :, :], flag[:, :, :], ALU.add))
        then(dve.tensor_tensor(near[:, :, :], near[:, :, :], picked[:, :, :], ALU.mult))
        then(dve.tensor_reduce(total[:, :], near[:, :, :], AX.X, ALU.add))
        then(dve.tensor_scalar(total[:, :], total[:, :], TINY, None, ALU.max))
        then(dve.reciprocal(total[:, :], total[:, :]))
        then(dve.tensor_tensor(total[:, :], total[:, :], lone[:, :], ALU.mult))
        then(dve.tensor_tensor(near[:, :, :], near[:, :, :], over_e(total[:, :]), ALU.mult))
        then(dve.tensor_tensor(weight[:, :, :], weight[:, :, :], over_e(keep[:, :]), ALU.mult))
        then(dve.tensor_tensor(weight[:, :, :], weight[:, :, :], near[:, :, :], ALU.add))
        then(dve.tensor_reduce(total[:, :], weight[:, :, :], AX.X, ALU.add))
        then(dve.tensor_scalar(total[:, :], total[:, :], TINY, None, ALU.max))
        then(dve.reciprocal(total[:, :], total[:, :]))
        then(dve.tensor_tensor(weight[:, :, :], weight[:, :, :], over_e(total[:, :]), ALU.mult))
        assert n == ZONE_STEPS

    return load_temperature, expert_order, sigmoid_exp, distance_exps, weights, step


def zone_mixture(nc, const, psum, logits, temperature, x, x_normed, w_gate, w_up, w_down, out):
    RAW = 6
    with ExitStack() as ctx:
        sc = Scope(nc, ctx, "zmix", const)
        weight = sc.sb("weight", [P, NT, E])
        load_temperature, expert_order, sigmoid_exp, distance_exps, weights, weight_steps = zone_router(sc, logits, temperature, weight)
        wg_hi, wg_lo = sc.sb("wg_hi", [P, E, KC, I_FF], F32R), sc.sb("wg_lo", [P, E, KC, I_FF], F32R)
        wu_hi, wu_lo = sc.sb("wu_hi", [P, E, KC, I_FF], F32R), sc.sb("wu_lo", [P, E, KC, I_FF], F32R)
        wd_hi, wd_lo = sc.sb("wd_hi", [P, E, IC, D], F32R), sc.sb("wd_lo", [P, E, IC, D], F32R)
        raw = sc.sb("raw", [P, RAW, 512])
        acc = sc.sb("acc", [P, 2, TT, D])
        xn = sc.sb("xn", [P, 2, TT, D])
        xT_hi, xT_lo = sc.sb("xT_hi", [P, 2, KC, S], F32R), sc.sb("xT_lo", [P, 2, KC, S], F32R)
        act_gate = sc.sb("act_gate", [P, IC, S])
        hid = sc.sb("hid", [P, IC, S])
        hid_hi, hid_lo = sc.sb("hid_hi", [P, 2, IC, S], F32R), sc.sb("hid_lo", [P, 2, IC, S], F32R)

        raw_in = [sc.sem(f"raw_in{k}") for k in range(RAW)]
        w_hi, w_ready = sc.sem("w_hi"), sc.sem("w_ready")
        acc_in, xn_in = ([sc.sem(f"{n}{p}") for p in range(2)] for n in ("acc_in", "xn_in"))
        stored = [sc.sem(f"stored{p}") for p in range(2)]
        turned, xT_hi_made, xT_ready = sc.sem("turned"), sc.sem("xT_hi_made"), sc.sem("xT_ready")
        gate_made, up_made, gate_out, up_out = sc.sem("gate_made"), sc.sem("up_made"), sc.sem("gate_out"), sc.sem("up_out")
        hi_made, lo_made = sc.sem("hi_made"), sc.sem("lo_made")
        down_made = sc.sem("down_made")
        acc_made = sc.sem("acc_made")
        block = ctx.enter_context(nc.Block())
        STEPS = 2 * E
        LAST = B // 2 - 1
        matrices = [(w, e) for e in range(E) for w in range(3)]

        def iterations(eng, body):
            with eng.Fori(0, LAST) as r:
                body(r, False)
            body(LAST, True)

        def parts(w, e):
            hi, lo = ((wg_hi, wg_lo), (wu_hi, wu_lo), (wd_hi, wd_lo))[w]
            return hi[:, e, :, :].rearrange("p c f -> p (c f)"), lo[:, e, :, :].rearrange("p c f -> p (c f)")

        def weights_for(pe, e, count):
            pe.wait_ge(w_ready, 3 * e + count)

        @block.sync
        def _(sp):
            def load(b, p, r):
                after(sp, turned, b - 1)
                sp.dma_start(xn[:, p, :, :], x_normed[bass.ds(b, 1), :, :].rearrange("o (t p) d -> p (o t) d", p=P)).then_inc(xn_in[p], 16)
                after(sp, stored[p], r * 16)
                sp.dma_start(acc[:, p, :, :], x[bass.ds(b, 1), :, :].rearrange("o (t p) d -> p (o t) d", p=P)).then_inc(acc_in[p], 16)

            def body(r, last):
                for p in range(2):
                    b = r * 2 + p
                    sp.wait_ge(acc_made, (b + 1) * (E * TT))
                    sp.dma_start(out[bass.ds(b, 1), :, :].rearrange("o (t p) d -> p (o t) d", p=P), acc[:, p, :, :]).then_inc(stored[p], 16)
                    if not last:
                        load(b + 2, p, r + 1)
            load_temperature(sp)
            load(0, 0, 0)
            for n, (w, e) in enumerate(matrices):
                after(sp, w_ready, n - RAW + 1)
                src = (w_gate, w_up, w_down)[w][e, :, :].rearrange("(c p) f -> p c f", p=P)
                sp.dma_start(raw[:, n % RAW, :].rearrange("p (c f) -> p c f", c=2), src).then_inc(raw_in[n % RAW], 16)
                if n == 5:
                    load(1, 1, 0)
            iterations(sp, body)
            for p in range(2):
                sp.wait_ge(stored[p], 16 * (B // 2))

        @block.gpsimd
        def _(pool):
            expert_order(pool)
            for n, (w, e) in enumerate(matrices):
                pool.wait_ge(w_hi, n + 1)
                pool.wait_ge(raw_in[n % RAW], n // RAW * 16 + 16)
                pool.tensor_tensor(parts(w, e)[1], raw[:, n % RAW, :], parts(w, e)[0].bitcast(F32), ALU.subtract).then_inc(w_ready, 1)

        @block.tensor
        def _(pe):
            def turn(b, p, r):
                pe.wait_ge(xn_in[p], r * 16 + 16)
                after(pe, xT_ready, b)
                for c in range(KC):
                    for t in range(TT):
                        m = pe.transpose(psum[:, 6 + c, t * P:(t + 1) * P], xn[:, p, t, c * P:(c + 1) * P], const["ident"][:, :])
                m.then_inc(turned, 1)

            def gate_up(b, p, e, first):
                n = b * E + e
                if e == 0:
                    pe.wait_ge(xT_ready, b + 1)
                for w, (hi, lo), bank, last_out, made in ((0, (wg_hi, wg_lo), 0, gate_out, gate_made), (1, (wu_hi, wu_lo), 2, up_out, up_made)):
                    if first:
                        pe.wait_ge(w_ready, 3 * e + w + 1)
                    after(pe, last_out, n)
                    for i in range(IC):
                        cols = slice(i * P, (i + 1) * P)
                        for c in range(KC):
                            m = three_passes(pe, psum[:, bank + i, :], hi[:, e, c, cols], lo[:, e, c, cols],
                                             xT_hi[:, p, c, :], xT_lo[:, p, c, :], c == 0, c == KC - 1)
                    m.then_inc(made, 1)

            def down(b, p, e, first):
                n = b * E + e
                if first:
                    pe.wait_ge(w_ready, 3 * e + 3)
                pe.wait_ge(lo_made, n + 1)
                for t in range(TT):
                    if t % 2 == 0:
                        after(pe, acc_made, n * TT - TT + t + 2)
                    rows = slice(t * P, (t + 1) * P)
                    for i in range(IC):
                        m = three_passes(pe, psum[:, 4 + t // 2, (t % 2) * D:(t % 2 + 1) * D], hid_hi[:, e % 2, i, rows],
                                         hid_lo[:, e % 2, i, rows], wd_hi[:, e, i, :], wd_lo[:, e, i, :], i == 0, i == IC - 1)
                    if t % 2:
                        m.then_inc(down_made, 1)

            def steps(r, last, first):
                for p in range(2):
                    b = r * 2 + p
                    for e in range(E):
                        if e < E - 1:
                            if e == 2 and not (last and p == 1):
                                turn(b + 1, 1 - p, r + p)
                            gate_up(b, p, e + 1, first and p == 0)
                        elif not (last and p == 1):
                            gate_up(b + 1, 1 - p, 0, False)
                        down(b, p, e, first and p == 0)

            turn(0, 0, 0)
            gate_up(0, 0, 0, True)
            steps(0, False, True)
            with pe.Fori(1, LAST) as r:
                steps(r, False, False)
            steps(LAST, True, False)

        @block.scalar
        def _(act):
            def rows_hi(b, p):
                act.wait_ge(turned, b + 1)
                after(act, gate_made, b * E - E)
                after(act, up_made, b * E - E)
                act.activation(xT_hi[:, p, :, :], psum[:, 6:8, :], ACT.Copy).then_inc(xT_hi_made, 1)

            def steps(r, last, first):
                for p in range(2):
                    b = r * 2 + p
                    for e in range(E):
                        n = b * E + e
                        act.wait_ge(gate_made, n + 1)
                        after(act, hi_ready_to_reuse, n)
                        act.activation(act_gate[:, :, :], psum[:, 0:2, :], ACT.Silu).then_inc(gate_out, 1)
                        if e == 3 and not (last and p == 1):
                            rows_hi(b + 1, 1 - p)
                        if first and p == 0 and e + 2 < E:
                            for k in range(3):
                                split_hi(3 * (e + 2) + k)
                        act.wait_ge(up_out, n + 1)
                        after(act, down_made, n * 2 - 2)
                        act.activation(hid_hi[:, e % 2, :, :], hid[:, :, :], ACT.Copy).then_inc(hi_made, 1)

            hi_ready_to_reuse = up_out
            def split_hi(n):
                act.wait_ge(raw_in[n % RAW], n // RAW * 16 + 16)
                act.activation(parts(*matrices[n])[0], raw[:, n % RAW, :], ACT.Copy).then_inc(w_hi, 1)

            for n in range(3):
                split_hi(n)
            rows_hi(0, 0)
            sigmoid_exp(act)
            for n in range(3, 6):
                split_hi(n)
            distance_exps(act)
            steps(0, False, True)
            with act.Fori(1, LAST) as r:
                steps(r, False, False)
            steps(LAST, True, False)

        @block.vector
        def _(dve):
            def rows_lo(b, p):
                dve.wait_ge(xT_hi_made, b + 1)
                dve.tensor_tensor(xT_lo[:, p, :, :], psum[:, 6:8, :], xT_hi[:, p, :, :].bitcast(F32), ALU.subtract).then_inc(xT_ready, 1)

            def add(b, p, e, r):
                n = b * E + e
                if e == 0:
                    dve.wait_ge(acc_in[p], r * 16 + 16)
                    dve.wait_ge(weight_steps, ZONE_STEPS)
                else:
                    dve.wait_ge(acc_made, n * TT)
                for t in range(TT):
                    if t % 2 == 0:
                        dve.wait_ge(down_made, n * 2 + t // 2 + 1)
                    dve.scalar_tensor_tensor(acc[:, p, t, :], psum[:, 4 + t // 2, (t % 2) * D:(t % 2 + 1) * D],
                                             weight[:, bass.ds(b * TT + t, 1), e], acc[:, p, t, :], ALU.mult, ALU.add).then_inc(acc_made, 1)

            def hidden(b, p, e):
                n = b * E + e
                dve.wait_ge(gate_out, n + 1)
                dve.wait_ge(up_made, n + 1)
                after(dve, lo_made, n)
                dve.tensor_tensor(hid[:, :, :], act_gate[:, :, :], psum[:, 2:4, :], ALU.mult).then_inc(up_out, 1)

            def hidden_lo(b, p, e):
                n = b * E + e
                dve.wait_ge(hi_made, n + 1)
                dve.tensor_tensor(hid_lo[:, e % 2, :, :], hid[:, :, :], hid_hi[:, e % 2, :, :].bitcast(F32), ALU.subtract).then_inc(lo_made, 1)

            def steps(r, last, first):
                for p in range(2):
                    b = r * 2 + p
                    for e in range(E):
                        if e < E - 1:
                            nb, np_, ne = b, p, e + 1
                        else:
                            nb, np_, ne = b + 1, 1 - p, 0
                        over = last and p == 1
                        if not (over and e == E - 1):
                            hidden(nb, np_, ne)
                        if e == 2 and not over:
                            rows_lo(b + 1, 1 - p)
                        if not (over and e == E - 1):
                            hidden_lo(nb, np_, ne)
                        add(b, p, e, r)

            def first_step():
                hidden(0, 0, 0)
                hidden_lo(0, 0, 0)
            rows_lo(0, 0)
            weights(dve, first_step)
            steps(0, False, True)
            with dve.Fori(1, LAST) as r:
                steps(r, False, False)
            steps(LAST, True, False)


def two_layers(nc, a, out):
    x1 = nc.dram_tensor("x1", (N_TOK, D), F32, kind="Internal").ap()
    rows1 = nc.dram_tensor("rows1", (N_TOK, ROW), F32, kind="Internal").ap()
    x3 = nc.dram_tensor("x3", (B, S, D), F32, kind="Internal").ap()
    normed3 = nc.dram_tensor("normed3", (B, S, D), F32, kind="Internal").ap()
    x1_by_batch = x1.rearrange("(b s) d -> b s d", s=S)
    with ExitStack() as ctx:
        sc = Scope(nc, ctx, "main")
        const = {"ident": sc.sb("ident", [P, P]), "headmask": sc.sb("headmask", [P, HH]),
                 "negsel": sc.sb("negsel", [P, NP, P], F32R), "keysel": sc.sb("keysel", [P, HH, SK], BF16)}
        psum = ctx.enter_context(nc.psum_tensor("psum", [P, 8, 512], F32))
        logits = sc.sb("logits", [P, NT, E])
        const["sems"] = Semaphores(nc)

        def layer_weights(n, **masks):
            names = ("wq", "wk", "wv", "wo", "bq", "bk", "bv", "bo", "wr")
            return {**{k: a[k + n] for k in names}, "ctx": a["ctx"], **masks}

        with ExitStack() as layer:
            kv = alloc_layer(Scope(nc, layer, "att0"), False)
            first_setup(nc, const, kv, layer_weights("0", mask=None, pad=None), psum)
            attention(nc, const, kv, psum, a["x"], x1_by_batch, rows1.rearrange("(b s) r -> b s r", s=S)[:, :, 0:D], logits)
        const["sems"].give_back()
        const["sems"] = Semaphores(nc)

        with ExitStack() as layer:
            kv = alloc_layer(Scope(nc, layer, "att1"), True)
            w1 = layer_weights("1", mask=a["mask"], pad=a["pad"])
            with ExitStack() as mixture:
                idx = Scope(nc, mixture, "lists").sb("idx", [P, E, TOPK // P], I32)
                route_expert_choice(nc, const, psum, logits, a["br"], rows1, idx,
                                    lambda sc: setup_parts(sc, const, kv, w1, psum, 4))
                expert_choice_mixture(nc, const, psum, idx, x1, rows1, a["w_up"], a["b_up"], a["w_down"])
            attention(nc, const, kv, psum, x1_by_batch, x3, normed3, logits)
        zone_mixture(nc, const, psum, logits, a["temperature"], x3, normed3, a["wg"], a["wu"], a["wd"], out)


def kernel(**inputs):
    import numpy as _np
    import concourse.bacc as _bacc
    from concourse import mybir as _mybir
    from concourse.bass_utils import run_bass_kernel_spmd as _run

    i = {k: _np.asarray(v) for k, v in inputs.items()}

    def columns(v):
        return v.reshape(-1, P).T

    w_up = _np.zeros((GROUPS_UP, D, FP), i["L0_ffn_W_up"].dtype)
    w_up[:, :, :F] = i["L0_ffn_W_up"]
    b_up = _np.zeros((GROUPS_UP, FP), i["L0_ffn_b_up"].dtype)
    b_up[:, :F] = i["L0_ffn_b_up"]
    w_down = _np.zeros((E, FP, D), i["L0_ffn_W_down"].dtype)
    w_down[:, :F] = i["L0_ffn_W_down"]
    w_down[:, (FC - 1) * P + BIAS_ROW] = i["L0_ffn_b_down"]
    laid = {
        "x": i["x"], "ctx": i["ctx_1024"].reshape(B * SK, D),
        "wq0": i["L0_xattn_Wq"], "wk0": i["L0_xattn_Wk"], "wv0": i["L0_xattn_Wv"], "wo0": i["L0_xattn_Wo"],
        "bq0": columns(i["L0_xattn_bq"]), "bk0": columns(i["L0_xattn_bk"]), "bv0": i["L0_xattn_bv"], "bo0": i["L0_xattn_bo"],
        "wr0": i["L0_ffn_Wr"], "br": i["L0_ffn_br"],
        "w_up": w_up, "b_up": b_up.reshape(GROUPS_UP, FC, P).transpose(0, 2, 1), "w_down": w_down,
        "wq1": i["L1_xattn_wq"].T, "wk1": i["L1_xattn_wk"].T, "wv1": i["L1_xattn_wv"].T, "wo1": i["L1_xattn_wo"].T,
        "bq1": columns(i["L1_xattn_bq"]), "bk1": columns(i["L1_xattn_bk"]), "bv1": i["L1_xattn_bv"], "bo1": i["L1_xattn_bo"],
        "wr1": i["L1_ffn_Wr"], "temperature": i["L1_ffn_temperature"],
        "mask": i["mask_SxS2_bk0"].T, "pad": i["mask_BxS2_bk1"].T,
        "wg": i["L1_ffn_Wg"], "wu": i["L1_ffn_Wu"], "wd": i["L1_ffn_Wd"],
    }
    nc = _bacc.Bacc("TRN2", target_bir_lowering=False, num_devices=1)
    arrays, args = {}, {}
    for name, v in laid.items():
        v = _np.ascontiguousarray(v)
        if v.dtype == _np.bool_:
            v = v.view(_np.int32)
        arrays[f"in_{name}"] = v
        args[name] = nc.dram_tensor(f"in_{name}", v.shape, _mybir.dt.from_np(v.dtype), kind="ExternalInput").ap()
    out = nc.dram_tensor("out_x", (B, S, D), _mybir.dt.float32, kind="ExternalOutput").ap()
    two_layers(nc, args, out)
    r = _run(nc, [arrays], core_ids=[0])
    return r.results[0]["out_x"]
```
